# Optimizing a Trainium2 kernel written in Bass

```python
import numpy as np
import jax
import jax.numpy as jnp

def _softmax(x, axis=-1):
    return jax.nn.softmax(x, axis=axis)

def _gelu(x):
    return jax.nn.gelu(x, approximate=True)

def _silu(x):
    return jax.nn.silu(x)

def _sigmoid(x):
    return jax.nn.sigmoid(x)

def _layernorm(x, axis=-1, eps=1e-05):
    m = jnp.mean(x, axis=axis, keepdims=True)
    v = jnp.var(x, axis=axis, keepdims=True)
    return (x - m) / jnp.sqrt(v + eps)

def _scatter_add(tgt, idx, src, axis=0):
    return tgt.at[idx].add(src)

def _segment_sum(src, seg, n):
    return jax.ops.segment_sum(src, seg, n)
kernel_name = 'mk_hybrid_d2_jaxref_r8_023277'

def setup_inputs(seed: int=0):
    np.random.seed(seed)
    _w = jnp.asarray

    def _L0_attn_a_setup():
        import jax, jax.numpy as jnp
        import numpy as np
        EMB = 128
        HEADS = 16
        ATT = EMB // HEADS
        key = jax.random.key(seed)
        ks = jax.random.split(key, 5)
        s = 1.0 / np.sqrt(EMB)
        return {'x': jax.random.normal(ks[0], (4, 256, EMB), dtype=jnp.float32), 'Wq': jax.random.uniform(ks[1], (EMB, HEADS * ATT), jnp.float32, -s, s), 'Wk': jax.random.uniform(ks[2], (EMB, HEADS * ATT), jnp.float32, -s, s), 'Wv': jax.random.uniform(ks[3], (EMB, HEADS * ATT), jnp.float32, -s, s), 'Wo': jax.random.uniform(ks[4], (HEADS * ATT, EMB), jnp.float32, -s, s)}
    _L0_attn_a_in = _L0_attn_a_setup()

    def _L0_attn_b_setup():
        import jax, jax.numpy as jnp
        import numpy as np
        B, T, D, H = (2, 256, 128, 16)
        HD = D // H
        SCALE = 1.0 / np.sqrt(D).astype(np.float32)
        key = jax.random.key(seed)
        k1, k2, k3 = jax.random.split(key, 3)
        x = jax.random.normal(k1, (B, T, D), dtype=jnp.float32)
        W_attn = jax.random.normal(k2, (3 * D, D), dtype=jnp.float32) * 0.02
        W_out = jax.random.normal(k3, (D, D), dtype=jnp.float32) * 0.02
        return {'x': x, 'W_attn': W_attn, 'W_out': W_out}
    _L0_attn_b_in = _L0_attn_b_setup()

    def _L0_ffn_setup():
        import jax, jax.numpy as jnp
        import numpy as np
        D, F, E, K = (128, 344, 8, 2)
        key = jax.random.key(seed)
        k0, k1, k2, k3, k4 = jax.random.split(key, 5)
        s = 0.02
        x = jax.random.normal(k0, (2, 64, D), jnp.float32)
        Ws = jax.random.normal(k1, (D, E), jnp.float32) * s
        bs = jnp.zeros((E,), jnp.float32)
        Wg = jax.random.normal(k2, (E, D, F), jnp.float32) * s
        Wu = jax.random.normal(k3, (E, D, F), jnp.float32) * s
        Wd = jax.random.normal(k4, (E, F, D), jnp.float32) * s
        return {'x': x, 'Ws': Ws, 'bs': bs, 'Wg': Wg, 'Wu': Wu, 'Wd': Wd}
    _L0_ffn_in = _L0_ffn_setup()

    def _L1_attn_a_setup():
        import math
        import jax, jax.numpy as jnp
        import numpy as np
        B, T, D = (1, 256, 128)
        H, DM = (16, 64)

        def _l2norm(a):
            n = jnp.sqrt(jnp.sum(a * a, axis=-1, keepdims=True))
            return a / jnp.maximum(n, 1e-12)
        key = jax.random.key(seed)
        ks = jax.random.split(key, 6)
        x = jax.random.normal(ks[0], (B, T, D), dtype=jnp.float32)
        std = 0.02
        Wk = jax.random.normal(ks[1], (D, H * DM), dtype=jnp.float32) * std
        Wv = jax.random.normal(ks[2], (D, H * DM), dtype=jnp.float32) * std
        Wq = jax.random.normal(ks[3], (D, H * DM), dtype=jnp.float32) * std
        Wbeta = jax.random.normal(ks[4], (D, H), dtype=jnp.float32) * std
        Wout = jax.random.normal(ks[5], (H * DM, D), dtype=jnp.float32) * std
        return {'x': x, 'Wk': Wk, 'Wv': Wv, 'Wq': Wq, 'Wbeta': Wbeta, 'Wout': Wout}
    _L1_attn_a_in = _L1_attn_a_setup()

    def _L1_attn_b_setup():
        import jax, jax.numpy as jnp
        import numpy as np
        B, N, D, NH, MAXLEN = (2, 256, 128, 16, 256)
        HD = D // NH

        def srel_skew(x):
            b, h, n, _ = x.shape
            v = jnp.pad(x, ((0, 0), (0, 0), (0, 0), (1, 0)))
            return v.reshape(b, h, n + 1, n)[:, :, :n, :]

        def split_head(x):
            b, n, _ = x.shape
            return x.reshape(b, n, NH, HD).transpose(0, 2, 1, 3)
        key = jax.random.key(seed)
        ks = jax.random.split(key, 7)
        scale = 0.02
        return {'x': jax.random.normal(ks[0], (B, N, D), dtype=jnp.float32), 'Wq': jax.random.normal(ks[1], (D, D), dtype=jnp.float32) * scale, 'Wk': jax.random.normal(ks[2], (D, D), dtype=jnp.float32) * scale, 'Wv': jax.random.normal(ks[3], (D, D), dtype=jnp.float32) * scale, 'Wp': jax.random.normal(ks[4], (D, D), dtype=jnp.float32) * scale, 'bp': jnp.zeros((D,), dtype=jnp.float32), 'rel_embed': jax.random.normal(ks[5], (MAXLEN, D), dtype=jnp.float32) * scale}
    _L1_attn_b_in = _L1_attn_b_setup()

    def _L1_ffn_setup():
        import jax, jax.numpy as jnp
        import numpy as np
        TOP_K = 2
        key = jax.random.key(seed)
        ks = jax.random.split(key, 6)
        B, S, D, BN, E = (32, 256, 128, 64, 8)
        return {'x': jax.random.normal(ks[0], (B, S, D), dtype=jnp.float32), 'gate_w': jax.random.normal(ks[1], (E, D), dtype=jnp.float32) * 0.02, 'down_w': jax.random.normal(ks[2], (E, BN, D), dtype=jnp.float32) * 0.02, 'down_b': jax.random.normal(ks[3], (E, BN), dtype=jnp.float32) * 0.02, 'up_w': jax.random.normal(ks[4], (E, D, BN), dtype=jnp.float32) * 0.02, 'up_b': jax.random.normal(ks[5], (E, D), dtype=jnp.float32) * 0.02}
    _L1_ffn_in = _L1_ffn_setup()
    _d = {'L0_attn_a_x': _L0_attn_a_in['x'], 'L0_attn_a_Wq': _L0_attn_a_in['Wq'], 'L0_attn_a_Wk': _L0_attn_a_in['Wk'], 'L0_attn_a_Wv': _L0_attn_a_in['Wv'], 'L0_attn_a_Wo': _L0_attn_a_in['Wo'], 'L0_attn_b_W_attn': _L0_attn_b_in['W_attn'], 'L0_attn_b_W_out': _L0_attn_b_in['W_out'], 'L0_ffn_Ws': _L0_ffn_in['Ws'], 'L0_ffn_bs': _L0_ffn_in['bs'], 'L0_ffn_Wg': _L0_ffn_in['Wg'], 'L0_ffn_Wu': _L0_ffn_in['Wu'], 'L0_ffn_Wd': _L0_ffn_in['Wd'], 'L1_attn_a_Wk': _L1_attn_a_in['Wk'], 'L1_attn_a_Wv': _L1_attn_a_in['Wv'], 'L1_attn_a_Wq': _L1_attn_a_in['Wq'], 'L1_attn_a_Wbeta': _L1_attn_a_in['Wbeta'], 'L1_attn_a_Wout': _L1_attn_a_in['Wout'], 'L1_attn_b_Wq': _L1_attn_b_in['Wq'], 'L1_attn_b_Wk': _L1_attn_b_in['Wk'], 'L1_attn_b_Wv': _L1_attn_b_in['Wv'], 'L1_attn_b_Wp': _L1_attn_b_in['Wp'], 'L1_attn_b_bp': _L1_attn_b_in['bp'], 'L1_attn_b_rel_embed': _L1_attn_b_in['rel_embed'], 'L1_ffn_gate_w': _L1_ffn_in['gate_w'], 'L1_ffn_down_w': _L1_ffn_in['down_w'], 'L1_ffn_down_b': _L1_ffn_in['down_b'], 'L1_ffn_up_w': _L1_ffn_in['up_w'], 'L1_ffn_up_b': _L1_ffn_in['up_b']}
    _x0 = _d['L0_attn_a_x']
    _d['L0_attn_a_x'] = jax.random.normal(jax.random.fold_in(jax.random.key(seed), 1), (8, 512, 128), dtype=_x0.dtype)
    del _x0
    return _d

def reference(L0_attn_a_x, L0_attn_a_Wq, L0_attn_a_Wk, L0_attn_a_Wv, L0_attn_a_Wo, L0_attn_b_W_attn, L0_attn_b_W_out, L0_ffn_Ws, L0_ffn_bs, L0_ffn_Wg, L0_ffn_Wu, L0_ffn_Wd, L1_attn_a_Wk, L1_attn_a_Wv, L1_attn_a_Wq, L1_attn_a_Wbeta, L1_attn_a_Wout, L1_attn_b_Wq, L1_attn_b_Wk, L1_attn_b_Wv, L1_attn_b_Wp, L1_attn_b_bp, L1_attn_b_rel_embed, L1_ffn_gate_w, L1_ffn_down_w, L1_ffn_down_b, L1_ffn_up_w, L1_ffn_up_b):

    def _L0_attn_a_ref(x, Wq, Wk, Wv, Wo):
        import jax, jax.numpy as jnp
        import numpy as np
        EMB = 128
        HEADS = 16
        ATT = EMB // HEADS
        b, t, _ = x.shape
        h, d = (HEADS, ATT)
        scale = d ** (-0.25)
        q = (x @ Wq).reshape(b, t, h, d) * scale
        k = (x @ Wk).reshape(b, t, h, d) * scale
        v = (x @ Wv).reshape(b, t, h, d)
        dot = jnp.einsum('bqhd,bkhd->bhqk', q, k)
        causal = jnp.tril(jnp.ones((t, t), dtype=bool))
        dot = jnp.where(causal[None, None], dot, -jnp.inf)
        attn = jax.nn.softmax(dot, axis=-1)
        out = jnp.einsum('bhqk,bkhd->bqhd', attn, v).reshape(b, t, h * d)
        return out @ Wo

    def _L0_attn_b_ref(x, W_attn, W_out):
        import jax, jax.numpy as jnp
        import numpy as np
        B, T, D, H = (2, 256, 128, 16)
        HD = D // H
        SCALE = 1.0 / np.sqrt(D).astype(np.float32)
        b, t, d = x.shape
        qkv = jnp.einsum('btd,ed->bte', x, W_attn)
        q, k, v = jnp.split(qkv, 3, axis=-1)
        q = q.reshape(b, t, H, HD).transpose(0, 2, 1, 3)
        k = k.reshape(b, t, H, HD).transpose(0, 2, 1, 3)
        v = v.reshape(b, t, H, HD).transpose(0, 2, 1, 3)
        att = jnp.einsum('bhqd,bhkd->bhqk', q, k)
        causal = jnp.tril(jnp.ones((t, t), dtype=bool))
        att = jnp.where(causal[None, None], att * SCALE, -jnp.inf)
        att = jax.nn.softmax(att, axis=-1)
        z = jnp.einsum('bhqk,bhkd->bhqd', att, v)
        z = z.transpose(0, 2, 1, 3).reshape(b, t, d)
        return jnp.einsum('btd,od->bto', z, W_out)

    def _L0_ffn_ref(x, Ws, bs, Wg, Wu, Wd):
        import jax, jax.numpy as jnp
        import numpy as np
        D, F, E, K = (128, 344, 8, 2)
        b, n, d = x.shape
        xt = x.reshape(-1, d)
        logits = xt @ Ws + bs
        topk_w, topk_idx = jax.lax.top_k(logits, K)
        topk_w = jax.nn.softmax(topk_w, axis=-1)
        combine = jnp.sum(jax.nn.one_hot(topk_idx, E, dtype=xt.dtype) * topk_w[..., None], axis=1)
        g = jnp.einsum('td,edf->tef', xt, Wg)
        u = jnp.einsum('td,edf->tef', xt, Wu)
        h = jax.nn.silu(g) * u
        y = jnp.einsum('tef,efd->ted', h, Wd)
        out = jnp.einsum('ted,te->td', y, combine)
        return out.reshape(b, n, d)

    def _L1_attn_a_ref(x, Wk, Wv, Wq, Wbeta, Wout):
        import math
        import jax, jax.numpy as jnp
        import numpy as np
        B, T, D = (1, 256, 128)
        H, DM = (16, 64)

        def _l2norm(a):
            n = jnp.sqrt(jnp.sum(a * a, axis=-1, keepdims=True))
            return a / jnp.maximum(n, 1e-12)
        b, t, d = x.shape
        keys = _l2norm(jnp.einsum('btd,de->bte', x, Wk).reshape(b, t, H, DM).transpose(0, 2, 1, 3))
        values = jnp.einsum('btd,de->bte', x, Wv).reshape(b, t, H, DM).transpose(0, 2, 1, 3)
        queries = _l2norm(jnp.einsum('btd,de->bte', x, Wq).reshape(b, t, H, DM).transpose(0, 2, 1, 3))
        beta = jax.nn.sigmoid(jnp.einsum('btd,dh->bht', x, Wbeta))
        log_retain = jnp.log(1.0 - beta + 1e-08)
        cum_log = jnp.cumsum(log_retain, axis=-1)
        log_decay = cum_log[..., :, None] - cum_log[..., None, :]
        mask = jnp.triu(jnp.ones((t, t), dtype=bool))
        decay = jnp.exp(jnp.minimum(log_decay, 0.0)) * mask
        kq = jnp.einsum('bhtd,bhsd->bhts', queries, keys) / math.sqrt(DM)
        weights = kq * decay
        out = jnp.einsum('bhts,bhsd->bhtd', weights, values) + beta[..., None] * values
        out = out.transpose(0, 2, 1, 3).reshape(b, t, H * DM)
        return jnp.einsum('bte,ed->btd', out, Wout)

    def _L1_attn_b_ref(x, Wq, Wk, Wv, Wp, bp, rel_embed):
        import jax, jax.numpy as jnp
        import numpy as np
        B, N, D, NH, MAXLEN = (2, 256, 128, 16, 256)
        HD = D // NH

        def srel_skew(x):
            b, h, n, _ = x.shape
            v = jnp.pad(x, ((0, 0), (0, 0), (0, 0), (1, 0)))
            return v.reshape(b, h, n + 1, n)[:, :, :n, :]

        def split_head(x):
            b, n, _ = x.shape
            return x.reshape(b, n, NH, HD).transpose(0, 2, 1, 3)
        b, n, d = x.shape
        qx = split_head(x @ Wq.T)
        kx = split_head(x @ Wk.T)
        vx = split_head(x @ Wv.T)
        ns = jnp.arange(n) + (MAXLEN - n)
        ex = rel_embed[ns].reshape(n, NH, HD).transpose(1, 0, 2)
        srel = srel_skew(jnp.einsum('bhnd,hmd->bhnm', qx, ex))
        inv_dim = 1.0 / np.sqrt(d / NH)
        qk = (jnp.einsum('bhnd,bhmd->bhnm', qx, kx) + srel) * inv_dim
        mask = 1000000000.0 * jnp.triu(jnp.ones((n, n), dtype=x.dtype), 1)
        atten = jax.nn.softmax(qk - mask, axis=-1)
        out = jnp.einsum('bhnm,bhmd->bhnd', atten, vx).transpose(0, 2, 1, 3).reshape(b, n, d)
        return out @ Wp.T + bp

    def _L1_ffn_ref(x, gate_w, down_w, down_b, up_w, up_b):
        import jax, jax.numpy as jnp
        import numpy as np
        TOP_K = 2
        pooled = x.mean(axis=1)
        gate = jax.nn.softmax(pooled @ gate_w.T, axis=-1)
        top_w, top_i = jax.lax.top_k(gate, TOP_K)
        top_w = top_w / (top_w.sum(axis=-1, keepdims=True) + 1e-08)
        Wd = down_w[top_i]
        bd = down_b[top_i]
        Wu = up_w[top_i]
        bu = up_b[top_i]
        h = jax.nn.gelu(jnp.einsum('bsd,bkcd->bksc', x, Wd) + bd[:, :, None, :], approximate=False)
        h = h * top_w[:, :, None, None]
        out = jnp.einsum('bksc,bkdc->bsd', h, Wu)
        out = out + (top_w[:, :, None] * bu).sum(axis=1)[:, None, :]
        return out
    x = L0_attn_a_x
    x = x + _L0_attn_a_ref(_layernorm(x, axis=-1), L0_attn_a_Wq, L0_attn_a_Wk, L0_attn_a_Wv, L0_attn_a_Wo)
    x = x + _L0_ffn_ref(_layernorm(x, axis=-1), L0_ffn_Ws, L0_ffn_bs, L0_ffn_Wg, L0_ffn_Wu, L0_ffn_Wd)
    x = x + _L0_attn_b_ref(_layernorm(x, axis=-1), L0_attn_b_W_attn, L0_attn_b_W_out)
    x = x + _L0_ffn_ref(_layernorm(x, axis=-1), L0_ffn_Ws, L0_ffn_bs, L0_ffn_Wg, L0_ffn_Wu, L0_ffn_Wd)
    x = x + _L1_attn_a_ref(_layernorm(x, axis=-1), L1_attn_a_Wk, L1_attn_a_Wv, L1_attn_a_Wq, L1_attn_a_Wbeta, L1_attn_a_Wout)
    x = x + _L1_ffn_ref(_layernorm(x, axis=-1), L1_ffn_gate_w, L1_ffn_down_w, L1_ffn_down_b, L1_ffn_up_w, L1_ffn_up_b)
    x = x + _L1_attn_b_ref(_layernorm(x, axis=-1), L1_attn_b_Wq, L1_attn_b_Wk, L1_attn_b_Wv, L1_attn_b_Wp, L1_attn_b_bp, L1_attn_b_rel_embed)
    x = x + _L1_ffn_ref(_layernorm(x, axis=-1), L1_ffn_gate_w, L1_ffn_down_w, L1_ffn_down_b, L1_ffn_up_w, L1_ffn_up_b)
    return x

_drawn_inputs = setup_inputs


def setup_inputs(seed=0):
    import zlib

    import numpy as np

    out = dict(_drawn_inputs(seed))
    spreads = {'L0_ffn_bs': (0.0, 0.8), 'L1_attn_b_bp': (0.0, 0.1)}
    factors = {'L0_attn_a_Wq': 3.833,
     'L0_attn_a_Wk': 3.641,
     'L0_attn_b_W_attn': 7.207,
     'L0_attn_b_W_out': 7.092,
     'L0_ffn_Ws': 4.506,
     'L0_ffn_Wg': 4.196,
     'L0_ffn_Wu': 4.157,
     'L0_ffn_Wd': 3.918,
     'L1_attn_a_Wbeta': 7.172,
     'L1_attn_b_Wq': 8.0,
     'L1_attn_b_Wk': 8.0,
     'L1_attn_b_Wv': 6.062,
     'L1_attn_b_Wp': 5.377,
     'L1_attn_b_rel_embed': 8.0,
     'L1_ffn_down_b': 38.011,
     'L1_ffn_down_w': 3.254,
     'L1_ffn_up_w': 2.722,
     'L1_ffn_up_b': 2.966}
    for name, (base, spread) in spreads.items():
        noise = np.random.default_rng([zlib.crc32(name.encode()), seed]).standard_normal(out[name].shape)
        drawn = base * np.exp(spread * noise) if base else spread * noise
        out[name] = jnp.asarray(drawn.astype(out[name].dtype))
    for name, factor in factors.items():
        out[name] = (out[name] * factor).astype(out[name].dtype)
    return out
```

```python
from contextlib import ExitStack

import concourse.bass as bass
from concourse import mybir

F32 = mybir.dt.float32
BF16 = mybir.dt.bfloat16
ACT = mybir.ActivationFunctionType
ALU = mybir.AluOpType
AX = mybir.AxisListType

P = 128
T = 512
NT = T // P
H = 16
HD = P // H
DM = 64
NC2 = H * DM // P
E = 8
EPS = 1e-5
MASKED = -1e30

Q_PART = [0, 1, 2, 0, 1, 0]
K_PART = [0, 0, 0, 1, 1, 2]
SLOTS = len(Q_PART)
KROWS = SLOTS * HD

G4 = 4
NG = H // G4

BLOCKS = [(0, 0), (0, 1), (0, 2), (0, 3), (1, 1), (1, 2), (1, 3), (3, 3), (2, 2), (2, 3)]
SLOT = {b: n for n, b in enumerate(BLOCKS)}
COLS = len(BLOCKS) * P
JOBS = [[0], [1, 3], [2]]
JOB_AT = [0, 512, 1024]
JOB_N = [512, 512, 256]

LAYERS = ["attn_a", "moe_1", "attn_b", "moe_2", "lin_attn", "adapter_1", "rel_attn", "adapter_2"]


def build(nc, a_x, a_wq, a_wk, a_wv, a_wo, b_wattn, b_wout, m_ws, m_bs, m_wg, m_wu, m_wd,
          l_wk, l_wv, l_wq, l_wbeta, l_wout, r_wq, r_wk, r_wv, r_wp, r_bp, r_rel,
          d_gate, d_dw, d_db, d_uw, d_ub, out):
    B = a_x.shape[0]
    F = m_wg.shape[2]
    FT = [(j * P, min(P, F - j * P)) for j in range((F + P - 1) // P)]
    NF = len(FT)
    BN = d_dw.shape[1]
    KD = E * BN // P
    assert (a_x.shape[1], a_x.shape[2]) == (T, P) and r_rel.shape[0] == 2 * P and 2 * BN == P

    with ExitStack() as ctx:
        def sb(name, shape, dt=F32):
            return ctx.enter_context(nc.sbuf_tensor(name, shape, dt))

        def sem(name):
            return ctx.enter_context(nc.semaphore(name))

        ident = sb("ident", [P, P])
        identb = sb("identb", [P, P], BF16)
        mask_qk = sb("mask_qk", [P, P], BF16)
        mask_kq = sb("mask_kq", [P, P], BF16)
        keep_ge = sb("keep_ge", [P, P])
        ones = sb("ones", [P, P])
        half = sb("half", [P, 2])
        spread_q = sb("spread_q", [P, 3, H // 2, 2, 8, HD], BF16)
        spread_k = sb("spread_k", [P, 3, H // 2, 2, 8, HD], BF16)
        pick_max = sb("pick_max", [P, G4, P], BF16)
        head_of = sb("head_of", [P, H])
        pair_of = sb("pair_of", [P, 2])
        before = sb("before", [P, E, E])
        w_a = sb("w_a", [P, 4, P])
        w_b = sb("w_b", [P, 4, P])
        w_r = sb("w_r", [P, 4, P])
        relT = sb("relT", [P, 3 * P])
        bp_row = sb("bp_row", [1, P])
        ws = sb("ws", [P, E])
        bs_row = sb("bs_row", [1, E])
        wg = sb("wg", [P, E, F])
        wu = sb("wu", [P, E, F])
        wd = sb("wd", [P, E, NF, P])
        wk_l = sb("wk_l", [P, H * DM])
        wv_l = sb("wv_l", [P, H * DM])
        wq_l = sb("wq_l", [P, H * DM])
        wbeta = sb("wbeta", [P, H])
        wout_l = sb("wout_l", [P, NC2, P])
        gateT = sb("gateT", [P, E])
        downT = sb("downT", [P, KD, P])
        upT = sb("upT", [P, KD, P])
        down_b = sb("down_b", [P, KD])
        up_b = sb("up_b", [E, P])
        x = sb("x", [P, NT, P])
        stats = sb("stats", [P, NT, 6])
        moments = sb("moments", [P, NT, 2])
        rstd = sb("rstd", [P, NT])
        xn = sb("xn", [P, NT, P])
        xnT = sb("xnT", [P, T])
        values = sb("values", [P, NT, H, HD + 1])
        neg_maxT = sb("neg_maxT", [P, 2, T], BF16)
        WORK = 29900
        work = sb("work", [P, WORK])

        def part(at, shape, dt=F32):
            n = 1
            for d in shape:
                n *= d
            words = n if dt == F32 else (n + 1) // 2
            assert at + words <= WORK, (at + words, WORK)
            ap = work[:, at:at + words]
            if dt != F32:
                ap = ap.bitcast(dt)
            if len(shape) > 1:
                names = "abcd"[:len(shape)]
                ap = ap.rearrange("p (" + " ".join(names) + ") -> p " + " ".join(names),
                                  **dict(zip(names[1:], shape[1:])))
            return ap, at + words

        NSTAGE = 3 + 1 + 4 + 2 + KD + KD
        stage, at = part(0, [NSTAGE, P])
        stage_gate, at = part(at, [P])
        q_st, at = part(0, [H // 2, T], BF16)
        k_st, at = part(at, [H // 2, T], BF16)
        ring_at = at
        res, at = part(ring_at, [2, T])
        parts, at = part(at, [2, 3, T], BF16)
        prob, at = part(at, [2, COLS])
        neg_max, at = part(at, [2, NT, G4])
        max_res, at = part(at, [2, NT, G4])
        max_part, at = part(at, [2, NT, 4 * G4], BF16)
        rden, at = part(at, [2, NT, G4])
        IC = 32
        q_masked, at = part(ring_at, [2, IC, NT * H])
        q_shift, at = part(at, [T + 4])
        r_prob, _ = part(ring_at, [2, COLS])
        r_probT, at2 = part(ring_at + 2 * COLS, [2, COLS])
        sc, at = part(max(at, at2), [H, len(BLOCKS), P])
        r_neg_max, at = part(at, [2, NT])
        r_rden, at = part(at, [2, NT, G4])
        silu, at = part(0, [2, T])
        hidden, at = part(at, [2, NF, T])
        lg, at = part(at, [NT, E])
        gt, at = part(at, [NT, E, E])
        eq, at = part(at, [NT, E, E])
        rank, at = part(at, [NT, E])
        top, at = part(at, [NT])
        lgd, at = part(at, [NT, E])
        ex, at = part(at, [NT, E])
        mix, at = part(at, [NT, E])
        tot, at = part(at, [NT])
        l_qT, at = part(0, [NC2, T])
        l_kT, at = part(at, [NC2, T])
        l_k, at = part(at, [NT, H * DM])
        l_v, at = part(at, [NT, H * DM])
        l_vk, at = part(at, [NT, H * DM])
        l_sq, at = part(at, [2, T])
        l_wt, at = part(at, [2, NT, P])
        l_st, at = part(at, [2, NT - 1, P])
        l_tmp, at = part(at, [2, NT, P])
        l_beta, at = part(at, [NT, H])
        l_inv, at = part(at, [2, NT, H])
        pooled, at = part(0, [1])
        pool_rep, at = part(at, [P])
        d_hid, at = part(at, [KD, T])
        d_up, at = part(at, [KD, P])
        d_lg, at = part(at, [E])
        d_negm, at = part(at, [1])
        d_ex, at = part(at, [E])
        d_z, at = part(at, [1])
        d_p, at = part(at, [E])
        d_gt, at = part(at, [E, E])
        d_eq, at = part(at, [E, E])
        d_rank, at = part(at, [E])
        d_w, at = part(at, [E])
        d_s, at = part(at, [1])
        d_w4, at = part(at, [KD])
        d_wT, at = part(at, [P])

        psum = ctx.enter_context(nc.psum_tensor("banks", [P, 8, 512], F32))

        def bank(n):
            return psum[:, n, :]

        loaded = sem("loaded")
        const = sem("constants")
        zeroed = sem("zeroed")
        stage_T = sem("stage_transposed")
        weights = sem("weights_ready")
        started = sem("turn_started")
        x_in = sem("x_loaded")
        step = sem("vector_step")
        x_done = sem("layer_done")
        normed = sem("norm_stats")
        rstd_ok = sem("norm_rstd")
        pool_step = sem("pool_step")
        xn_ok = sem("norm_rows")
        xn_T = sem("norm_transposed")
        xnT_ok = sem("norm_columns")
        a_proj = sem("attn_projected")
        a_hi = sem("attn_part_hi")
        a_res = sem("attn_part_rest")
        a_mid = sem("attn_part_mid")
        a_lo = sem("attn_part_lo")
        a_v = sem("attn_values")
        a_spread = sem("attn_spread")
        a_qst = sem("attn_q_stacked")
        a_kst = sem("attn_k_stacked")
        a_s1 = sem("attn_scores_rows")
        a_max = sem("attn_row_max")
        a_mparts = sem("attn_max_parts")
        a_maxT = sem("attn_max_transposed")
        a_mrow = sem("attn_max_rows")
        a_s2 = sem("attn_scores_columns")
        a_prob = sem("attn_probabilities")
        a_pv = sem("attn_weighted_values")
        a_o = sem("attn_heads_out")
        a_oT = sem("attn_out_transposed")
        a_oTs = sem("attn_out_columns")
        a_y = sem("attn_out_projected")
        r_shift = sem("rel_q_shifted")
        r_qm = sem("rel_q_masked")
        r_rel_ok = sem("rel_products")
        r_even = sem("rel_even_blocks")
        r_odd = sem("rel_odd_blocks")
        r_diag = sem("rel_diagonals")
        r_main = sem("rel_scores_qk")
        r_sum = sem("rel_scores_summed")
        r_sT = sem("rel_scores_transposed")
        r_max = sem("rel_row_max")
        r_p = sem("rel_probabilities")
        r_pT = sem("rel_prob_transposed")
        r_pTa = sem("rel_prob_columns_act")
        r_pTv = sem("rel_prob_columns_vec")
        m_logit = sem("moe_logits")
        m_lgd = sem("moe_logits_shifted")
        m_ex = sem("moe_exp")
        m_mix = sem("moe_mixed")
        m_g = sem("moe_gate_products")
        m_u = sem("moe_up_products")
        m_silu = sem("moe_silu")
        m_h = sem("moe_hidden")
        m_y = sem("moe_down_products")
        m_acc = sem("moe_added")
        l_bz = sem("lin_beta_logits")
        l_be = sem("lin_beta_exp")
        l_bok = sem("lin_beta")
        l_pq = sem("lin_qk_products")
        l_pn = sem("lin_kv_products")
        l_qk = sem("lin_qk_columns")
        l_kv = sem("lin_kv_rows")
        l_sqr = sem("lin_squares")
        l_ss = sem("lin_square_sums")
        l_ssc = sem("lin_square_sums_copied")
        l_norm = sem("lin_norms")
        l_invs = sem("lin_inverse_norms")
        l_vks = sem("lin_scaled_values")
        l_bv = sem("lin_beta_values")
        l_sc = sem("lin_scores")
        l_wts = sem("lin_masked_scores")
        l_zero = sem("lin_states_zeroed")
        l_stp = sem("lin_state_products")
        l_sts = sem("lin_states")
        l_o = sem("lin_out_products")
        l_ts = sem("lin_out_scaled")
        l_os = sem("lin_out_rows")
        l_oT = sem("lin_out_transposed")
        l_oTs = sem("lin_out_columns")
        l_y = sem("lin_out_projected")
        d_pool = sem("ad_pooled")
        d_gate_ok = sem("ad_gate_logits")
        d_lgs = sem("ad_logits_ready")
        d_exs = sem("ad_exp")
        d_dn = sem("ad_down_products")
        d_hs = sem("ad_hidden")
        d_ws = sem("ad_mix")
        d_ups = sem("ad_up_scaled")
        d_wTp = sem("ad_mix_transposed")
        d_wTs = sem("ad_mix_column")
        d_y = sem("ad_up_products")
        ended = sem("turn_ended")
        x_out = sem("x_stored")
        turn_sems = range(x_in.num, x_out.num + 1)

        x_rows = a_x.rearrange("b (t p) d -> b p t d", p=P)
        out_rows = out.rearrange("b (t p) d -> b p t d", p=P)

        CONSTS = 6 + 2 * SLOTS + 3 + 4
        ROW_JOBS = [(3, 2, 0), (2, 3, 0), (0, 3, 3 * P), (1, 4, 0)]

        block = ctx.enter_context(nc.Block())

        loads = [
            (ws[:, :], m_ws), (bs_row[:, :], m_bs.rearrange("(a n) -> a n", a=1)),
            (w_a[:, 0, :], a_wq), (w_a[:, 1, :], a_wk), (w_a[:, 2, :], a_wv), (w_a[:, 3, :], a_wo),
            (stage[:, 0:3, :], b_wattn.rearrange("(j p) d -> p j d", p=P)),
            (stage[:, 3, :], b_wout), (stage[:, 4, :], r_wq), (stage[:, 5, :], r_wk),
            (stage[:, 6, :], r_wv), (stage[:, 7, :], r_wp),
            (stage[:, 8:10, :], r_rel.rearrange("(j p) d -> p j d", p=P)),
            (stage[:, 10:10 + KD, :], d_dw.rearrange("e c d -> (e c) d").rearrange("(j p) d -> p j d", p=P)),
            (stage[:, 10 + KD:10 + 2 * KD, :].rearrange("p j (e c) -> p (j e) c", e=2),
             d_uw.rearrange("e d c -> d e c")),
            (stage_gate[0:E, :], d_gate),
            (bp_row[:, :], r_bp.rearrange("(a n) -> a n", a=1)),
            (up_b[:, :], d_ub), (down_b[:, :], d_db.rearrange("e c -> (e c)").rearrange("(k p) -> p k", p=P)),
            (wg[:, :, :], m_wg.rearrange("e d f -> d e f")), (wu[:, :, :], m_wu.rearrange("e d f -> d e f")),
            (wk_l[:, :], l_wk), (wv_l[:, :], l_wv), (wq_l[:, :], l_wq), (wbeta[:, :], l_wbeta),
            (wout_l[:, :, :], l_wout.rearrange("(c p) d -> p c d", p=P)),
        ] + [(wd[0:n, :, j, :], m_wd[:, f0:f0 + n, :].rearrange("e f d -> f e d")) for j, (f0, n) in enumerate(FT)]
        LOADED = 16 * len(loads)

        @block.sync
        def _(sp):
            with nc.allow_non_contiguous_dma(reason="biases by partition"):
                for dst, src in loads:
                    sp.dma_start(dst, src).then_inc(loaded, 16)
            with sp.Fori(0, B) as b:
                sp.dma_start(x[:, :, :], x_rows[b]).then_inc(x_in, 16)
                sp.wait_ge(x_done, 8)
                sp.dma_start(out_rows[b], x[:, :, :]).then_inc(x_out, 16)
                sp.wait_ge(ended, 4)
                sp.wait_ge(x_out, 16)
                sp.sem_clear(turn_sems)
                sp.nop().then_inc(started, 1)

        def pool_norm(eng, n):
            eng.wait_ge(normed, 8 * n + 8)
            eng.tensor_scalar(rstd[:, :], moments[:, :, 1], EPS, None, ALU.add).then_inc(pool_step, 1)
            eng.wait_ge(pool_step, n + 1)
            eng.tensor_tensor(rstd[:, :], rstd[:, :], half[:, 1:2].to_broadcast([P, NT]),
                              ALU.pow).then_inc(rstd_ok, 1)

        def pool_split(eng, n):
            for w in range(2):
                eng.wait_ge(a_res, 2 * n + w + 1)
                eng.tensor_copy(parts[:, w, 1, :], res[:, w, :]).then_inc(a_mid, 1)

        def pool_rel(eng):
            for c in range(P // IC):
                eng.wait_ge(r_even, 4 * (c + 1))
                for b in (0, 4, 7, 8):
                    v = sc[:, :, b, IC * c:IC * c + IC]
                    eng.affine_select(out=v, in_=v, compare_op=ALU.is_gt, fill=0.0, base=IC * c,
                                      pattern=[[0, H], [1, IC]], channel_multiplier=-1).then_inc(r_diag, 1)

        def pool_lin(eng):
            eng.wait_ge(xnT_ok, 5)
            eng.memset(l_st[:, :, :, :], 0.0).then_inc(l_zero, 1)
            eng.wait_ge(l_ssc, 1)
            eng.tensor_tensor(l_inv[:, :, :, :], l_inv[:, :, :, :],
                              half[:, 0:1].unsqueeze(2).unsqueeze(3).to_broadcast([P, 2, NT, H]),
                              ALU.pow).then_inc(l_norm, 1)
            eng.wait_ge(l_bok, 1)
            for c in range(NC2 + 2):
                if c < NC2:
                    eng.wait_ge(l_vks, c + 1)
                    v = l_v[:, :, P * c:P * c + P].rearrange("p t (r d) -> p t r d", r=2)
                    eng.tensor_tensor(v, v, l_beta[:, :, 2 * c:2 * c + 2].unsqueeze(3)
                                      .to_broadcast([P, NT, 2, DM]), ALU.mult).then_inc(l_bv, 1)
                if c >= 2:
                    eng.wait_ge(l_ts, c - 1)
                    eng.wait_ge(l_bv, c - 1)
                    v = l_v[:, :, P * (c - 2):P * (c - 1)]
                    eng.tensor_tensor(v, v, l_tmp[:, c % 2, :, :], ALU.add).then_inc(l_os, 1)

        @block.gpsimd
        def _(eng):
            zeros = [ident, identb, mask_qk, mask_kq, spread_q, spread_k, pick_max, neg_maxT]
            for z in zeros:
                eng.memset(z[...], 0.0).then_inc(zeroed, 1)
            for o in (keep_ge, head_of, pair_of, before, ones):
                eng.memset(o[...], 1.0).then_inc(zeroed, 1)
            eng.memset(half[:, 0:1], 0.5).then_inc(zeroed, 1)
            eng.memset(half[:, 1:2], -0.5).then_inc(zeroed, 1)
            eng.memset(values[:, :, :, HD:HD + 1], 1.0).then_inc(zeroed, 1)
            eng.wait_ge(zeroed, len(zeros) + 8)
            for m in (ident, identb):
                eng.affine_select(out=m[:, :], in_=m[:, :], compare_op=ALU.not_equal, fill=1.0, base=0,
                                  pattern=[[-1, P]], channel_multiplier=1).then_inc(const, 1)
            eng.affine_select(out=mask_qk[:, :], in_=mask_qk[:, :], compare_op=ALU.is_ge, fill=MASKED, base=0,
                              pattern=[[-1, P]], channel_multiplier=1).then_inc(const, 1)
            eng.affine_select(out=mask_kq[:, :], in_=mask_kq[:, :], compare_op=ALU.is_ge, fill=MASKED, base=0,
                              pattern=[[1, P]], channel_multiplier=-1).then_inc(const, 1)
            eng.affine_select(out=keep_ge[:, :], in_=keep_ge[:, :], compare_op=ALU.is_ge, fill=0.0, base=0,
                              pattern=[[-1, P]], channel_multiplier=1).then_inc(const, 1)
            eng.affine_select(out=before[:, :, :], in_=before[:, :, :], compare_op=ALU.is_gt, fill=0.0, base=0,
                              pattern=[[1, E], [-1, E]], channel_multiplier=0).then_inc(const, 1)
            n_const = 6
            for spread, of_slot in ((spread_q, Q_PART), (spread_k, K_PART)):
                for slot, x_part in enumerate(of_slot):
                    v = spread[:, x_part, :, :, slot, :]
                    eng.affine_select(out=v, in_=v, compare_op=ALU.not_equal, fill=1.0, base=0,
                                      pattern=[[-16, H // 2], [-8, 2], [-1, HD]],
                                      channel_multiplier=1).then_inc(const, 1)
                    n_const += 1
            for p3 in range(3):
                eng.wait_ge(const, n_const)
                eng.affine_select(out=pick_max[:, :, :], in_=pick_max[:, :, :], compare_op=ALU.not_equal,
                                  fill=1.0, base=-G4 * p3, pattern=[[-1, G4], [0, P]],
                                  channel_multiplier=1).then_inc(const, 1)
                n_const += 1
            for tab, n, width in ((head_of, H, HD), (pair_of, 2, DM)):
                eng.affine_select(out=tab[:, :], in_=tab[:, :], compare_op=ALU.is_ge, fill=0.0, base=0,
                                  pattern=[[-width, n]], channel_multiplier=1).then_inc(const, 1)
                n_const += 1
                eng.wait_ge(const, n_const)
                eng.affine_select(out=tab[:, :], in_=tab[:, :], compare_op=ALU.is_gt, fill=0.0, base=width,
                                  pattern=[[width, n]], channel_multiplier=-1).then_inc(const, 1)
                n_const += 1
            assert n_const == CONSTS
            with eng.Fori(0, B) as b:
                pool_norm(eng, 0)
                pool_split(eng, 0)
                pool_norm(eng, 1)
                pool_norm(eng, 2)
                pool_split(eng, 1)
                pool_norm(eng, 3)
                pool_norm(eng, 4)
                pool_lin(eng)
                pool_norm(eng, 5)
                pool_norm(eng, 6)
                pool_split(eng, 2)
                pool_rel(eng)
                pool_norm(eng, 7)
                eng.nop().then_inc(ended, 1)
                eng.wait_ge(started, b + 1)

        def act_norm(eng, n):
            eng.wait_ge(xn_T, n + 1)
            eng.activation(xnT[:, :], bank(7), ACT.Copy).then_inc(xnT_ok, 1)

        def act_parts(eng, n, scale):
            eng.wait_ge(a_proj, 3 * n + 1)
            eng.activation(parts[:, 0, 0, :], bank(0), ACT.Copy, scale=scale).then_inc(a_hi, 1)
            eng.wait_ge(a_proj, 3 * n + 2)
            eng.activation(parts[:, 1, 0, :], bank(1), ACT.Copy).then_inc(a_hi, 1)
            for g in range(H // 2):
                eng.wait_ge(a_spread, H * n + 2 * g + 1)
                eng.activation(q_st[:, g, :], bank(3 + 2 * g % 4), ACT.Copy).then_inc(a_qst, 1)

        def act_attn(eng, n, scale):
            act_parts(eng, n, scale)

            def max_rows(G):
                eng.wait_ge(a_maxT, NG * n + G + 1)
                if G >= 2:
                    eng.wait_ge(a_s2, 3 * (H * n + G4 * (G - 1)))
                eng.activation(neg_maxT[0:3 * G4, G % 2, :], bank(6 + G % 2)[0:3 * G4, 0:T // 2].bitcast(BF16),
                               ACT.Copy).then_inc(a_mrow, 1)

            max_rows(0)
            for h in range(H):
                if h >= 2:
                    eng.wait_ge(a_pv, H * n + h - 1)
                for j in range(3):
                    eng.wait_ge(a_s2, 3 * (H * n + h) + j + 1)
                    eng.activation(prob[:, h % 2, JOB_AT[j]:JOB_AT[j] + JOB_N[j]],
                                   bank(3 + j)[:, 0:JOB_N[j]], ACT.Exp).then_inc(a_prob, 1)
                if h % G4 == G4 - 1 and h < H - 1:
                    max_rows(h // G4 + 1)
            eng.wait_ge(a_oT, n + 1)
            eng.activation(xnT[:, :], bank(0), ACT.Copy).then_inc(a_oTs, 1)

        def act_moe(eng, n):
            eng.wait_ge(m_lgd, n + 1)
            eng.activation(ex[:, :, :], lgd[:, :, :], ACT.Exp).then_inc(m_ex, 1)
            for i in range(E * NF):
                w = FT[i % NF][1]
                eng.wait_ge(m_g, E * NF * n + i + 1)
                if i >= 2:
                    eng.wait_ge(m_h, E * NF * n + i - 1)
                eng.activation(silu[0:w, i % 2, :], bank(i % 2)[0:w, :], ACT.Silu).then_inc(m_silu, 1)

        def act_lin(eng):
            eng.wait_ge(l_bz, 1)
            eng.activation(l_beta[:, :, :], bank(6)[:, 0:NT * H].rearrange("p (t h) -> p t h", t=NT),
                           ACT.Exp, scale=-1.0).then_inc(l_be, 1)
            for i in range(2 * NC2):
                dst = (l_qT, l_kT)[i % 2][:, i // 2, :]
                eng.wait_ge(l_pq, i + 1)
                eng.activation(dst, bank(i % 2), ACT.Copy).then_inc(l_qk, 1)
                eng.wait_ge(l_qk, i + 1)
                if i >= 2:
                    eng.wait_ge(l_ss, i - 1)
                eng.activation(l_sq[:, i % 2, :], dst, ACT.Square).then_inc(l_sqr, 1)

            def columns(c):
                eng.wait_ge(l_oT, c + 1)
                eng.activation(l_kT[:, c, :], bank(6 + c % 2), ACT.Copy).then_inc(l_oTs, 1)

            for c in range(NC2):
                eng.wait_ge(l_stp, c + 1)
                if c >= 2:
                    eng.wait_ge(l_o, c - 1)
                else:
                    eng.wait_ge(l_zero, 1)
                for r in range(2):
                    own = slice(DM * r, DM * r + DM)
                    i = eng.activation(l_st[own, c % 2, :, own],
                                       bank(2 + c % 2)[own, 0:(NT - 1) * P].rearrange("p (u d) -> p u d", d=P)[:, :, own],
                                       ACT.Copy)
                i.then_inc(l_sts, 1)
                if c >= 2:
                    columns(c - 2)
            columns(NC2 - 2)
            columns(NC2 - 1)

        def act_adapter(eng, n):
            eng.wait_ge(d_lgs, n + 1)
            eng.activation(d_ex[:, :], d_lg[:, :], ACT.Exp, bias=d_negm[:, 0:1],
                           accum_out=d_z[:, 0:1]).then_inc(d_exs, 1)
            for k in range(KD):
                eng.wait_ge(d_dn, KD * n + k + 1)
                eng.activation(d_hid[:, k, :], bank(k), ACT.Gelu, bias=down_b[:, k:k + 1]).then_inc(d_hs, 1)
            eng.wait_ge(d_wTp, n + 1)
            eng.activation(d_wT[0:E, :], bank(5)[0:E, 0:P], ACT.Copy).then_inc(d_wTs, 1)

        def act_rel(eng):
            act_parts(eng, 2, float(HD) ** -0.5)
            for i in range(P // 8):
                eng.wait_ge(r_rel_ok, 2 * i + 2)
                v = bank((2 * i + 1) % 4).rearrange("p (i t h) -> p h t i", i=8, t=NT)
                eng.activation(sc[:, :, 1:10:4, 8 * i:8 * i + 8], v[:, :, 1:4, :], ACT.Copy)
                eng.activation(sc[:, :, 3, 8 * i:8 * i + 8], v[:, :, 3, :], ACT.Copy).then_inc(r_odd, 1)

            def exps(h):
                at = {0: 0, 1: P, 2: 3 * P, 3: 6 * P}
                if h >= 2:
                    eng.wait_ge(r_pT, 3 * (h - 1))
                for n, (t, bk, col) in enumerate(ROW_JOBS):
                    eng.wait_ge(r_max, 4 * h + (3 if n == 1 else n + 1))
                    eng.activation(r_prob[:, h % 2, at[t]:at[t] + (t + 1) * P],
                                   bank(bk)[:, col:col + (t + 1) * P], ACT.Exp,
                                   bias=r_neg_max[:, h % 2, t:t + 1]).then_inc(r_p, 1)

            def columns(h):
                for j in range(2):
                    eng.wait_ge(r_pT, 3 * h + j + 1)
                    if h >= 2:
                        eng.wait_ge(a_pv, 2 * H + h - 1)
                    eng.activation(r_probT[:, h % 2, JOB_AT[j]:JOB_AT[j] + JOB_N[j]],
                                   bank(5 + (3 * h + j) % 2)[:, 0:JOB_N[j]], ACT.Copy).then_inc(r_pTa, 1)

            for i in range(1, H + 2):
                if i <= H:
                    exps(i - 1)
                if i >= 2:
                    columns(i - 2)
            eng.wait_ge(a_oT, 3)
            eng.activation(xnT[:, :], bank(0), ACT.Copy).then_inc(a_oTs, 1)

        @block.scalar
        def _(eng):
            eng.wait_ge(weights, 6)
            with eng.Fori(0, B) as b:
                act_norm(eng, 0)
                act_attn(eng, 0, float(HD) ** -0.5)
                act_norm(eng, 1)
                act_moe(eng, 0)
                act_norm(eng, 2)
                act_attn(eng, 1, float(P) ** -0.5)
                act_norm(eng, 3)
                act_moe(eng, 1)
                act_norm(eng, 4)
                act_lin(eng)
                act_norm(eng, 5)
                act_adapter(eng, 0)
                act_norm(eng, 6)
                act_rel(eng)
                act_norm(eng, 7)
                act_adapter(eng, 1)
                eng.nop().then_inc(ended, 1)
                eng.wait_ge(started, b + 1)

        def pe_norm(eng, n):
            for t in range(NT):
                eng.wait_ge(xn_ok, 4 * n + t + 1)
                m = eng.transpose(bank(7)[:, P * t:P * t + P], xn[:, t, :], ident[:, :])
            m.then_inc(xn_T, 1)

        def pe_stack(eng, n, w):
            eng.wait_ge(xnT_ok, (0, 2, 6)[n] + 1)
            eng.matmul(bank(0), w[:, 0, :], xnT[:, :], start=True, stop=True).then_inc(a_proj, 1)
            eng.matmul(bank(1), w[:, 1, :], xnT[:, :], start=True, stop=True).then_inc(a_proj, 1)
            for t in range(NT):
                m = eng.matmul(bank(2)[:, P * t:P * t + P], xnT[:, P * t:P * t + P], w[:, 2, :],
                               start=True, stop=True)
            m.then_inc(a_proj, 1)
            for i in range(H):
                g, w2 = i // 2, i % 2
                if g == 0:
                    eng.wait_ge(a_hi, 2 * n + w2 + 1)
                    eng.wait_ge(a_mid, 2 * n + w2 + 1)
                    eng.wait_ge(a_lo, 2 * n + w2 + 1)
                if i >= 4:
                    eng.wait_ge((a_qst, a_kst)[w2], H // 2 * n + g - 1)
                for x_part in range(3):
                    spread = (spread_q, spread_k)[w2][:, x_part, g].rearrange("p r s d -> p (r s d)")
                    m = eng.matmul(bank(3 + i % 4), spread, parts[:, w2, x_part, :],
                                   start=(x_part == 0), stop=(x_part == 2))
                m.then_inc(a_spread, 1)

        def pe_out(eng, n, w, bias):
            eng.wait_ge(a_o, NG * (n + 1))
            for t in range(NT):
                m = eng.transpose(bank(0)[:, P * t:P * t + P], xn[:, t, :], ident[:, :])
            m.then_inc(a_oT, 1)
            eng.wait_ge(a_oTs, n + 1)
            for t in range(NT):
                m = eng.matmul(bank(1)[:, P * t:P * t + P], xnT[:, P * t:P * t + P], w[:, 3, :],
                               start=True, stop=bias is None)
                if bias is not None:
                    m = eng.matmul(bank(1)[:, P * t:P * t + P], ones[0:1, 0:P], bias, start=False, stop=True)
            m.then_inc(a_y, 1)

        def rows_of(G):
            return ([[(hh, 3, 0)] for hh in range(G4)] + [[(hh, 2, 0)] for hh in range(G4)] +
                    [[(r, t, 0), (r + 2, t, (t + 1) * P)] for t in (1, 0) for r in range(2)])

        NROW = len(rows_of(0))

        def stacked(st, h, cols):
            r = h % 2
            return st[64 * r:64 * r + KROWS, h // 2, cols]

        def pe_attn(eng, n, w):
            pe_stack(eng, n, w)

            def score_rows(G, jobs):
                for i in jobs:
                    k = NROW * G + i
                    if k == 2:
                        eng.wait_ge(a_v, n + 1)
                    if k >= 3:
                        eng.wait_ge(a_max, NROW * NG * n + k - 2)
                    for hh, t, col in rows_of(G)[i]:
                        h, N = G4 * G + hh, (t + 1) * P
                        eng.wait_ge(a_qst, H // 2 * n + h // 2 + 1)
                        eng.wait_ge(a_kst, H // 2 * n + h // 2 + 1)
                        eng.matmul(bank(k % 3)[:, col:col + N], stacked(q_st, h, slice(P * t, P * t + P)),
                                   stacked(k_st, h, slice(0, N)), start=True, stop=False)
                        m = eng.matmul(bank(k % 3)[:, col + N - P:col + N], identb[:, :], mask_qk[:, :],
                                       start=False, stop=True)
                    m.then_inc(a_s1, 1)

            def max_columns(G):
                eng.wait_ge(a_mparts, NG * n + G + 1)
                if G >= 2:
                    eng.wait_ge(a_o, NG * n + G - 1)
                for t in range(NT):
                    m = eng.transpose(bank(6 + G % 2)[0:3 * G4, P // 2 * t:P // 2 * (t + 1)].bitcast(BF16),
                                      max_part[:, G % 2, t, 0:3 * G4], identb[:, :])
                m.then_inc(a_maxT, 1)

            def score_columns(h):
                G, hh = h // G4, h % G4
                if hh == 0:
                    eng.wait_ge(a_mrow, NG * n + G + 1)
                for j in range(3):
                    if h >= 1:
                        eng.wait_ge(a_prob, 3 * (H * n + h - 1) + j + 1)
                    col = 0
                    for s in JOBS[j]:
                        N = T - P * s
                        eng.matmul(bank(3 + j)[:, col:col + N], stacked(k_st, h, slice(P * s, P * s + P)),
                                   stacked(q_st, h, slice(P * s, T)), start=True, stop=False)
                        eng.matmul(bank(3 + j)[:, col:col + P], identb[:, :], mask_kq[:, :],
                                   start=False, stop=False)
                        m = eng.matmul(bank(3 + j)[:, col:col + N], pick_max[:, hh, :],
                                       neg_maxT[:, G % 2, P * s:T], start=False, stop=True)
                        col += N
                    m.then_inc(a_s2, 1)

            def weigh(h):
                G, hh = h // G4, h % G4
                eng.wait_ge(a_prob, 3 * (H * n + h + 1))
                for t in range(NT):
                    o = bank(6 + G % 2)[:, (G4 * t + hh) * (HD + 1):(G4 * t + hh + 1) * (HD + 1)]
                    for s in range(t + 1):
                        b = SLOT[(s, t)]
                        m = eng.matmul(o, prob[:, h % 2, P * b:P * b + P], values[:, s, h, :],
                                       start=(s == 0), stop=(s == t))
                m.then_inc(a_pv, 1)

            score_rows(0, range(NROW))
            max_columns(0)
            chunks = [range(0, 3), range(3, 6), range(6, 9), range(9, NROW)]
            for h in range(H):
                G = h // G4
                score_columns(h)
                if G < NG - 1:
                    score_rows(G + 1, chunks[h % G4])
                if h >= 1:
                    weigh(h - 1)
                if h % G4 == G4 - 1 and G < NG - 1:
                    max_columns(G + 1)
            weigh(H - 1)
            pe_out(eng, n, w, None)

        def pe_moe(eng, n):
            eng.wait_ge(xnT_ok, 2 * n + 2)
            for t in range(NT):
                eng.matmul(bank(6)[:, E * t:E * t + E], xnT[:, P * t:P * t + P], ws[:, :], start=True, stop=False)
                m = eng.matmul(bank(6)[:, E * t:E * t + E], ones[0:1, 0:P], bs_row[:, :], start=False, stop=True)
            m.then_inc(m_logit, 1)

            def down(e):
                eng.wait_ge(m_h, NF * (E * n + e + 1))
                if e >= 2:
                    eng.wait_ge(m_acc, E * n + e - 1)
                for t in range(NT):
                    for j, (_, w) in enumerate(FT):
                        m = eng.matmul(bank(4 + e % 2)[:, P * t:P * t + P],
                                       hidden[0:w, e % 2, j, P * t:P * t + P], wd[0:w, e, j, :],
                                       start=(j == 0), stop=(j == NF - 1))
                m.then_inc(m_y, 1)

            for e in range(E):
                for j, (f0, w) in enumerate(FT):
                    i = NF * e + j
                    if i >= 2:
                        eng.wait_ge(m_silu, E * NF * n + i - 1)
                    eng.matmul(bank(i % 2)[0:w, :], wg[:, e, f0:f0 + w], xnT[:, :],
                               start=True, stop=True).then_inc(m_g, 1)
                    if i >= 2:
                        eng.wait_ge(m_h, E * NF * n + i - 1)
                    eng.matmul(bank(2 + i % 2)[0:w, :], wu[:, e, f0:f0 + w], xnT[:, :],
                               start=True, stop=True).then_inc(m_u, 1)
                if e >= 1:
                    down(e - 1)
            down(E - 1)

        def pe_lin(eng):
            eng.wait_ge(xnT_ok, 5)
            for t in range(NT):
                m = eng.matmul(bank(6)[:, H * t:H * t + H], xnT[:, P * t:P * t + P], wbeta[:, :],
                               start=True, stop=True)
            m.then_inc(l_bz, 1)

            def sum_squares(i):
                eng.wait_ge(l_sqr, i + 1)
                for t in range(NT):
                    at = (i % 2) * NT * H + H * t + 2 * (i // 2)
                    m = eng.matmul(bank(5)[:, at:at + 2], l_sq[:, i % 2, P * t:P * t + P], pair_of[:, :],
                                   start=True, stop=True)
                m.then_inc(l_ss, 1)

            for i in range(2 * NC2):
                if i >= 2:
                    eng.wait_ge(l_qk, i - 1)
                eng.matmul(bank(i % 2), (wq_l, wk_l)[i % 2][:, P * (i // 2):P * (i // 2) + P], xnT[:, :],
                           start=True, stop=True).then_inc(l_pq, 1)
                if i >= 2:
                    eng.wait_ge(l_kv, i - 1)
                t, c = (i % 8) // 2, i % 2
                eng.matmul(bank(2 + i % 2), xnT[:, P * t:P * t + P],
                           (wk_l, wv_l)[i // 8][:, 512 * c:512 * c + 512], start=True, stop=True).then_inc(l_pn, 1)
                if i >= 1:
                    sum_squares(i - 1)
            sum_squares(2 * NC2 - 1)

            def scores(c):
                for r in range(2):
                    h = 2 * c + r
                    if h >= 2:
                        eng.wait_ge(l_wts, h - 1)
                    else:
                        eng.wait_ge(l_qk, 2 * NC2)
                    for t in range(NT):
                        m = eng.matmul(bank(r)[:, P * t:P * t + P], l_kT[64 * r:64 * r + 64, c, P * t:P * t + P],
                                       l_qT[64 * r:64 * r + 64, c, P * t:P * t + P], start=True, stop=True)
                    m.then_inc(l_sc, 1)

            def states(c):
                eng.wait_ge(l_vks, c + 1)
                if c >= 2:
                    eng.wait_ge(l_sts, c - 1)
                else:
                    eng.wait_ge(l_kv, 2 * NC2)
                for u in range(NT - 1):
                    for s in range(u + 1, NT):
                        m = eng.matmul(bank(2 + c % 2)[:, P * u:P * u + P], l_k[:, s, P * c:P * c + P],
                                       l_vk[:, s, P * c:P * c + P], start=(s == u + 1), stop=(s == NT - 1))
                m.then_inc(l_stp, 1)

            def outputs(c):
                eng.wait_ge(l_wts, 2 * c + 2)
                eng.wait_ge(l_sts, c + 1)
                if c >= 2:
                    eng.wait_ge(l_ts, c - 1)
                else:
                    eng.wait_ge(l_ssc, 1)
                for t in range(NT):
                    o = bank(4 + c % 2)[:, P * t:P * t + P]
                    for r in range(2):
                        m = eng.matmul(o[:, DM * r:DM * r + DM], l_wt[:, r, t, :],
                                       l_vk[:, t, P * c + DM * r:P * c + DM * r + DM],
                                       start=(r == 0), stop=(t == NT - 1 and r == 1), skip_group_check=True)
                    if t < NT - 1:
                        m = eng.matmul(o, l_qT[:, c, P * t:P * t + P], l_st[:, c % 2, t, :],
                                       start=False, stop=True, skip_group_check=True)
                m.then_inc(l_o, 1)

            def transposes(c):
                eng.wait_ge(l_os, c + 1)
                if c >= 2:
                    eng.wait_ge(l_oTs, c - 1)
                for t in range(NT):
                    m = eng.transpose(bank(6 + c % 2)[:, P * t:P * t + P], l_v[:, t, P * c:P * c + P], ident[:, :])
                m.then_inc(l_oT, 1)

            for c in range(NC2 + 3):
                if c < NC2:
                    scores(c)
                    states(c)
                if 1 <= c <= NC2:
                    outputs(c - 1)
                if c >= 3:
                    transposes(c - 3)
            eng.wait_ge(l_oTs, NC2)
            for t in range(NT):
                for c in range(NC2):
                    m = eng.matmul(bank(0)[:, P * t:P * t + P], l_kT[:, c, P * t:P * t + P], wout_l[:, c, :],
                                   start=(c == 0), stop=(c == NC2 - 1))
            m.then_inc(l_y, 1)

        def pe_adapter(eng, n):
            eng.wait_ge(xnT_ok, (6, 8)[n])
            for k in range(KD):
                eng.matmul(bank(k), downT[:, k, :], xnT[:, :], start=True, stop=True).then_inc(d_dn, 1)
            eng.wait_ge(d_pool, n + 1)
            eng.matmul(bank(6)[:, 0:E], pool_rep[:, :], gateT[:, :], start=True, stop=True).then_inc(d_gate_ok, 1)
            eng.wait_ge(d_ws, n + 1)
            eng.transpose(bank(5)[0:E, 0:P], d_w[:, :], ident[:, :]).then_inc(d_wTp, 1)
            eng.wait_ge(d_wTs, n + 1)
            eng.wait_ge(d_hs, KD * (n + 1))
            eng.wait_ge(d_ups, n + 1)
            for t in range(NT):
                o = bank(4)[:, P * t:P * t + P]
                for k in range(KD):
                    eng.matmul(o, d_hid[:, k, P * t:P * t + P], d_up[:, k, :], start=(k == 0), stop=False)
                m = eng.matmul(o, d_wT[0:E, :], up_b[:, :], start=False, stop=True)
            m.then_inc(d_y, 1)

        def pe_rel(eng, w):
            pe_stack(eng, 2, w)
            eng.wait_ge(a_v, 3)
            eng.wait_ge(r_shift, 1)
            eng.wait_ge(a_qst, 3 * H // 2)
            for i in range(P // 8):
                for par in range(2):
                    k = 2 * i + par
                    if i >= 2:
                        eng.wait_ge((r_even, r_odd)[par], i - 1)
                    eng.wait_ge(r_qm, 8 * i // IC + 1)
                    for q in range(8 * i, 8 * i + 8):
                        first = (P * par - q) % (2 * P)
                        m = eng.matmul(bank(k % 4)[:, 64 * (q % 8):64 * (q % 8) + 64], relT[:, first:first + P],
                                       q_masked[:, (q // IC) % 2, q % IC, :], start=True, stop=True)
                    m.then_inc(r_rel_ok, 1)

            def qk(h):
                for j in range(3):
                    k = 3 * h + j
                    if k >= 2:
                        eng.wait_ge(r_sum, k - 1)
                    else:
                        eng.wait_ge(r_even, P // 8)
                        eng.wait_ge(r_odd, P // 8)
                        eng.wait_ge(a_kst, 3 * H // 2)
                    col = 0
                    for s in JOBS[j]:
                        N = T - P * s
                        eng.matmul(bank(k % 2)[:, col:col + N], stacked(k_st, h, slice(P * s, P * s + P)),
                                   stacked(q_st, h, slice(P * s, T)), start=True, stop=False)
                        m = eng.matmul(bank(k % 2)[:, col:col + P], identb[:, :], mask_kq[:, :],
                                       start=False, stop=True)
                        col += N
                    m.then_inc(r_main, 1)

            def rows(h):
                eng.wait_ge(r_sum, 3 * (h + 1))
                for i, (t, bk, col) in enumerate(ROW_JOBS):
                    if h >= 1 and i != 2:
                        eng.wait_ge(r_p, 4 * (h - 1) + (1, 3, 3, 4)[i])
                    for s in range(t + 1):
                        m = eng.transpose(bank(bk)[:, col + P * s:col + P * s + P], sc[:, h, SLOT[(s, t)], :],
                                          ident[:, :])
                    if i != 1:
                        m.then_inc(r_sT, 1)

            def columns(h):
                at = {0: 0, 1: P, 2: 3 * P, 3: 6 * P}
                eng.wait_ge(r_p, 4 * (h + 1))
                for j in range(3):
                    k = 3 * h + j
                    if k >= 2:
                        h2, j2 = (k - 2) // 3, (k - 2) % 3
                        if j2 < 2:
                            eng.wait_ge(r_pTa, 2 * h2 + j2 + 1)
                        else:
                            eng.wait_ge(r_pTv, h2 + 1)
                    first = JOB_AT[j] // P
                    for b in range(first, first + JOB_N[j] // P):
                        s, t = BLOCKS[b]
                        m = eng.transpose(bank(5 + k % 2)[:, P * (b - first):P * (b - first) + P],
                                          r_prob[:, h % 2, at[t] + P * s:at[t] + P * s + P], ident[:, :])
                    m.then_inc(r_pT, 1)

            def weigh(h):
                G, hh = h // G4, h % G4
                eng.wait_ge(r_pTa, 2 * h + 2)
                eng.wait_ge(r_pTv, h + 1)
                if hh == 0 and G >= 1:
                    eng.wait_ge(a_o, 2 * NG + G)
                for t in range(NT):
                    o = bank(7)[:, (G4 * t + hh) * (HD + 1):(G4 * t + hh + 1) * (HD + 1)]
                    for s in range(t + 1):
                        b = SLOT[(s, t)]
                        m = eng.matmul(o, r_probT[:, h % 2, P * b:P * b + P], values[:, s, h, :],
                                       start=(s == 0), stop=(s == t))
                m.then_inc(a_pv, 1)

            for i in range(H + 3):
                if i < H:
                    qk(i)
                if 1 <= i <= H:
                    rows(i - 1)
                if 2 <= i <= H + 1:
                    columns(i - 2)
                if i >= 3:
                    weigh(i - 3)
            pe_out(eng, 2, w, bp_row[:, :])

        @block.tensor
        def _(eng):
            eng.wait_ge(loaded, LOADED)
            eng.wait_ge(const, CONSTS)
            for n in range(NSTAGE):
                m = eng.transpose(bank(n // 4)[:, P * (n % 4):P * (n % 4) + P], stage[:, n, :], ident[:, :])
                if n % 4 == 3 or n == NSTAGE - 1:
                    m.then_inc(stage_T, 1)
            eng.transpose(bank(6)[:, 0:E], stage_gate[0:E, :], ident[0:E, 0:E]).then_inc(stage_T, 1)
            eng.wait_ge(weights, 6)
            with eng.Fori(0, B) as b:
                pe_norm(eng, 0)
                pe_attn(eng, 0, w_a)
                pe_norm(eng, 1)
                pe_moe(eng, 0)
                pe_norm(eng, 2)
                pe_attn(eng, 1, w_b)
                pe_norm(eng, 3)
                pe_moe(eng, 1)
                pe_norm(eng, 4)
                pe_lin(eng)
                pe_norm(eng, 5)
                pe_adapter(eng, 0)
                pe_norm(eng, 6)
                pe_rel(eng, w_r)
                pe_norm(eng, 7)
                pe_adapter(eng, 1)
                eng.nop().then_inc(ended, 1)
                eng.wait_ge(started, b + 1)

        @block.vector
        def _(eng):
            steps = [0]

            def link(ins):
                steps[0] += 1
                ins.then_inc(step, 1)
                eng.wait_ge(step, steps[0])

            def flat(n):
                return bank(n).rearrange("p (t d) -> p t d", t=NT)

            def norm(n):
                if n == 0:
                    eng.wait_ge(x_in, 16)
                else:
                    eng.wait_ge(x_done, n)
                for t in range(NT):
                    eng.bn_stats(stats[:, t, :], x[:, t, :]).then_inc(normed, 1)
                for t in range(NT):
                    eng.wait_ge(normed, 8 * n + (t + 1 if t == 0 else 4 + t))
                    eng.bn_aggr(moments[:, t, :], stats[:, t, :]).then_inc(normed, 1)
                eng.wait_ge(rstd_ok, n + 1)
                for t in range(NT):
                    eng.tensor_scalar(xn[:, t, :], x[:, t, :], moments[:, t, 0:1], rstd[:, t:t + 1],
                                      ALU.subtract, ALU.mult).then_inc(xn_ok, 1)

            def add_to_x(bk):
                eng.tensor_tensor(x[:, :, :], x[:, :, :], flat(bk), ALU.add).then_inc(x_done, 1)

            def parts_of_qk(n, scale):
                for w in range(2):
                    eng.wait_ge(a_hi, 2 * n + w + 1)
                    eng.scalar_tensor_tensor(out=res[:, w, :], in0=bank(w), scalar=(scale, 1.0)[w],
                                             in1=parts[:, w, 0, :], op0=ALU.mult,
                                             op1=ALU.subtract).then_inc(a_res, 1)
                if n == 2:
                    eng.tensor_scalar(q_shift[:, 1:T + 1], bank(0), scale, None, ALU.mult)
                    eng.memset(q_shift[:, 0:1], 0.0).then_inc(r_shift, 1)
                eng.wait_ge(a_proj, 3 * n + 3)
                eng.tensor_copy(values[:, :, :, 0:HD], bank(2).rearrange("p (t h d) -> p t h d", t=NT, h=H))\
                   .then_inc(a_v, 1)
                for w in range(2):
                    eng.wait_ge(a_res, 2 * n + w + 1)
                    eng.wait_ge(a_mid, 2 * n + w + 1)
                    eng.tensor_tensor(parts[:, w, 2, :], res[:, w, :], parts[:, w, 1, :],
                                      ALU.subtract).then_inc(a_lo, 1)
                for g in range(H // 2):
                    eng.wait_ge(a_spread, H * n + 2 * g + 2)
                    eng.tensor_copy(k_st[:, g, :], bank(3 + (2 * g + 1) % 4)).then_inc(a_kst, 1)

            def heads_out(n, G, bk, inv):
                eng.wait_ge(a_pv, H * n + G4 * (G + 1))
                o = bank(bk)[:, 0:NT * G4 * (HD + 1)].rearrange("p (t h d) -> p t h d", t=NT, h=G4)
                link(eng.reciprocal(inv[:, G % 2, :, :].unsqueeze(3), o[:, :, :, HD:HD + 1]))
                eng.tensor_tensor(
                    xn[:, :, HD * G4 * G:HD * G4 * (G + 1)].rearrange("p t (h d) -> p t h d", h=G4),
                    o[:, :, :, 0:HD], inv[:, G % 2, :, :].unsqueeze(3).to_broadcast([P, NT, G4, HD]),
                    ALU.mult).then_inc(a_o, 1)

            def attn(n, scale):
                parts_of_qk(n, scale)

                def row_max(G, jobs):
                    for i in jobs:
                        k = NROW * (NG * n + G) + i
                        eng.wait_ge(a_s1, k + 1)
                        job = rows_of(G)[i]
                        hh, t, _ = job[0]
                        src = bank((NROW * G + i) % 3)[:, 0:len(job) * (t + 1) * P]
                        src = src.rearrange("p (h k) -> p h k", h=len(job))
                        hs = slice(hh, hh + 2 * len(job) - 1, 2)
                        eng.tensor_reduce(neg_max[:, G % 2, t, hs], src, AX.X, ALU.max,
                                          negate=True).then_inc(a_max, 1)

                def split_max(G):
                    b = G % 2
                    eng.wait_ge(a_max, NROW * (NG * n + G + 1))
                    hi, mid, lo = (max_part[:, b, :, G4 * p:G4 * p + G4] for p in range(3))
                    link(eng.tensor_copy(hi, neg_max[:, b, :, :]))
                    link(eng.tensor_tensor(max_res[:, b, :, :], neg_max[:, b, :, :], hi, ALU.subtract))
                    link(eng.tensor_copy(mid, max_res[:, b, :, :]))
                    eng.tensor_tensor(lo, max_res[:, b, :, :], mid, ALU.subtract).then_inc(a_mparts, 1)

                row_max(0, range(NROW))
                split_max(0)
                for G in range(NG):
                    if G < NG - 1:
                        row_max(G + 1, range(0, 3))
                    if G >= 1:
                        heads_out(n, G - 1, 6 + (G - 1) % 2, rden)
                    if G < NG - 1:
                        row_max(G + 1, range(3, NROW))
                        split_max(G + 1)
                heads_out(n, NG - 1, 6 + (NG - 1) % 2, rden)
                eng.wait_ge(a_y, n + 1)
                add_to_x(1)

            def moe(n):
                eng.wait_ge(m_logit, n + 1)
                link(eng.tensor_copy(lg[:, :, :], bank(6)[:, 0:NT * E].rearrange("p (t e) -> p t e", t=NT)))
                link(eng.tensor_reduce(top[:, :], lg[:, :, :], AX.X, ALU.max))
                eng.tensor_tensor(lgd[:, :, :], lg[:, :, :], top[:, :].unsqueeze(2).to_broadcast([P, NT, E]),
                                  ALU.subtract).then_inc(m_lgd, 1)
                mine = lg[:, :, :].unsqueeze(3).to_broadcast([P, NT, E, E])
                other = lg[:, :, :].unsqueeze(2).to_broadcast([P, NT, E, E])
                link(eng.tensor_tensor(eq[:, :, :, :], other, mine, ALU.is_equal))
                link(eng.tensor_tensor(eq[:, :, :, :], eq[:, :, :, :],
                                       before[:, :, :].unsqueeze(1).to_broadcast([P, NT, E, E]), ALU.mult))
                link(eng.tensor_tensor(gt[:, :, :, :], other, mine, ALU.is_gt))
                link(eng.tensor_tensor(gt[:, :, :, :], gt[:, :, :, :], eq[:, :, :, :], ALU.add))
                link(eng.tensor_reduce(rank[:, :, :], gt[:, :, :, :], AX.X, ALU.add))
                eng.wait_ge(m_ex, n + 1)
                link(eng.scalar_tensor_tensor(out=mix[:, :, :], in0=rank[:, :, :], scalar=2.0, in1=ex[:, :, :],
                                              op0=ALU.is_lt, op1=ALU.mult))
                link(eng.tensor_reduce(tot[:, :], mix[:, :, :], AX.X, ALU.add))
                link(eng.reciprocal(tot[:, :], tot[:, :]))
                eng.tensor_tensor(mix[:, :, :], mix[:, :, :], tot[:, :].unsqueeze(2).to_broadcast([P, NT, E]),
                                  ALU.mult).then_inc(m_mix, 1)

                def add(e):
                    eng.wait_ge(m_y, E * n + e + 1)
                    if e == 0:
                        eng.wait_ge(m_mix, n + 1)
                    else:
                        eng.wait_ge(m_acc, E * n + e)
                    for t in range(NT):
                        i = eng.scalar_tensor_tensor(out=x[:, t, :], in0=bank(4 + e % 2)[:, P * t:P * t + P],
                                                     scalar=mix[:, t, e:e + 1], in1=x[:, t, :],
                                                     op0=ALU.mult, op1=ALU.add)
                    i.then_inc(m_acc, 1)
                    if e == E - 1:
                        eng.wait_ge(m_acc, E * (n + 1))
                        eng.nop().then_inc(x_done, 1)

                for e in range(E):
                    for j, (_, w) in enumerate(FT):
                        i = NF * e + j
                        eng.wait_ge(m_u, E * NF * n + i + 1)
                        eng.wait_ge(m_silu, E * NF * n + i + 1)
                        if e >= 2:
                            eng.wait_ge(m_y, E * n + e - 1)
                        eng.tensor_tensor(hidden[0:w, e % 2, j, :], silu[0:w, i % 2, :], bank(2 + i % 2)[0:w, :],
                                          ALU.mult).then_inc(m_h, 1)
                    if e >= 1:
                        add(e - 1)
                add(E - 1)

            def lin():
                eng.wait_ge(l_be, 1)
                link(eng.tensor_scalar(l_beta[:, :, :], l_beta[:, :, :], 1.0, None, ALU.add))
                eng.reciprocal(l_beta[:, :, :], l_beta[:, :, :]).then_inc(l_bok, 1)
                for i in range(2 * NC2):
                    t, c = (i % 8) // 2, i % 2
                    eng.wait_ge(l_pn, i + 1)
                    eng.tensor_copy((l_k, l_v)[i // 8][:, t, 512 * c:512 * c + 512], bank(2 + i % 2))\
                       .then_inc(l_kv, 1)
                eng.wait_ge(l_ss, 2 * NC2)
                eng.tensor_copy(l_inv[:, :, :, :].rearrange("p a t h -> p (a t h)"),
                                bank(5)[:, 0:2 * NT * H]).then_inc(l_ssc, 1)
                eng.wait_ge(l_norm, 1)
                link(eng.tensor_scalar(l_inv[:, :, :, :], l_inv[:, :, :, :], 1e-12, None, ALU.max))
                link(eng.reciprocal(l_inv[:, :, :, :], l_inv[:, :, :, :]))
                link(eng.tensor_scalar(l_inv[:, 0, :, :], l_inv[:, 0, :, :], float(DM) ** -0.5, None, ALU.mult))
                eng.wait_ge(l_kv, 2 * NC2)

                def scale_values(c):
                    src = l_v[:, :, P * c:P * c + P].rearrange("p t (r d) -> p t r d", r=2)
                    dst = l_vk[:, :, P * c:P * c + P].rearrange("p t (r d) -> p t r d", r=2)
                    eng.tensor_tensor(dst, src,
                                      l_inv[:, 1, :, 2 * c:2 * c + 2].unsqueeze(3).to_broadcast([P, NT, 2, DM]),
                                      ALU.mult).then_inc(l_vks, 1)

                def mask_scores(c):
                    for r in range(2):
                        h = 2 * c + r
                        eng.wait_ge(l_sc, h + 1)
                        if c >= 1:
                            eng.wait_ge(l_o, c)
                        eng.tensor_tensor(l_wt[:, r, :, :], flat(r),
                                          keep_ge[:, :].unsqueeze(1).to_broadcast([P, NT, P]),
                                          ALU.mult).then_inc(l_wts, 1)

                def scale_out(c):
                    eng.wait_ge(l_o, c + 1)
                    if c >= 2:
                        eng.wait_ge(l_os, c - 1)
                    o = bank(4 + c % 2).rearrange("p (t r d) -> p t r d", t=NT, r=2)
                    dst = l_tmp[:, c % 2, :, :].rearrange("p t (r d) -> p t r d", r=2)
                    eng.tensor_tensor(dst, o,
                                      l_inv[:, 0, :, 2 * c:2 * c + 2].unsqueeze(3).to_broadcast([P, NT, 2, DM]),
                                      ALU.mult).then_inc(l_ts, 1)

                scale_values(0)
                scale_values(1)
                for c in range(NC2):
                    mask_scores(c)
                    if c + 2 < NC2:
                        scale_values(c + 2)
                    if c >= 1:
                        scale_out(c - 1)
                scale_out(NC2 - 1)
                eng.wait_ge(l_y, 1)
                add_to_x(0)

            def adapter(n):
                eng.wait_ge(xnT_ok, (6, 8)[n])
                link(eng.tensor_reduce(pooled[:, 0:1], xnT[:, :], AX.X, ALU.add))
                eng.tensor_scalar(pool_rep[:, :], ones[:, :], pooled[:, 0:1], 1.0 / T, ALU.mult,
                                  ALU.mult).then_inc(d_pool, 1)
                eng.wait_ge(d_gate_ok, n + 1)
                link(eng.tensor_copy(d_lg[:, :], bank(6)[:, 0:E]))
                eng.tensor_reduce(d_negm[:, 0:1], d_lg[:, :], AX.X, ALU.max, negate=True).then_inc(d_lgs, 1)
                eng.wait_ge(d_exs, n + 1)
                link(eng.reciprocal(d_z[:, 0:1], d_z[:, 0:1]))
                link(eng.tensor_scalar(d_p[:, :], d_ex[:, :], d_z[:, 0:1], None, ALU.mult))
                mine = d_p[:, :].unsqueeze(2).to_broadcast([P, E, E])
                other = d_p[:, :].unsqueeze(1).to_broadcast([P, E, E])
                link(eng.tensor_tensor(d_eq[:, :, :], other, mine, ALU.is_equal))
                link(eng.tensor_tensor(d_eq[:, :, :], d_eq[:, :, :], before[:, :, :], ALU.mult))
                link(eng.tensor_tensor(d_gt[:, :, :], other, mine, ALU.is_gt))
                link(eng.tensor_tensor(d_gt[:, :, :], d_gt[:, :, :], d_eq[:, :, :], ALU.add))
                link(eng.tensor_reduce(d_rank[:, :], d_gt[:, :, :], AX.X, ALU.add))
                link(eng.scalar_tensor_tensor(out=d_w[:, :], in0=d_rank[:, :], scalar=2.0, in1=d_p[:, :],
                                              op0=ALU.is_lt, op1=ALU.mult))
                link(eng.tensor_reduce(d_s[:, 0:1], d_w[:, :], AX.X, ALU.add))
                link(eng.tensor_scalar(d_s[:, 0:1], d_s[:, 0:1], 1e-8, None, ALU.add))
                link(eng.reciprocal(d_s[:, 0:1], d_s[:, 0:1]))
                eng.tensor_scalar(d_w[:, :], d_w[:, :], d_s[:, 0:1], None, ALU.mult).then_inc(d_ws, 1)
                eng.wait_ge(d_ws, n + 1)
                link(eng.tensor_scalar(d_w4[:, :], d_w[:, 0:E:2], pair_of[:, 0:1], None, ALU.mult))
                link(eng.scalar_tensor_tensor(out=d_w4[:, :], in0=d_w[:, 1:E:2], scalar=pair_of[:, 1:2],
                                              in1=d_w4[:, :], op0=ALU.mult, op1=ALU.add))
                for k in range(KD):
                    i = eng.tensor_scalar(d_up[:, k, :], upT[:, k, :], d_w4[:, k:k + 1], None, ALU.mult)
                i.then_inc(d_ups, 1)
                eng.wait_ge(d_y, n + 1)
                add_to_x(4)

            def rel():
                parts_of_qk(2, float(HD) ** -0.5)

                def mask_q(c):
                    if c == 0:
                        eng.wait_ge(r_shift, 1)
                        eng.wait_ge(a_spread, 3 * H)
                    if c >= 2:
                        eng.wait_ge(r_rel_ok, 2 * (IC // 8) * (c - 1))
                    src = q_shift[:, 0:T].rearrange("p (t i) -> p i t", t=NT)[:, IC * c:IC * c + IC, :]
                    eng.tensor_tensor(q_masked[:, c % 2, :, :].rearrange("p i (t h) -> p i t h", t=NT),
                                      src.unsqueeze(3).to_broadcast([P, IC, NT, H]),
                                      head_of[:, :].unsqueeze(1).unsqueeze(1).to_broadcast([P, IC, NT, H]),
                                      ALU.mult).then_inc(r_qm, 1)

                mask_q(0)
                mask_q(1)
                for i in range(P // 8):
                    eng.wait_ge(r_rel_ok, 2 * i + 1)
                    v = bank((2 * i) % 4).rearrange("p (i t h) -> p h t i", i=8, t=NT)
                    q8 = slice(8 * i, 8 * i + 8)
                    eng.tensor_copy(sc[:, :, 0:9:4, q8], v[:, :, 0:3, :])
                    eng.tensor_copy(sc[:, :, 7, q8], v[:, :, 3, :])
                    eng.tensor_copy(sc[:, :, 2:7:4, q8], v[:, :, 2:4, :]).then_inc(r_even, 1)
                    if i % 4 == 3 and i // 4 + 2 < P // IC:
                        mask_q(i // 4 + 2)
                eng.wait_ge(r_odd, P // 8)
                eng.wait_ge(r_even, P // 8)
                eng.wait_ge(r_diag, 4 * (P // IC))

                def add(h):
                    for j in range(3):
                        k = 3 * h + j
                        eng.wait_ge(r_main, k + 1)
                        b = JOB_AT[j] // P
                        v = sc[:, h, b:b + JOB_N[j] // P, :].rearrange("p b i -> p (b i)")
                        eng.tensor_tensor(v, v, bank(k % 2)[:, 0:JOB_N[j]], ALU.add).then_inc(r_sum, 1)

                def row_max(h):
                    for i, (t, bk, col) in enumerate(ROW_JOBS):
                        eng.wait_ge(r_sT, 3 * h + (1, 2, 2, 3)[i])
                        eng.tensor_reduce(r_neg_max[:, h % 2, t:t + 1], bank(bk)[:, col:col + (t + 1) * P], AX.X,
                                          ALU.max, negate=True).then_inc(r_max, 1)

                def column(h):
                    eng.wait_ge(r_pT, 3 * h + 3)
                    if h >= 2:
                        eng.wait_ge(a_pv, 2 * H + h - 1)
                    eng.tensor_copy(r_probT[:, h % 2, JOB_AT[2]:JOB_AT[2] + JOB_N[2]],
                                    bank(5 + (3 * h + 2) % 2)[:, 0:JOB_N[2]]).then_inc(r_pTv, 1)

                for i in range(H + 3):
                    if i < H:
                        add(i)
                    if 1 <= i <= H:
                        row_max(i - 1)
                    if 2 <= i <= H + 1:
                        column(i - 2)
                    if i >= 4 and (i - 4) % G4 == G4 - 1:
                        heads_out(2, (i - 4) // G4, 7, r_rden)
                heads_out(2, NG - 1, 7, r_rden)
                eng.wait_ge(a_y, 3)
                add_to_x(1)

            for n in range((NSTAGE + 3) // 4):
                eng.wait_ge(stage_T, n + 1)
            b4 = [bank(n).rearrange("p (j d) -> p j d", d=P) for n in range(8)]
            eng.tensor_copy(w_b[:, :, :], b4[0]).then_inc(weights, 1)
            eng.tensor_copy(w_r[:, :, :], b4[1]).then_inc(weights, 1)
            eng.tensor_copy(relT[:, 0:2 * P], bank(2)[:, 0:2 * P])
            eng.tensor_copy(relT[:, 2 * P:3 * P], bank(2)[:, 0:P])
            eng.tensor_copy(downT[:, 0:2, :], b4[2][:, 2:4, :]).then_inc(weights, 1)
            eng.tensor_copy(downT[:, 2:4, :], b4[3][:, 0:2, :])
            eng.tensor_copy(upT[:, 0:2, :], b4[3][:, 2:4, :]).then_inc(weights, 1)
            eng.tensor_copy(upT[:, 2:4, :], b4[4][:, 0:2, :]).then_inc(weights, 1)
            eng.wait_ge(stage_T, (NSTAGE + 3) // 4 + 1)
            eng.tensor_copy(gateT[:, :], bank(6)[:, 0:E]).then_inc(weights, 1)
            eng.wait_ge(const, CONSTS)
            with eng.Fori(0, B) as b:
                steps[0] = 0
                norm(0)
                attn(0, float(HD) ** -0.5)
                norm(1)
                moe(0)
                norm(2)
                attn(1, float(P) ** -0.5)
                norm(3)
                moe(1)
                norm(4)
                lin()
                norm(5)
                adapter(0)
                norm(6)
                rel()
                norm(7)
                adapter(1)
                eng.nop().then_inc(ended, 1)
                eng.wait_ge(started, b + 1)


_INS = ['L0_attn_a_x', 'L0_attn_a_Wq', 'L0_attn_a_Wk', 'L0_attn_a_Wv', 'L0_attn_a_Wo', 'L0_attn_b_W_attn',
        'L0_attn_b_W_out', 'L0_ffn_Ws', 'L0_ffn_bs', 'L0_ffn_Wg', 'L0_ffn_Wu', 'L0_ffn_Wd', 'L1_attn_a_Wk',
        'L1_attn_a_Wv', 'L1_attn_a_Wq', 'L1_attn_a_Wbeta', 'L1_attn_a_Wout', 'L1_attn_b_Wq', 'L1_attn_b_Wk',
        'L1_attn_b_Wv', 'L1_attn_b_Wp', 'L1_attn_b_bp', 'L1_attn_b_rel_embed', 'L1_ffn_gate_w',
        'L1_ffn_down_w', 'L1_ffn_down_b', 'L1_ffn_up_w', 'L1_ffn_up_b']


def kernel(**inputs):
    import numpy as _np
    import concourse.bacc as _bacc
    from concourse import mybir as _mybir
    from concourse.bass_utils import run_bass_kernel_spmd as _run

    nc = _bacc.Bacc("TRN2", target_bir_lowering=False, num_devices=1)
    arrays, args = {}, []
    for name in _INS:
        a = _np.ascontiguousarray(inputs[name])
        arrays[f"in_{name}_dram"] = a
        args.append(nc.dram_tensor(f"in_{name}_dram", a.shape, _mybir.dt.from_np(a.dtype), kind="ExternalInput").ap())
    shape = arrays["in_L0_attn_a_x_dram"].shape
    args.append(nc.dram_tensor("out_0_dram", shape, _mybir.dt.float32, kind="ExternalOutput").ap())
    build(nc, *args)
    r = _run(nc, [arrays], core_ids=[0])
    return r.results[0]["out_0_dram"]
```

```python
from contextlib import ExitStack

import concourse.bass as bass
from concourse import mybir

F32 = mybir.dt.float32
BF16 = mybir.dt.bfloat16
ACT = mybir.ActivationFunctionType
ALU = mybir.AluOpType
AX = mybir.AxisListType

P = 128
T = 512
NT = T // P
H = 16
HD = P // H
DM = 64
NC2 = H * DM // P
E = 8
EPS = 1e-5
MASKED = -1e30

Q_PART = [0, 1, 2, 0, 1, 0]
K_PART = [0, 0, 0, 1, 1, 2]
SLOTS = len(Q_PART)
KROWS = SLOTS * HD

G4 = 4
NG = H // G4

BLOCKS = [(0, 0), (0, 1), (0, 2), (0, 3), (1, 1), (1, 2), (1, 3), (3, 3), (2, 2), (2, 3)]
SLOT = {b: n for n, b in enumerate(BLOCKS)}
COLS = len(BLOCKS) * P
JOBS = [[0], [1, 3], [2]]
JOB_AT = [0, 512, 1024]
JOB_N = [512, 512, 256]

LAYERS = ["attn_a", "moe_1", "attn_b", "moe_2", "lin_attn", "adapter_1", "rel_attn", "adapter_2"]


def build(nc, a_x, a_wq, a_wk, a_wv, a_wo, b_wattn, b_wout, m_ws, m_bs, m_wg, m_wu, m_wd,
          l_wk, l_wv, l_wq, l_wbeta, l_wout, r_wq, r_wk, r_wv, r_wp, r_bp, r_rel,
          d_gate, d_dw, d_db, d_uw, d_ub, out):
    B = a_x.shape[0]
    F = m_wg.shape[2]
    FT = [(j * P, min(P, F - j * P)) for j in range((F + P - 1) // P)]
    NF = len(FT)
    BN = d_dw.shape[1]
    KD = E * BN // P
    assert (a_x.shape[1], a_x.shape[2]) == (T, P) and r_rel.shape[0] == 2 * P and 2 * BN == P

    with ExitStack() as ctx:
        def sb(name, shape, dt=F32):
            return ctx.enter_context(nc.sbuf_tensor(name, shape, dt))

        def sem(name):
            return ctx.enter_context(nc.semaphore(name))

        ident = sb("ident", [P, P])
        identb = sb("identb", [P, P], BF16)
        mask_qk = sb("mask_qk", [P, P], BF16)
        mask_kq = sb("mask_kq", [P, P], BF16)
        keep_ge = sb("keep_ge", [P, P])
        ones = sb("ones", [P, P])
        half = sb("half", [P, 1])
        spread_q = sb("spread_q", [P, 3, H // 2, 2, 8, HD], BF16)
        spread_k = sb("spread_k", [P, 3, H // 2, 2, 8, HD], BF16)
        pick_max = sb("pick_max", [P, G4, P], BF16)
        head_of = sb("head_of", [P, H])
        pair_of = sb("pair_of", [P, 2])
        before = sb("before", [P, E, E])
        w_a = sb("w_a", [P, 4, P])
        w_b = sb("w_b", [P, 4, P])
        w_r = sb("w_r", [P, 4, P])
        relT = sb("relT", [P, 2, 3 * P], BF16)
        rel_res = sb("rel_res", [P, 2 * P])
        bp_row = sb("bp_row", [1, P])
        ws = sb("ws", [P, E])
        bs_row = sb("bs_row", [1, E])
        wg = sb("wg", [P, E, F])
        wu = sb("wu", [P, E, F])
        wd = sb("wd", [P, E, NF, P])
        wk_l = sb("wk_l", [P, H * DM])
        wv_l = sb("wv_l", [P, H * DM])
        wq_l = sb("wq_l", [P, H * DM])
        wbeta = sb("wbeta", [P, H])
        wout_l = sb("wout_l", [P, NC2, P])
        gateT = sb("gateT", [P, E])
        downT = sb("downT", [P, KD, P])
        upT = sb("upT", [P, KD, P])
        down_b = sb("down_b", [P, KD])
        up_b = sb("up_b", [E, P])
        x = sb("x", [P, NT, P])
        stats = sb("stats", [P, NT, 6])
        moments = sb("moments", [P, NT, 2])
        rstd = sb("rstd", [P, NT])
        xn = sb("xn", [P, NT, P])
        xnT = sb("xnT", [P, T])
        values = sb("values", [P, NT, H, HD + 1])
        neg_maxT = sb("neg_maxT", [P, 2, T], BF16)
        WORK = 29900
        work = sb("work", [P, WORK])

        def part(at, shape, dt=F32):
            n = 1
            for d in shape:
                n *= d
            words = n if dt == F32 else (n + 1) // 2
            assert at + words <= WORK, (at + words, WORK)
            ap = work[:, at:at + words]
            if dt != F32:
                ap = ap.bitcast(dt)
            if len(shape) > 1:
                names = "abcd"[:len(shape)]
                ap = ap.rearrange("p (" + " ".join(names) + ") -> p " + " ".join(names),
                                  **dict(zip(names[1:], shape[1:])))
            return ap, at + words

        NSTAGE = 3 + 1 + 4 + 2 + KD + KD
        stage, at = part(0, [NSTAGE, P])
        stage_gate, at = part(at, [P])
        q_st, at = part(0, [H // 2, T], BF16)
        k_st, at = part(at, [H // 2, T], BF16)
        ring_at = at
        res, at = part(ring_at, [2, T])
        k_parts, at = part(at, [3, T], BF16)
        q_parts, at = part(ring_at + 3072, [3, T + 2], BF16)
        qk_part = lambda w, n: (q_parts[:, n, 1:T + 1], k_parts[:, n, :])[w]
        prob, at = part(at, [2, COLS])
        neg_max, at = part(at, [2, NT, G4])
        max_res, at = part(at, [2, NT, G4])
        max_part, at = part(at, [2, NT, 4 * G4], BF16)
        rden, at = part(at, [2, NT, G4])
        IC = 16
        q_masked0, _ = part(ring_at, [2, IC, NT * H], BF16)
        q_masked1, at = part(ring_at + 2 * T + 3 * T // 2, [2, IC, NT * H], BF16)
        q_masked = (q_masked0, q_masked1)
        assert at <= ring_at + 3072
        r_prob, _ = part(ring_at, [2, COLS])
        r_probT, at2 = part(ring_at + 2 * COLS, [2, COLS])
        sc, at = part(at2, [H, len(BLOCKS), P])
        r_neg_max, at = part(at, [2, NT])
        r_rden, at = part(at, [2, NT, G4])
        silu, at = part(0, [2, T])
        hidden, at = part(at, [2, NF, T])
        lg, at = part(at, [NT, E])
        gt, at = part(at, [NT, E, E])
        eq, at = part(at, [NT, E, E])
        rank, at = part(at, [NT, E])
        top, at = part(at, [NT])
        lgd, at = part(at, [NT, E])
        ex, at = part(at, [NT, E])
        mix, at = part(at, [NT, E])
        tot, at = part(at, [NT])
        l_qT, at = part(0, [NC2, T])
        l_kT, at = part(at, [NC2, T])
        l_k, at = part(at, [NT, H * DM])
        l_v, at = part(at, [NT, H * DM])
        l_vk, at = part(at, [NT, H * DM])
        l_sq, at = part(at, [2, T])
        l_sqk, at = part(at, [2, 512])
        l_wt, at = part(at, [2, 2, NT, P])
        l_st, at = part(at, [2, NT - 1, P])
        l_tmp, at = part(at, [2, NT, P])
        l_beta, at = part(at, [NT, H])
        l_ssum, at = part(at, [2, NT, H])
        l_rec, at = part(at, [2, NT, H])
        l_inv, at = part(at, [2, NT, H])
        pooled, at = part(0, [1])
        pool_rep, at = part(at, [P])
        d_hid, at = part(at, [KD, T])
        d_up, at = part(at, [KD, P])
        d_lg, at = part(at, [E])
        d_negm, at = part(at, [1])
        d_ex, at = part(at, [E])
        d_z, at = part(at, [1])
        d_p, at = part(at, [E])
        d_gt, at = part(at, [E, E])
        d_eq, at = part(at, [E, E])
        d_rank, at = part(at, [E])
        d_w, at = part(at, [E])
        d_s, at = part(at, [1])
        d_w4, at = part(at, [KD])
        d_wT, at = part(at, [P])

        psum = ctx.enter_context(nc.psum_tensor("banks", [P, 8, 512], F32))

        def bank(n):
            return psum[:, n, :]

        loaded = sem("loaded")
        const = sem("constants")
        zeroed = sem("zeroed")
        stage_T = sem("stage_transposed")
        set_up = sem("vector_set_up")
        weights = sem("weights_ready")
        started = sem("turn_started")
        x_in = sem("x_loaded")
        step = sem("vector_step")
        x_done = sem("layer_done")
        normed = sem("norm_stats")
        rstd_ok = sem("norm_rstd")
        pool_step = sem("pool_step")
        xn_ok = sem("norm_rows")
        xn_T = sem("norm_transposed")
        xnT_ok = sem("norm_columns")
        a_proj = sem("attn_projected")
        a_hi = sem("attn_part_hi")
        a_res = sem("attn_part_rest")
        a_mid = sem("attn_part_mid")
        a_lo = sem("attn_part_lo")
        a_v = sem("attn_values")
        a_spread = sem("attn_spread")
        a_qst = sem("attn_q_stacked")
        a_kst = sem("attn_k_stacked")
        a_s1 = sem("attn_scores_rows")
        a_max = sem("attn_row_max")
        a_mparts = sem("attn_max_parts")
        a_maxT = sem("attn_max_transposed")
        a_mrow = sem("attn_max_rows")
        a_s2 = sem("attn_scores_columns")
        a_prob = sem("attn_probabilities")
        a_pv = sem("attn_weighted_values")
        a_cols = sem("attn_group_columns")
        a_rows = sem("attn_group_rows")
        a_o = sem("attn_heads_out")
        a_oT = sem("attn_out_transposed")
        a_oTs = sem("attn_out_columns")
        a_y = sem("attn_out_projected")
        r_shift = sem("rel_q_shifted")
        r_qm = sem("rel_q_masked_vec")
        r_qmp = sem("rel_q_masked_pool")
        r_rel_ok = sem("rel_products")
        r_even = sem("rel_even_blocks")
        r_late = sem("rel_even_blocks_act")
        r_odd = sem("rel_odd_blocks")
        r_diag = sem("rel_diagonals")
        r_main = sem("rel_scores_qk")
        r_sum = sem("rel_scores_summed")
        r_sT = sem("rel_scores_transposed")
        r_max = sem("rel_row_max")
        r_p = sem("rel_probabilities")
        r_pT = sem("rel_prob_transposed")
        r_pTa = sem("rel_prob_columns_act")
        r_pTv = sem("rel_prob_columns_vec")
        m_logit = sem("moe_logits")
        m_lgd = sem("moe_logits_shifted")
        m_ex = sem("moe_exp")
        m_mix = sem("moe_mixed")
        m_g = sem("moe_gate_products")
        m_u = sem("moe_up_products")
        m_silu = sem("moe_silu")
        m_h = sem("moe_hidden")
        m_y = sem("moe_down_products")
        m_acc = sem("moe_added")
        l_bz = sem("lin_beta_logits")
        l_be = sem("lin_beta_exp")
        l_bok = sem("lin_beta")
        l_pq = sem("lin_qk_products")
        l_pn = sem("lin_kv_products")
        l_qk = sem("lin_qk_columns")
        l_kv = sem("lin_kv_rows")
        l_sqr = sem("lin_squares")
        l_ss = sem("lin_square_sums")
        l_sqks = sem("lin_key_squares")
        l_ssk = sem("lin_key_square_sums")
        l_ssc = sem("lin_square_sums_copied")
        l_norm = sem("lin_norms")
        l_invs = sem("lin_inverse_norms")
        l_vks = sem("lin_scaled_values")
        l_bv = sem("lin_beta_values")
        l_sc = sem("lin_scores")
        l_wts = sem("lin_masked_scores")
        l_zero = sem("lin_states_zeroed")
        l_stp = sem("lin_state_products")
        l_sts = sem("lin_states")
        l_o = sem("lin_out_products")
        l_ts = sem("lin_out_scaled")
        l_os = sem("lin_out_rows")
        l_oT = sem("lin_out_transposed")
        l_oTs = sem("lin_out_columns")
        l_y = sem("lin_out_projected")
        d_pool = sem("ad_pooled")
        d_gate_ok = sem("ad_gate_logits")
        d_lgs = sem("ad_logits_ready")
        d_exs = sem("ad_exp")
        d_dn = sem("ad_down_products")
        d_hs = sem("ad_hidden")
        d_ws = sem("ad_mix")
        d_ups = sem("ad_up_scaled")
        d_wTp = sem("ad_mix_transposed")
        d_wTs = sem("ad_mix_column")
        d_y = sem("ad_up_products")
        ended = sem("turn_ended")
        x_out = sem("x_stored")
        turn_sems = range(x_in.num, x_out.num + 1)

        x_rows = a_x.rearrange("b (t p) d -> b p t d", p=P)
        out_rows = out.rearrange("b (t p) d -> b p t d", p=P)

        CONSTS = 6 + 2 * SLOTS + 3 + 4
        ROW_JOBS = [(3, 2, 0), (2, 3, 0), (0, 3, 3 * P), (1, 4, 0)]

        block = ctx.enter_context(nc.Block())

        loads = [
            (ws[:, :], m_ws), (bs_row[:, :], m_bs.rearrange("(a n) -> a n", a=1)),
            (w_a[:, 0, :], a_wq), (w_a[:, 1, :], a_wk), (w_a[:, 2, :], a_wv), (w_a[:, 3, :], a_wo),
            (stage[:, 0:3, :], b_wattn.rearrange("(j p) d -> p j d", p=P)),
            (stage[:, 3, :], b_wout), (stage[:, 4, :], r_wq), (stage[:, 5, :], r_wk),
            (stage[:, 6, :], r_wv), (stage[:, 7, :], r_wp),
            (stage[:, 8:10, :], r_rel.rearrange("(j p) d -> p j d", p=P)),
            (stage[:, 10:10 + KD, :], d_dw.rearrange("e c d -> (e c) d").rearrange("(j p) d -> p j d", p=P)),
            (stage[:, 10 + KD:10 + 2 * KD, :].rearrange("p j (e c) -> p (j e) c", e=2),
             d_uw.rearrange("e d c -> d e c")),
            (stage_gate[0:E, :], d_gate),
            (bp_row[:, :], r_bp.rearrange("(a n) -> a n", a=1)),
            (up_b[:, :], d_ub), (down_b[:, :], d_db.rearrange("e c -> (e c)").rearrange("(k p) -> p k", p=P)),
            (wg[:, :, :], m_wg.rearrange("e d f -> d e f")), (wu[:, :, :], m_wu.rearrange("e d f -> d e f")),
            (wk_l[:, :], l_wk), (wv_l[:, :], l_wv), (wq_l[:, :], l_wq), (wbeta[:, :], l_wbeta),
            (wout_l[:, :, :], l_wout.rearrange("(c p) d -> p c d", p=P)),
        ] + [(wd[0:n, :, j, :], m_wd[:, f0:f0 + n, :].rearrange("e f d -> f e d")) for j, (f0, n) in enumerate(FT)]
        LOADED = 16 * len(loads)

        @block.sync
        def _(sp):
            with nc.allow_non_contiguous_dma(reason="biases by partition"):
                for dst, src in loads:
                    sp.dma_start(dst, src).then_inc(loaded, 16)
            with sp.Fori(0, B) as b:
                sp.dma_start(x[:, :, :], x_rows[b]).then_inc(x_in, 16)
                sp.wait_ge(x_done, 8)
                sp.dma_start(out_rows[b], x[:, :, :]).then_inc(x_out, 16)
                sp.wait_ge(ended, 4)
                sp.wait_ge(x_out, 16)
                sp.sem_clear(turn_sems)
                sp.nop().then_inc(started, 1)

        def pool_norm(eng, n):
            eng.wait_ge(normed, 8 * n + 8)
            eng.tensor_scalar(rstd[:, :], moments[:, :, 1], EPS, None, ALU.add).then_inc(pool_step, 1)
            eng.wait_ge(pool_step, n + 1)
            eng.tensor_tensor(rstd[:, :], rstd[:, :], half[:, 0:1].to_broadcast([P, NT]),
                              ALU.pow).then_inc(rstd_ok, 1)

        def pool_split(eng, n):
            for w in range(2):
                eng.wait_ge(a_res, 2 * n + w + 1)
                eng.tensor_copy(qk_part(w, 1), res[:, w, :]).then_inc(a_mid, 1)

        def mask_q(eng, c, n):
            src = q_parts[:, n, 0:T].rearrange("p (t i) -> p i t", t=NT)[:, IC * c:IC * c + IC, :]
            return eng.tensor_tensor(q_masked[c % 2][:, n, :, :].rearrange("p i (t h) -> p i t h", t=NT),
                                     src.unsqueeze(3).to_broadcast([P, IC, NT, H]),
                                     head_of[:, :].unsqueeze(1).unsqueeze(1).to_broadcast([P, IC, NT, H]),
                                     ALU.mult)

        def pool_rel(eng):
            def mask(c):
                if c % 2 == 0:
                    return
                if c == 1:
                    eng.wait_ge(r_shift, 1)
                    eng.wait_ge(a_lo, 6)
                else:
                    eng.wait_ge(r_rel_ok, 2 * (IC // 8) * (c - 1))
                mask_q(eng, c, 1).then_inc(r_qmp, 1)

            mask(1)
            for c in range(P // IC):
                if c + 2 < P // IC:
                    mask(c + 2)
                eng.wait_ge(r_even, IC // 8 * (c + 1))
                for b in (0, 4, 7, 8):
                    v = sc[:, :, b, IC * c:IC * c + IC]
                    eng.affine_select(out=v, in_=v, compare_op=ALU.is_gt, fill=0.0, base=IC * c,
                                      pattern=[[0, H], [1, IC]],
                                      channel_multiplier=-1).then_inc(r_diag, 1)

        def pool_lin(eng):
            eng.wait_ge(xnT_ok, 5)
            eng.memset(l_st[:, :, :, :], 0.0).then_inc(l_zero, 1)
            for i in range(NC2):
                t, c = i // 2, i % 2
                eng.wait_ge(l_kv, i + 1)
                if i >= 2:
                    eng.wait_ge(l_ssk, i - 1)
                k = l_k[:, t, 512 * c:512 * c + 512]
                eng.tensor_tensor(l_sqk[:, i % 2, :], k, k, ALU.mult).then_inc(l_sqks, 1)
            eng.wait_ge(l_bok, 1)
            for c in range(NC2 + 2):
                if c < NC2:
                    eng.wait_ge(l_vks, c + 1)
                    v = l_v[:, :, P * c:P * c + P].rearrange("p t (r d) -> p t r d", r=2)
                    eng.tensor_tensor(v, v, l_beta[:, :, 2 * c:2 * c + 2].unsqueeze(3)
                                      .to_broadcast([P, NT, 2, DM]), ALU.mult).then_inc(l_bv, 1)
                if c >= 2:
                    eng.wait_ge(l_ts, c - 1)
                    eng.wait_ge(l_bv, c - 1)
                    v = l_v[:, :, P * (c - 2):P * (c - 1)]
                    eng.tensor_tensor(v, v, l_tmp[:, c % 2, :, :], ALU.add).then_inc(l_os, 1)

        @block.gpsimd
        def _(eng):
            zeros = [ident, identb, mask_qk, mask_kq, spread_q, spread_k, pick_max, neg_maxT]
            for z in zeros:
                eng.memset(z[...], 0.0).then_inc(zeroed, 1)
            for o in (keep_ge, head_of, pair_of, before, ones):
                eng.memset(o[...], 1.0).then_inc(zeroed, 1)
            eng.memset(half[:, :], -0.5).then_inc(zeroed, 1)
            eng.memset(values[:, :, :, HD:HD + 1], 1.0).then_inc(zeroed, 1)
            eng.wait_ge(zeroed, len(zeros) + 7)
            for m in (ident, identb):
                eng.affine_select(out=m[:, :], in_=m[:, :], compare_op=ALU.not_equal, fill=1.0, base=0,
                                  pattern=[[-1, P]], channel_multiplier=1).then_inc(const, 1)
            eng.affine_select(out=mask_qk[:, :], in_=mask_qk[:, :], compare_op=ALU.is_ge, fill=MASKED, base=0,
                              pattern=[[-1, P]], channel_multiplier=1).then_inc(const, 1)
            eng.affine_select(out=mask_kq[:, :], in_=mask_kq[:, :], compare_op=ALU.is_ge, fill=MASKED, base=0,
                              pattern=[[1, P]], channel_multiplier=-1).then_inc(const, 1)
            eng.affine_select(out=keep_ge[:, :], in_=keep_ge[:, :], compare_op=ALU.is_ge, fill=0.0, base=0,
                              pattern=[[-1, P]], channel_multiplier=1).then_inc(const, 1)
            eng.affine_select(out=before[:, :, :], in_=before[:, :, :], compare_op=ALU.is_gt, fill=0.0, base=0,
                              pattern=[[1, E], [-1, E]], channel_multiplier=0).then_inc(const, 1)
            n_const = 6
            for spread, of_slot in ((spread_q, Q_PART), (spread_k, K_PART)):
                for slot, x_part in enumerate(of_slot):
                    v = spread[:, x_part, :, :, slot, :]
                    eng.affine_select(out=v, in_=v, compare_op=ALU.not_equal, fill=1.0, base=0,
                                      pattern=[[-16, H // 2], [-8, 2], [-1, HD]],
                                      channel_multiplier=1).then_inc(const, 1)
                    n_const += 1
            for p3 in range(3):
                eng.wait_ge(const, n_const)
                eng.affine_select(out=pick_max[:, :, :], in_=pick_max[:, :, :], compare_op=ALU.not_equal,
                                  fill=1.0, base=-G4 * p3, pattern=[[-1, G4], [0, P]],
                                  channel_multiplier=1).then_inc(const, 1)
                n_const += 1
            for tab, n, width in ((head_of, H, HD), (pair_of, 2, DM)):
                eng.affine_select(out=tab[:, :], in_=tab[:, :], compare_op=ALU.is_ge, fill=0.0, base=0,
                                  pattern=[[-width, n]], channel_multiplier=1).then_inc(const, 1)
                n_const += 1
                eng.wait_ge(const, n_const)
                eng.affine_select(out=tab[:, :], in_=tab[:, :], compare_op=ALU.is_gt, fill=0.0, base=width,
                                  pattern=[[width, n]], channel_multiplier=-1).then_inc(const, 1)
                n_const += 1
            assert n_const == CONSTS
            with eng.Fori(0, B) as b:
                pool_norm(eng, 0)
                pool_split(eng, 0)
                pool_norm(eng, 1)
                pool_norm(eng, 2)
                pool_split(eng, 1)
                pool_norm(eng, 3)
                pool_norm(eng, 4)
                pool_lin(eng)
                pool_norm(eng, 5)
                pool_norm(eng, 6)
                pool_split(eng, 2)
                pool_rel(eng)
                pool_norm(eng, 7)
                eng.nop().then_inc(ended, 1)
                eng.wait_ge(started, b + 1)

        def spread_bank(n, i):
            return (4 if n == 2 else 3) + i % 4

        def act_norm(eng, n):
            eng.wait_ge(xn_T, n + 1)
            eng.activation(xnT[:, :], bank(7), ACT.Copy).then_inc(xnT_ok, 1)

        def act_hi(eng, n, scale):
            eng.wait_ge(a_proj, 3 * n + 1)
            eng.activation(qk_part(0, 0), bank(0), ACT.Copy, scale=scale).then_inc(a_hi, 1)
            eng.wait_ge(a_proj, 3 * n + 2)
            eng.activation(qk_part(1, 0), bank(1), ACT.Copy).then_inc(a_hi, 1)

        def act_stack(eng, n, g):
            eng.wait_ge(a_spread, H * n + 2 * g + 1)
            eng.activation(q_st[:, g, :], bank(spread_bank(n, 2 * g)), ACT.Copy).then_inc(a_qst, 1)

        def group_columns(eng, n, G, bk):
            eng.wait_ge(a_pv, H * n + G4 * (G + 1))
            if G >= 1:
                eng.wait_ge(a_rows, NG * n + G)
            eng.activation(xnT[:, :], bank(bk), ACT.Copy).then_inc(a_cols, 1)

        def act_attn(eng, n, scale):
            act_hi(eng, n, scale)
            for g in range(H // 2):
                act_stack(eng, n, g)

            def max_rows(G):
                eng.wait_ge(a_maxT, NG * n + G + 1)
                if G >= 2:
                    eng.wait_ge(a_s2, 3 * (H * n + G4 * (G - 1)))
                eng.activation(neg_maxT[0:3 * G4, G % 2, :], bank(6 + G % 2)[0:3 * G4, 0:T // 2].bitcast(BF16),
                               ACT.Copy).then_inc(a_mrow, 1)

            max_rows(0)
            for h in range(H):
                if h >= 2:
                    eng.wait_ge(a_pv, H * n + h - 1)
                for j in range(3):
                    eng.wait_ge(a_s2, 3 * (H * n + h) + j + 1)
                    eng.activation(prob[:, h % 2, JOB_AT[j]:JOB_AT[j] + JOB_N[j]],
                                   bank(3 + j)[:, 0:JOB_N[j]], ACT.Exp).then_inc(a_prob, 1)
                if h % G4 == 0 and h > 0:
                    group_columns(eng, n, h // G4 - 1, 6 + (h // G4 - 1) % 2)
                if h % G4 == G4 - 1 and h < H - 1:
                    max_rows(h // G4 + 1)
            group_columns(eng, n, NG - 1, 6 + (NG - 1) % 2)
            eng.wait_ge(a_oT, n + 1)
            eng.activation(xnT[:, :], bank(0), ACT.Copy).then_inc(a_oTs, 1)

        def act_moe(eng, n):
            eng.wait_ge(m_lgd, n + 1)
            eng.activation(ex[:, :, :], lgd[:, :, :], ACT.Exp).then_inc(m_ex, 1)
            for i in range(E * NF):
                w = FT[i % NF][1]
                eng.wait_ge(m_g, E * NF * n + i + 1)
                if i >= 2:
                    eng.wait_ge(m_h, E * NF * n + i - 1)
                eng.activation(silu[0:w, i % 2, :], bank(i % 2)[0:w, :], ACT.Silu).then_inc(m_silu, 1)

        def act_lin(eng):
            eng.wait_ge(l_bz, 1)
            eng.activation(l_beta[:, :, :], bank(6)[:, 0:NT * H].rearrange("p (t h) -> p t h", t=NT),
                           ACT.Exp, scale=-1.0).then_inc(l_be, 1)
            for i in range(2 * NC2):
                dst = (l_qT, l_kT)[i % 2][:, i // 2, :]
                eng.wait_ge(l_pq, i + 1)
                eng.activation(dst, bank(i % 2), ACT.Copy).then_inc(l_qk, 1)
                if i % 2 == 0:
                    eng.wait_ge(l_qk, i + 1)
                    if i >= 4:
                        eng.wait_ge(l_ss, i // 2 - 1)
                    eng.activation(l_sq[:, i // 2 % 2, :], dst, ACT.Square).then_inc(l_sqr, 1)
            eng.wait_ge(l_ssc, 1)
            eng.activation(l_inv[:, :, :, :], l_ssum[:, :, :, :], ACT.Sqrt).then_inc(l_norm, 1)

            def columns(c):
                eng.wait_ge(l_oT, c + 1)
                eng.activation(l_kT[:, c, :], bank(6 + c % 2), ACT.Copy).then_inc(l_oTs, 1)

            for c in range(NC2):
                eng.wait_ge(l_stp, c + 1)
                if c >= 2:
                    eng.wait_ge(l_o, c - 1)
                else:
                    eng.wait_ge(l_zero, 1)
                for r in range(2):
                    own = slice(DM * r, DM * r + DM)
                    i = eng.activation(l_st[own, c % 2, :, own],
                                       bank(2 + c % 2)[own, 0:(NT - 1) * P].rearrange("p (u d) -> p u d", d=P)[:, :, own],
                                       ACT.Copy)
                i.then_inc(l_sts, 1)
                if c >= 2:
                    columns(c - 2)
            columns(NC2 - 2)
            columns(NC2 - 1)

        def act_adapter(eng, n):
            eng.wait_ge(d_lgs, n + 1)
            eng.activation(d_ex[:, :], d_lg[:, :], ACT.Exp, bias=d_negm[:, 0:1],
                           accum_out=d_z[:, 0:1]).then_inc(d_exs, 1)
            for k in range(KD):
                eng.wait_ge(d_dn, KD * n + k + 1)
                eng.activation(d_hid[:, k, :], bank(k), ACT.Gelu, bias=down_b[:, k:k + 1]).then_inc(d_hs, 1)
            eng.wait_ge(d_wTp, n + 1)
            eng.activation(d_wT[0:E, :], bank(5)[0:E, 0:P], ACT.Copy).then_inc(d_wTs, 1)

        def act_rel(eng):
            act_hi(eng, 2, float(HD) ** -0.5)
            for i in range(P // 8):
                q8 = slice(8 * i, 8 * i + 8)
                eng.wait_ge(r_rel_ok, 2 * i + 2)
                v = bank((2 * i + 1) % 4).rearrange("p (i t h) -> p h t i", i=8, t=NT)
                eng.activation(sc[:, :, 1:10:4, q8], v[:, :, 1:4, :], ACT.Copy)
                eng.activation(sc[:, :, 3, q8], v[:, :, 3, :], ACT.Copy).then_inc(r_odd, 1)
                eng.wait_ge(r_even, i + 1)
                v = bank((2 * i) % 4).rearrange("p (i t h) -> p h t i", i=8, t=NT)
                eng.activation(sc[:, :, 2:7:4, q8], v[:, :, 2:4, :], ACT.Copy).then_inc(r_late, 1)
                if i % 2 == 0:
                    act_stack(eng, 2, i // 2)

            def exps(h):
                at = {0: 0, 1: P, 2: 3 * P, 3: 6 * P}
                if h >= 2:
                    eng.wait_ge(r_pT, 3 * (h - 1))
                for n, (t, bk, col) in enumerate(ROW_JOBS):
                    eng.wait_ge(r_max, 4 * h + (3 if n == 1 else n + 1))
                    eng.activation(r_prob[:, h % 2, at[t]:at[t] + (t + 1) * P],
                                   bank(bk)[:, col:col + (t + 1) * P], ACT.Exp,
                                   bias=r_neg_max[:, h % 2, t:t + 1]).then_inc(r_p, 1)

            def columns(h):
                for j in range(2):
                    eng.wait_ge(r_pT, 3 * h + j + 1)
                    if h >= 2:
                        eng.wait_ge(a_pv, 2 * H + h - 1)
                    eng.activation(r_probT[:, h % 2, JOB_AT[j]:JOB_AT[j] + JOB_N[j]],
                                   bank(5 + (3 * h + j) % 2)[:, 0:JOB_N[j]], ACT.Copy).then_inc(r_pTa, 1)

            for i in range(1, H + 2):
                if i >= G4 + 2 and (i - 2) % G4 == 0:
                    group_columns(eng, 2, (i - 2) // G4 - 1, 7)
                if i >= 2:
                    columns(i - 2)
                if i <= H:
                    exps(i - 1)
            group_columns(eng, 2, NG - 1, 7)
            eng.wait_ge(a_oT, 3)
            eng.activation(xnT[:, :], bank(0), ACT.Copy).then_inc(a_oTs, 1)

        @block.scalar
        def _(eng):
            eng.wait_ge(weights, 6)
            with eng.Fori(0, B) as b:
                act_norm(eng, 0)
                act_attn(eng, 0, float(HD) ** -0.5)
                act_norm(eng, 1)
                act_moe(eng, 0)
                act_norm(eng, 2)
                act_attn(eng, 1, float(P) ** -0.5)
                act_norm(eng, 3)
                act_moe(eng, 1)
                act_norm(eng, 4)
                act_lin(eng)
                act_norm(eng, 5)
                act_adapter(eng, 0)
                act_norm(eng, 6)
                act_rel(eng)
                act_norm(eng, 7)
                act_adapter(eng, 1)
                eng.nop().then_inc(ended, 1)
                eng.wait_ge(started, b + 1)

        def pe_norm(eng, n):
            for t in range(NT):
                eng.wait_ge(xn_ok, 4 * n + t + 1)
                m = eng.transpose(bank(7)[:, P * t:P * t + P], xn[:, t, :], ident[:, :])
            m.then_inc(xn_T, 1)

        def pe_project(eng, n, w):
            eng.wait_ge(xnT_ok, (0, 2, 6)[n] + 1)
            eng.matmul(bank(0), w[:, 0, :], xnT[:, :], start=True, stop=True).then_inc(a_proj, 1)
            eng.matmul(bank(1), w[:, 1, :], xnT[:, :], start=True, stop=True).then_inc(a_proj, 1)
            for t in range(NT):
                m = eng.matmul(bank(2)[:, P * t:P * t + P], xnT[:, P * t:P * t + P], w[:, 2, :],
                               start=True, stop=True)
            m.then_inc(a_proj, 1)

        def pe_spread(eng, n, i):
            g, w2 = i // 2, i % 2
            if g == 0:
                eng.wait_ge(a_hi, 2 * n + w2 + 1)
                eng.wait_ge(a_mid, 2 * n + w2 + 1)
                eng.wait_ge(a_lo, 2 * n + w2 + 1)
            if i >= 4:
                eng.wait_ge((a_qst, a_kst)[w2], H // 2 * n + g - 1)
            for x_part in range(3):
                spread = (spread_q, spread_k)[w2][:, x_part, g].rearrange("p r s d -> p (r s d)")
                m = eng.matmul(bank(spread_bank(n, i)), spread, qk_part(w2, x_part),
                               start=(x_part == 0), stop=(x_part == 2))
            m.then_inc(a_spread, 1)

        def weigh_columns(eng, bk, h, p_cols):
            row = 32 * (h % G4)
            for s in range(NT):
                at = P * SLOT[(s, s)]
                m = eng.matmul(bank(bk)[row:row + HD + 1, P * s:T], values[:, s, h, :],
                               p_cols[:, h % 2, at:at + T - P * s], start=(s == 0), stop=(s == NT - 1))
            m.then_inc(a_pv, 1)

        def group_rows(eng, n, G, bk):
            eng.wait_ge(a_cols, NG * n + G + 1)
            for t in range(NT):
                m = eng.transpose(bank(bk)[:, P * t:P * t + P], xnT[:, P * t:P * t + P], ident[:, :])
            m.then_inc(a_rows, 1)

        def pe_out(eng, n, w, bias):
            eng.wait_ge(a_o, NG * (n + 1))
            for t in range(NT):
                m = eng.transpose(bank(0)[:, P * t:P * t + P], xn[:, t, :], ident[:, :])
            m.then_inc(a_oT, 1)
            eng.wait_ge(a_oTs, n + 1)
            for t in range(NT):
                m = eng.matmul(bank(1)[:, P * t:P * t + P], xnT[:, P * t:P * t + P], w[:, 3, :],
                               start=True, stop=bias is None)
                if bias is not None:
                    m = eng.matmul(bank(1)[:, P * t:P * t + P], ones[0:1, 0:P], bias, start=False, stop=True)
            m.then_inc(a_y, 1)

        def rows_of(G):
            return ([[(hh, 3, 0)] for hh in range(G4)] + [[(hh, 2, 0)] for hh in range(G4)] +
                    [[(r, t, 0), (r + 2, t, (t + 1) * P)] for t in (1, 0) for r in range(2)])

        NROW = len(rows_of(0))
        FIRST_ROWS = [range(2 * i, 2 * i + 2) for i in range(NROW // 2)]

        def stacked(st, h, cols):
            r = h % 2
            return st[64 * r:64 * r + KROWS, h // 2, cols]

        def pe_attn(eng, n, w):
            pe_project(eng, n, w)

            def score_rows(G, jobs):
                for i in jobs:
                    k = NROW * G + i
                    if k == 2:
                        eng.wait_ge(a_v, n + 1)
                    if k >= 3:
                        eng.wait_ge(a_max, NROW * NG * n + k - 2)
                    for hh, t, col in rows_of(G)[i]:
                        h, N = G4 * G + hh, (t + 1) * P
                        eng.wait_ge(a_qst, H // 2 * n + h // 2 + 1)
                        eng.wait_ge(a_kst, H // 2 * n + h // 2 + 1)
                        eng.matmul(bank(k % 3)[:, col:col + N], stacked(q_st, h, slice(P * t, P * t + P)),
                                   stacked(k_st, h, slice(0, N)), start=True, stop=False)
                        m = eng.matmul(bank(k % 3)[:, col + N - P:col + N], identb[:, :], mask_qk[:, :],
                                       start=False, stop=True)
                    m.then_inc(a_s1, 1)

            def max_columns(G):
                eng.wait_ge(a_mparts, NG * n + G + 1)
                if G >= 2:
                    eng.wait_ge(a_o, NG * n + G - 1)
                for t in range(NT):
                    m = eng.transpose(bank(6 + G % 2)[0:3 * G4, P // 2 * t:P // 2 * (t + 1)].bitcast(BF16),
                                      max_part[:, G % 2, t, 0:3 * G4], identb[:, :])
                m.then_inc(a_maxT, 1)

            def score_columns(h):
                G, hh = h // G4, h % G4
                if hh == 0:
                    eng.wait_ge(a_mrow, NG * n + G + 1)
                for j in range(3):
                    if h >= 1:
                        eng.wait_ge(a_prob, 3 * (H * n + h - 1) + j + 1)
                    col = 0
                    for s in JOBS[j]:
                        N = T - P * s
                        eng.matmul(bank(3 + j)[:, col:col + N], stacked(k_st, h, slice(P * s, P * s + P)),
                                   stacked(q_st, h, slice(P * s, T)), start=True, stop=False)
                        eng.matmul(bank(3 + j)[:, col:col + P], identb[:, :], mask_kq[:, :],
                                   start=False, stop=False)
                        m = eng.matmul(bank(3 + j)[:, col:col + N], pick_max[:, hh, :],
                                       neg_maxT[:, G % 2, P * s:T], start=False, stop=True)
                        col += N
                    m.then_inc(a_s2, 1)

            def weigh(h):
                G, hh = h // G4, h % G4
                eng.wait_ge(a_prob, 3 * (H * n + h + 1))
                weigh_columns(eng, 6 + G % 2, h, prob)

            for g in range(H // 2):
                pe_spread(eng, n, 2 * g)
                pe_spread(eng, n, 2 * g + 1)
                if g >= 2:
                    score_rows(0, FIRST_ROWS[g - 2])
            max_columns(0)
            chunks = [range(0, 4), range(4, 8), range(8, NROW), range(0)]
            for h in range(H):
                G = h // G4
                score_columns(h)
                if G < NG - 1:
                    score_rows(G + 1, chunks[h % G4])
                if h % G4 == G4 - 1 and G < NG - 1:
                    max_columns(G + 1)
                if h >= 1:
                    weigh(h - 1)
                if h % G4 == 1 and G >= 1:
                    group_rows(eng, n, G - 1, 6 + (G - 1) % 2)
            weigh(H - 1)
            group_rows(eng, n, NG - 1, 6 + (NG - 1) % 2)
            pe_out(eng, n, w, None)

        def pe_moe(eng, n):
            eng.wait_ge(xnT_ok, 2 * n + 2)
            for t in range(NT):
                eng.matmul(bank(6)[:, E * t:E * t + E], xnT[:, P * t:P * t + P], ws[:, :], start=True, stop=False)
                m = eng.matmul(bank(6)[:, E * t:E * t + E], ones[0:1, 0:P], bs_row[:, :], start=False, stop=True)
            m.then_inc(m_logit, 1)

            def down(e):
                eng.wait_ge(m_h, NF * (E * n + e + 1))
                if e >= 2:
                    eng.wait_ge(m_acc, E * n + e - 1)
                for t in range(NT):
                    for j, (_, w) in enumerate(FT):
                        m = eng.matmul(bank(4 + e % 2)[:, P * t:P * t + P],
                                       hidden[0:w, e % 2, j, P * t:P * t + P], wd[0:w, e, j, :],
                                       start=(j == 0), stop=(j == NF - 1))
                m.then_inc(m_y, 1)

            for e in range(E):
                for j, (f0, w) in enumerate(FT):
                    i = NF * e + j
                    if i >= 2:
                        eng.wait_ge(m_silu, E * NF * n + i - 1)
                    eng.matmul(bank(i % 2)[0:w, :], wg[:, e, f0:f0 + w], xnT[:, :],
                               start=True, stop=True).then_inc(m_g, 1)
                    if i >= 2:
                        eng.wait_ge(m_h, E * NF * n + i - 1)
                    eng.matmul(bank(2 + i % 2)[0:w, :], wu[:, e, f0:f0 + w], xnT[:, :],
                               start=True, stop=True).then_inc(m_u, 1)
                if e >= 1:
                    down(e - 1)
            down(E - 1)

        def pe_lin(eng):
            eng.wait_ge(xnT_ok, 5)
            for t in range(NT):
                m = eng.matmul(bank(6)[:, H * t:H * t + H], xnT[:, P * t:P * t + P], wbeta[:, :],
                               start=True, stop=True)
            m.then_inc(l_bz, 1)

            def sum_squares(i):
                eng.wait_ge(l_sqr, i + 1)
                for t in range(NT):
                    at = H * t + 2 * i
                    m = eng.matmul(bank(5)[:, at:at + 2], l_sq[:, i % 2, P * t:P * t + P], pair_of[:, :],
                                   start=True, stop=True)
                m.then_inc(l_ss, 1)

            for i in range(2 * NC2):
                if i >= 2:
                    eng.wait_ge(l_qk, i - 1)
                eng.matmul(bank(i % 2), (wq_l, wk_l)[i % 2][:, P * (i // 2):P * (i // 2) + P], xnT[:, :],
                           start=True, stop=True).then_inc(l_pq, 1)
                if i >= 2:
                    eng.wait_ge(l_kv, i - 1)
                t, c = (i % 8) // 2, i % 2
                eng.matmul(bank(2 + i % 2), xnT[:, P * t:P * t + P],
                           (wk_l, wv_l)[i // 8][:, 512 * c:512 * c + 512], start=True, stop=True).then_inc(l_pn, 1)
                if i % 2 == 1:
                    sum_squares(i // 2)

            def scores(c):
                for r in range(2):
                    h = 2 * c + r
                    if h >= 2:
                        eng.wait_ge(l_wts, h - 1)
                    else:
                        eng.wait_ge(l_qk, 2 * NC2)
                    for t in range(NT):
                        m = eng.matmul(bank(r)[:, P * t:P * t + P], l_kT[64 * r:64 * r + 64, c, P * t:P * t + P],
                                       l_qT[64 * r:64 * r + 64, c, P * t:P * t + P], start=True, stop=True)
                    m.then_inc(l_sc, 1)

            def states(c):
                eng.wait_ge(l_vks, c + 1)
                if c >= 2:
                    eng.wait_ge(l_sts, c - 1)
                else:
                    eng.wait_ge(l_kv, 2 * NC2)
                for u in range(NT - 1):
                    for s in range(u + 1, NT):
                        m = eng.matmul(bank(2 + c % 2)[:, P * u:P * u + P], l_k[:, s, P * c:P * c + P],
                                       l_vk[:, s, P * c:P * c + P], start=(s == u + 1), stop=(s == NT - 1))
                m.then_inc(l_stp, 1)

            def outputs(c):
                eng.wait_ge(l_wts, 2 * c + 2)
                eng.wait_ge(l_sts, c + 1)
                if c >= 2:
                    eng.wait_ge(l_ts, c - 1)
                else:
                    eng.wait_ge(l_ssc, 1)
                for t in range(NT):
                    o = bank(4 + c % 2)[:, P * t:P * t + P]
                    for r in range(2):
                        m = eng.matmul(o[:, DM * r:DM * r + DM], l_wt[:, c % 2, r, t, :],
                                       l_vk[:, t, P * c + DM * r:P * c + DM * r + DM],
                                       start=(r == 0), stop=(t == NT - 1 and r == 1), skip_group_check=True)
                    if t < NT - 1:
                        m = eng.matmul(o, l_qT[:, c, P * t:P * t + P], l_st[:, c % 2, t, :],
                                       start=False, stop=True, skip_group_check=True)
                m.then_inc(l_o, 1)

            def transposes(c):
                eng.wait_ge(l_os, c + 1)
                if c >= 2:
                    eng.wait_ge(l_oTs, c - 1)
                for t in range(NT):
                    m = eng.transpose(bank(6 + c % 2)[:, P * t:P * t + P], l_v[:, t, P * c:P * c + P], ident[:, :])
                m.then_inc(l_oT, 1)

            for c in range(NC2 + 3):
                if c < NC2:
                    scores(c)
                    states(c)
                if 1 <= c <= NC2:
                    outputs(c - 1)
                if c >= 3:
                    transposes(c - 3)
            eng.wait_ge(l_oTs, NC2)
            for t in range(NT):
                for c in range(NC2):
                    m = eng.matmul(bank(0)[:, P * t:P * t + P], l_kT[:, c, P * t:P * t + P], wout_l[:, c, :],
                                   start=(c == 0), stop=(c == NC2 - 1))
            m.then_inc(l_y, 1)

        def pe_adapter(eng, n):
            eng.wait_ge(xnT_ok, (6, 8)[n])
            for k in range(KD):
                eng.matmul(bank(k), downT[:, k, :], xnT[:, :], start=True, stop=True).then_inc(d_dn, 1)
            eng.wait_ge(d_pool, n + 1)
            eng.matmul(bank(6)[:, 0:E], pool_rep[:, :], gateT[:, :], start=True, stop=True).then_inc(d_gate_ok, 1)
            eng.wait_ge(d_ws, n + 1)
            eng.transpose(bank(5)[0:E, 0:P], d_w[:, :], ident[:, :]).then_inc(d_wTp, 1)
            eng.wait_ge(d_wTs, n + 1)
            eng.wait_ge(d_hs, KD * (n + 1))
            eng.wait_ge(d_ups, n + 1)
            for t in range(NT):
                o = bank(4)[:, P * t:P * t + P]
                for k in range(KD):
                    eng.matmul(o, d_hid[:, k, P * t:P * t + P], d_up[:, k, :], start=(k == 0), stop=False)
                m = eng.matmul(o, d_wT[0:E, :], up_b[:, :], start=False, stop=True)
            m.then_inc(d_y, 1)

        def pe_rel(eng, w):
            pe_project(eng, 2, w)
            eng.wait_ge(a_res, 6)
            eng.wait_ge(a_v, 3)
            for i in range(P // 8):
                for par in range(2):
                    k = 2 * i + par
                    if i >= 2:
                        eng.wait_ge((r_even, r_odd)[par], i - 1)
                    if i >= 2 and par == 0:
                        eng.wait_ge(r_late, i - 1)
                    c = 8 * i // IC
                    eng.wait_ge(r_qm, c + 1 + c // 2 + 1)
                    if c >= 1:
                        eng.wait_ge(r_qmp, (c + 1) // 2)
                    for q in range(8 * i, 8 * i + 8):
                        first = (P * par - q) % (2 * P)
                        for n, (rp, qp) in enumerate([(0, 0), (0, 1), (1, 0)]):
                            m = eng.matmul(bank(k % 4)[:, 64 * (q % 8):64 * (q % 8) + 64],
                                           relT[:, rp, first:first + P], q_masked[c % 2][:, qp, q % IC, :],
                                           start=(n == 0), stop=(n == 2))
                    m.then_inc(r_rel_ok, 1)
                pe_spread(eng, 2, i)

            def qk(h, j):
                k = 3 * h + j
                if k >= 2:
                    eng.wait_ge(r_sum, k - 1)
                else:
                    eng.wait_ge(r_even, P // 8)
                    eng.wait_ge(r_late, P // 8)
                    eng.wait_ge(r_odd, P // 8)
                    eng.wait_ge(a_qst, 3 * H // 2)
                    eng.wait_ge(a_kst, 3 * H // 2)
                col = 0
                for s in JOBS[j]:
                    N = T - P * s
                    eng.matmul(bank(k % 2)[:, col:col + N], stacked(k_st, h, slice(P * s, P * s + P)),
                               stacked(q_st, h, slice(P * s, T)), start=True, stop=False)
                    m = eng.matmul(bank(k % 2)[:, col:col + P], identb[:, :], mask_kq[:, :],
                                   start=False, stop=True)
                    col += N
                m.then_inc(r_main, 1)

            def rows(h):
                eng.wait_ge(r_sum, 3 * (h + 1))
                for i, (t, bk, col) in enumerate(ROW_JOBS):
                    if h >= 1 and i != 2:
                        eng.wait_ge(r_p, 4 * (h - 1) + (1, 3, 3, 4)[i])
                    for s in range(t + 1):
                        m = eng.transpose(bank(bk)[:, col + P * s:col + P * s + P], sc[:, h, SLOT[(s, t)], :],
                                          ident[:, :])
                    if i != 1:
                        m.then_inc(r_sT, 1)

            def columns(h, j):
                at = {0: 0, 1: P, 2: 3 * P, 3: 6 * P}
                k = 3 * h + j
                if j == 0:
                    eng.wait_ge(r_p, 4 * (h + 1))
                    if h >= G4 + 1 and h % G4 == 1:
                        eng.wait_ge(a_o, 2 * NG + h // G4)
                if k >= 2:
                    h2, j2 = (k - 2) // 3, (k - 2) % 3
                    if j2 < 2:
                        eng.wait_ge(r_pTa, 2 * h2 + j2 + 1)
                    else:
                        eng.wait_ge(r_pTv, h2 + 1)
                first = JOB_AT[j] // P
                for b in range(first, first + JOB_N[j] // P):
                    s, t = BLOCKS[b]
                    m = eng.transpose(bank(5 + k % 2)[:, P * (b - first):P * (b - first) + P],
                                      r_prob[:, h % 2, at[t] + P * s:at[t] + P * s + P], ident[:, :])
                m.then_inc(r_pT, 1)

            def weigh(h):
                G, hh = h // G4, h % G4
                eng.wait_ge(r_pTa, 2 * h + 2)
                eng.wait_ge(r_pTv, h + 1)
                if hh == 0 and G >= 1:
                    eng.wait_ge(a_cols, 2 * NG + G)
                weigh_columns(eng, 7, h, r_probT)

            for i in range(H + 2):
                h = i - 2
                if h >= 0:
                    columns(h, 0)
                    columns(h, 1)
                if i < H:
                    qk(i, 0)
                if h >= 0:
                    columns(h, 2)
                if i < H:
                    qk(i, 1)
                if h >= G4 and h % G4 == 0:
                    eng.wait_ge(r_pTa, 2 * h + 2)
                    group_rows(eng, 2, h // G4 - 1, 5 + (3 * h + 1) % 2)
                if 1 <= i <= H:
                    rows(i - 1)
                if i < H:
                    qk(i, 2)
                if h >= 0:
                    weigh(h)
            group_rows(eng, 2, NG - 1, 7)
            pe_out(eng, 2, w, bp_row[:, :])

        @block.tensor
        def _(eng):
            eng.wait_ge(loaded, LOADED)
            eng.wait_ge(const, CONSTS)
            for n in range(NSTAGE):
                m = eng.transpose(bank(n // 4)[:, P * (n % 4):P * (n % 4) + P], stage[:, n, :], ident[:, :])
                if n % 4 == 3 or n == NSTAGE - 1:
                    m.then_inc(stage_T, 1)
            eng.transpose(bank(6)[:, 0:E], stage_gate[0:E, :], ident[0:E, 0:E]).then_inc(stage_T, 1)
            eng.wait_ge(weights, 6)
            with eng.Fori(0, B) as b:
                pe_norm(eng, 0)
                pe_attn(eng, 0, w_a)
                pe_norm(eng, 1)
                pe_moe(eng, 0)
                pe_norm(eng, 2)
                pe_attn(eng, 1, w_b)
                pe_norm(eng, 3)
                pe_moe(eng, 1)
                pe_norm(eng, 4)
                pe_lin(eng)
                pe_norm(eng, 5)
                pe_adapter(eng, 0)
                pe_norm(eng, 6)
                pe_rel(eng, w_r)
                pe_norm(eng, 7)
                pe_adapter(eng, 1)
                eng.nop().then_inc(ended, 1)
                eng.wait_ge(started, b + 1)

        @block.vector
        def _(eng):
            steps = [0]

            def link(ins):
                steps[0] += 1
                ins.then_inc(step, 1)
                eng.wait_ge(step, steps[0])

            def flat(n):
                return bank(n).rearrange("p (t d) -> p t d", t=NT)

            def norm(n):
                if n == 0:
                    eng.wait_ge(x_in, 16)
                else:
                    eng.wait_ge(x_done, n)
                for t in range(NT):
                    eng.bn_stats(stats[:, t, :], x[:, t, :]).then_inc(normed, 1)
                for t in range(NT):
                    eng.wait_ge(normed, 8 * n + (t + 1 if t == 0 else 4 + t))
                    eng.bn_aggr(moments[:, t, :], stats[:, t, :]).then_inc(normed, 1)
                eng.wait_ge(rstd_ok, n + 1)
                for t in range(NT):
                    eng.tensor_scalar(xn[:, t, :], x[:, t, :], moments[:, t, 0:1], rstd[:, t:t + 1],
                                      ALU.subtract, ALU.mult).then_inc(xn_ok, 1)

            def add_to_x(bk):
                eng.tensor_tensor(x[:, :, :], x[:, :, :], flat(bk), ALU.add).then_inc(x_done, 1)

            def parts_of_qk(n, scale):
                for w in range(2):
                    eng.wait_ge(a_hi, 2 * n + w + 1)
                    eng.scalar_tensor_tensor(out=res[:, w, :], in0=bank(w), scalar=(scale, 1.0)[w],
                                             in1=qk_part(w, 0), op0=ALU.mult,
                                             op1=ALU.subtract).then_inc(a_res, 1)
                if n == 2:
                    eng.memset(q_parts[:, 0:2, 0:1], 0.0).then_inc(r_shift, 1)
                eng.wait_ge(a_proj, 3 * n + 3)
                eng.tensor_copy(values[:, :, :, 0:HD], bank(2).rearrange("p (t h d) -> p t h d", t=NT, h=H))\
                   .then_inc(a_v, 1)
                for w in range(2):
                    eng.wait_ge(a_res, 2 * n + w + 1)
                    eng.wait_ge(a_mid, 2 * n + w + 1)
                    eng.tensor_tensor(qk_part(w, 2), res[:, w, :], qk_part(w, 1),
                                      ALU.subtract).then_inc(a_lo, 1)

            def stack_k(n, g):
                eng.wait_ge(a_spread, H * n + 2 * g + 2)
                eng.tensor_copy(k_st[:, g, :], bank(spread_bank(n, 2 * g + 1))).then_inc(a_kst, 1)

            def heads_out(n, G, bk, inv):
                eng.wait_ge(a_rows, NG * n + G + 1)
                o = bank(bk).rearrange("p (t h d) -> p t h d", t=NT, h=G4)
                link(eng.reciprocal(inv[:, G % 2, :, :].unsqueeze(3), o[:, :, :, HD:HD + 1]))
                eng.tensor_tensor(
                    xn[:, :, HD * G4 * G:HD * G4 * (G + 1)].rearrange("p t (h d) -> p t h d", h=G4),
                    o[:, :, :, 0:HD], inv[:, G % 2, :, :].unsqueeze(3).to_broadcast([P, NT, G4, HD]),
                    ALU.mult).then_inc(a_o, 1)

            def attn(n, scale):
                parts_of_qk(n, scale)

                def row_max(G, jobs):
                    for i in jobs:
                        k = NROW * (NG * n + G) + i
                        eng.wait_ge(a_s1, k + 1)
                        job = rows_of(G)[i]
                        hh, t, _ = job[0]
                        src = bank((NROW * G + i) % 3)[:, 0:len(job) * (t + 1) * P]
                        src = src.rearrange("p (h k) -> p h k", h=len(job))
                        hs = slice(hh, hh + 2 * len(job) - 1, 2)
                        eng.tensor_reduce(neg_max[:, G % 2, t, hs], src, AX.X, ALU.max,
                                          negate=True).then_inc(a_max, 1)

                def split_max(G):
                    b = G % 2
                    eng.wait_ge(a_max, NROW * (NG * n + G + 1))
                    hi, mid, lo = (max_part[:, b, :, G4 * p:G4 * p + G4] for p in range(3))
                    link(eng.tensor_copy(hi, neg_max[:, b, :, :]))
                    link(eng.tensor_tensor(max_res[:, b, :, :], neg_max[:, b, :, :], hi, ALU.subtract))
                    link(eng.tensor_copy(mid, max_res[:, b, :, :]))
                    eng.tensor_tensor(lo, max_res[:, b, :, :], mid, ALU.subtract).then_inc(a_mparts, 1)

                for g in range(H // 2):
                    stack_k(n, g)
                    if g >= 2:
                        row_max(0, FIRST_ROWS[g - 2])
                split_max(0)
                for G in range(NG):
                    if G < NG - 1:
                        row_max(G + 1, range(0, 8))
                    if G >= 1:
                        heads_out(n, G - 1, 6 + (G - 1) % 2, rden)
                    if G < NG - 1:
                        row_max(G + 1, range(8, NROW))
                        split_max(G + 1)
                heads_out(n, NG - 1, 6 + (NG - 1) % 2, rden)
                eng.wait_ge(a_y, n + 1)
                add_to_x(1)

            def moe(n):
                eng.wait_ge(m_logit, n + 1)
                link(eng.tensor_copy(lg[:, :, :], bank(6)[:, 0:NT * E].rearrange("p (t e) -> p t e", t=NT)))
                link(eng.tensor_reduce(top[:, :], lg[:, :, :], AX.X, ALU.max))
                eng.tensor_tensor(lgd[:, :, :], lg[:, :, :], top[:, :].unsqueeze(2).to_broadcast([P, NT, E]),
                                  ALU.subtract).then_inc(m_lgd, 1)
                mine = lg[:, :, :].unsqueeze(3).to_broadcast([P, NT, E, E])
                other = lg[:, :, :].unsqueeze(2).to_broadcast([P, NT, E, E])
                link(eng.tensor_tensor(eq[:, :, :, :], other, mine, ALU.is_equal))
                link(eng.tensor_tensor(eq[:, :, :, :], eq[:, :, :, :],
                                       before[:, :, :].unsqueeze(1).to_broadcast([P, NT, E, E]), ALU.mult))
                link(eng.tensor_tensor(gt[:, :, :, :], other, mine, ALU.is_gt))
                link(eng.tensor_tensor(gt[:, :, :, :], gt[:, :, :, :], eq[:, :, :, :], ALU.add))
                link(eng.tensor_reduce(rank[:, :, :], gt[:, :, :, :], AX.X, ALU.add))
                eng.wait_ge(m_ex, n + 1)
                link(eng.scalar_tensor_tensor(out=mix[:, :, :], in0=rank[:, :, :], scalar=2.0, in1=ex[:, :, :],
                                              op0=ALU.is_lt, op1=ALU.mult))
                link(eng.tensor_reduce(tot[:, :], mix[:, :, :], AX.X, ALU.add))
                link(eng.reciprocal(tot[:, :], tot[:, :]))
                eng.tensor_tensor(mix[:, :, :], mix[:, :, :], tot[:, :].unsqueeze(2).to_broadcast([P, NT, E]),
                                  ALU.mult).then_inc(m_mix, 1)

                def add(e):
                    eng.wait_ge(m_y, E * n + e + 1)
                    if e == 0:
                        eng.wait_ge(m_mix, n + 1)
                    else:
                        eng.wait_ge(m_acc, E * n + e)
                    for t in range(NT):
                        i = eng.scalar_tensor_tensor(out=x[:, t, :], in0=bank(4 + e % 2)[:, P * t:P * t + P],
                                                     scalar=mix[:, t, e:e + 1], in1=x[:, t, :],
                                                     op0=ALU.mult, op1=ALU.add)
                    i.then_inc(m_acc, 1)
                    if e == E - 1:
                        eng.wait_ge(m_acc, E * (n + 1))
                        eng.nop().then_inc(x_done, 1)

                for e in range(E):
                    for j, (_, w) in enumerate(FT):
                        i = NF * e + j
                        eng.wait_ge(m_u, E * NF * n + i + 1)
                        eng.wait_ge(m_silu, E * NF * n + i + 1)
                        if e >= 2:
                            eng.wait_ge(m_y, E * n + e - 1)
                        eng.tensor_tensor(hidden[0:w, e % 2, j, :], silu[0:w, i % 2, :], bank(2 + i % 2)[0:w, :],
                                          ALU.mult).then_inc(m_h, 1)
                    if e >= 1:
                        add(e - 1)
                add(E - 1)

            def lin():
                eng.wait_ge(l_be, 1)
                link(eng.tensor_scalar(l_beta[:, :, :], l_beta[:, :, :], 1.0, None, ALU.add))
                eng.reciprocal(l_beta[:, :, :], l_beta[:, :, :]).then_inc(l_bok, 1)
                for i in range(2 * NC2):
                    t, c = (i % 8) // 2, i % 2
                    eng.wait_ge(l_pn, i + 1)
                    eng.tensor_copy((l_k, l_v)[i // 8][:, t, 512 * c:512 * c + 512], bank(2 + i % 2))\
                       .then_inc(l_kv, 1)
                    if 1 <= i <= NC2:
                        j = i - 1
                        eng.wait_ge(l_sqks, j + 1)
                        eng.tensor_reduce(l_ssum[:, 1, j // 2, 8 * (j % 2):8 * (j % 2) + 8],
                                          l_sqk[:, j % 2, :].rearrange("p (h d) -> p h d", d=DM), AX.X,
                                          ALU.add).then_inc(l_ssk, 1)
                eng.wait_ge(l_ss, NC2)
                eng.tensor_copy(l_ssum[:, 0, :, :].rearrange("p t h -> p (t h)"),
                                bank(5)[:, 0:NT * H]).then_inc(l_ssc, 1)
                eng.wait_ge(l_norm, 1)
                eng.wait_ge(l_ssc, 1)
                eng.wait_ge(l_ssk, NC2)
                link(eng.tensor_scalar(l_inv[:, :, :, :], l_inv[:, :, :, :], 1e-18, None, ALU.max))
                link(eng.reciprocal(l_rec[:, :, :, :], l_inv[:, :, :, :]))
                link(eng.tensor_tensor(l_rec[:, :, :, :], l_rec[:, :, :, :], l_ssum[:, :, :, :], ALU.mult))
                link(eng.tensor_tensor(l_inv[:, :, :, :], l_inv[:, :, :, :], l_rec[:, :, :, :], ALU.add))
                link(eng.tensor_scalar(l_inv[:, :, :, :], l_inv[:, :, :, :], 0.5, None, ALU.mult))
                link(eng.tensor_scalar(l_inv[:, :, :, :], l_inv[:, :, :, :], 1e-12, None, ALU.max))
                link(eng.reciprocal(l_inv[:, :, :, :], l_inv[:, :, :, :]))
                link(eng.tensor_scalar(l_inv[:, 0, :, :], l_inv[:, 0, :, :], float(DM) ** -0.5, None, ALU.mult))
                eng.wait_ge(l_kv, 2 * NC2)

                def scale_values(c):
                    src = l_v[:, :, P * c:P * c + P].rearrange("p t (r d) -> p t r d", r=2)
                    dst = l_vk[:, :, P * c:P * c + P].rearrange("p t (r d) -> p t r d", r=2)
                    eng.tensor_tensor(dst, src,
                                      l_inv[:, 1, :, 2 * c:2 * c + 2].unsqueeze(3).to_broadcast([P, NT, 2, DM]),
                                      ALU.mult).then_inc(l_vks, 1)

                def mask_scores(c):
                    for r in range(2):
                        h = 2 * c + r
                        eng.wait_ge(l_sc, h + 1)
                        if c >= 2:
                            eng.wait_ge(l_o, c - 1)
                        eng.tensor_tensor(l_wt[:, c % 2, r, :, :], flat(r),
                                          keep_ge[:, :].unsqueeze(1).to_broadcast([P, NT, P]),
                                          ALU.mult).then_inc(l_wts, 1)

                def scale_out(c):
                    eng.wait_ge(l_o, c + 1)
                    if c >= 2:
                        eng.wait_ge(l_os, c - 1)
                    o = bank(4 + c % 2).rearrange("p (t r d) -> p t r d", t=NT, r=2)
                    dst = l_tmp[:, c % 2, :, :].rearrange("p t (r d) -> p t r d", r=2)
                    eng.tensor_tensor(dst, o,
                                      l_inv[:, 0, :, 2 * c:2 * c + 2].unsqueeze(3).to_broadcast([P, NT, 2, DM]),
                                      ALU.mult).then_inc(l_ts, 1)

                scale_values(0)
                scale_values(1)
                for c in range(NC2):
                    mask_scores(c)
                    if c + 2 < NC2:
                        scale_values(c + 2)
                    if c >= 1:
                        scale_out(c - 1)
                scale_out(NC2 - 1)
                eng.wait_ge(l_y, 1)
                add_to_x(0)

            def adapter(n):
                eng.wait_ge(xnT_ok, (6, 8)[n])
                link(eng.tensor_reduce(pooled[:, 0:1], xnT[:, :], AX.X, ALU.add))
                eng.tensor_scalar(pool_rep[:, :], ones[:, :], pooled[:, 0:1], 1.0 / T, ALU.mult,
                                  ALU.mult).then_inc(d_pool, 1)
                eng.wait_ge(d_gate_ok, n + 1)
                link(eng.tensor_copy(d_lg[:, :], bank(6)[:, 0:E]))
                eng.tensor_reduce(d_negm[:, 0:1], d_lg[:, :], AX.X, ALU.max, negate=True).then_inc(d_lgs, 1)
                eng.wait_ge(d_exs, n + 1)
                link(eng.reciprocal(d_z[:, 0:1], d_z[:, 0:1]))
                link(eng.tensor_scalar(d_p[:, :], d_ex[:, :], d_z[:, 0:1], None, ALU.mult))
                mine = d_p[:, :].unsqueeze(2).to_broadcast([P, E, E])
                other = d_p[:, :].unsqueeze(1).to_broadcast([P, E, E])
                link(eng.tensor_tensor(d_eq[:, :, :], other, mine, ALU.is_equal))
                link(eng.tensor_tensor(d_eq[:, :, :], d_eq[:, :, :], before[:, :, :], ALU.mult))
                link(eng.tensor_tensor(d_gt[:, :, :], other, mine, ALU.is_gt))
                link(eng.tensor_tensor(d_gt[:, :, :], d_gt[:, :, :], d_eq[:, :, :], ALU.add))
                link(eng.tensor_reduce(d_rank[:, :], d_gt[:, :, :], AX.X, ALU.add))
                link(eng.scalar_tensor_tensor(out=d_w[:, :], in0=d_rank[:, :], scalar=2.0, in1=d_p[:, :],
                                              op0=ALU.is_lt, op1=ALU.mult))
                link(eng.tensor_reduce(d_s[:, 0:1], d_w[:, :], AX.X, ALU.add))
                link(eng.tensor_scalar(d_s[:, 0:1], d_s[:, 0:1], 1e-8, None, ALU.add))
                link(eng.reciprocal(d_s[:, 0:1], d_s[:, 0:1]))
                eng.tensor_scalar(d_w[:, :], d_w[:, :], d_s[:, 0:1], None, ALU.mult).then_inc(d_ws, 1)
                eng.wait_ge(d_ws, n + 1)
                link(eng.tensor_scalar(d_w4[:, :], d_w[:, 0:E:2], pair_of[:, 0:1], None, ALU.mult))
                link(eng.scalar_tensor_tensor(out=d_w4[:, :], in0=d_w[:, 1:E:2], scalar=pair_of[:, 1:2],
                                              in1=d_w4[:, :], op0=ALU.mult, op1=ALU.add))
                for k in range(KD):
                    i = eng.tensor_scalar(d_up[:, k, :], upT[:, k, :], d_w4[:, k:k + 1], None, ALU.mult)
                i.then_inc(d_ups, 1)
                eng.wait_ge(d_y, n + 1)
                add_to_x(4)

            def rel():
                parts_of_qk(2, float(HD) ** -0.5)

                def mask(c):
                    if c == 0:
                        eng.wait_ge(r_shift, 1)
                        eng.wait_ge(a_lo, 6)
                    if c >= 2:
                        eng.wait_ge(r_rel_ok, 2 * (IC // 8) * (c - 1))
                    mask_q(eng, c, 0).then_inc(r_qm, 1)
                    if c % 2 == 0:
                        mask_q(eng, c, 1).then_inc(r_qm, 1)

                mask(0)
                mask(1)
                for i in range(P // 8):
                    eng.wait_ge(r_rel_ok, 2 * i + 1)
                    v = bank((2 * i) % 4).rearrange("p (i t h) -> p h t i", i=8, t=NT)
                    q8 = slice(8 * i, 8 * i + 8)
                    eng.tensor_copy(sc[:, :, 0:9:4, q8], v[:, :, 0:3, :])
                    eng.tensor_copy(sc[:, :, 7, q8], v[:, :, 3, :]).then_inc(r_even, 1)
                    if i % 2 == 1:
                        if i // 2 + 2 < P // IC:
                            mask(i // 2 + 2)
                        stack_k(2, i // 2)
                eng.wait_ge(r_late, P // 8)
                eng.wait_ge(r_odd, P // 8)
                eng.wait_ge(r_even, P // 8)
                eng.wait_ge(r_diag, 4 * (P // IC))

                def add(h, j):
                    k = 3 * h + j
                    eng.wait_ge(r_main, k + 1)
                    b = JOB_AT[j] // P
                    v = sc[:, h, b:b + JOB_N[j] // P, :].rearrange("p b i -> p (b i)")
                    eng.tensor_tensor(v, v, bank(k % 2)[:, 0:JOB_N[j]], ALU.add).then_inc(r_sum, 1)

                def row_max(h):
                    for i, (t, bk, col) in enumerate(ROW_JOBS):
                        eng.wait_ge(r_sT, 3 * h + (1, 2, 2, 3)[i])
                        eng.tensor_reduce(r_neg_max[:, h % 2, t:t + 1], bank(bk)[:, col:col + (t + 1) * P], AX.X,
                                          ALU.max, negate=True).then_inc(r_max, 1)

                def column(h):
                    eng.wait_ge(r_pT, 3 * h + 3)
                    if h >= 2:
                        eng.wait_ge(a_pv, 2 * H + h - 1)
                    eng.tensor_copy(r_probT[:, h % 2, JOB_AT[2]:JOB_AT[2] + JOB_N[2]],
                                    bank(5 + (3 * h + 2) % 2)[:, 0:JOB_N[2]]).then_inc(r_pTv, 1)

                for i in range(H + 2):
                    h = i - 2
                    if i < H:
                        add(i, 0)
                    if h >= 0:
                        column(h)
                    if i < H:
                        add(i, 1)
                    if h >= G4 and h % G4 == 0:
                        heads_out(2, h // G4 - 1, 5 + (3 * h + 1) % 2, r_rden)
                    if 1 <= i <= H:
                        row_max(i - 1)
                    if i < H:
                        add(i, 2)
                heads_out(2, NG - 1, 7, r_rden)
                eng.wait_ge(a_y, 3)
                add_to_x(1)

            for n in range((NSTAGE + 3) // 4):
                eng.wait_ge(stage_T, n + 1)
            b4 = [bank(n).rearrange("p (j d) -> p j d", d=P) for n in range(8)]
            eng.tensor_copy(w_b[:, :, :], b4[0]).then_inc(weights, 1)
            eng.tensor_copy(w_r[:, :, :], b4[1]).then_inc(weights, 1)
            eng.tensor_copy(relT[:, 0, 0:2 * P], bank(2)[:, 0:2 * P]).then_inc(set_up, 1)
            eng.tensor_copy(relT[:, 0, 2 * P:3 * P], bank(2)[:, 0:P])
            eng.wait_ge(set_up, 1)
            eng.tensor_tensor(rel_res[:, :], bank(2)[:, 0:2 * P], relT[:, 0, 0:2 * P],
                              ALU.subtract).then_inc(set_up, 1)
            eng.wait_ge(set_up, 2)
            eng.tensor_copy(relT[:, 1, 0:2 * P], rel_res[:, :])
            eng.tensor_copy(relT[:, 1, 2 * P:3 * P], rel_res[:, 0:P])
            eng.tensor_copy(downT[:, 0:2, :], b4[2][:, 2:4, :]).then_inc(weights, 1)
            eng.tensor_copy(downT[:, 2:4, :], b4[3][:, 0:2, :])
            eng.tensor_copy(upT[:, 0:2, :], b4[3][:, 2:4, :]).then_inc(weights, 1)
            eng.tensor_copy(upT[:, 2:4, :], b4[4][:, 0:2, :]).then_inc(weights, 1)
            eng.wait_ge(stage_T, (NSTAGE + 3) // 4 + 1)
            eng.tensor_copy(gateT[:, :], bank(6)[:, 0:E]).then_inc(set_up, 1)
            eng.wait_ge(set_up, 3)
            eng.memset(bank(6), 0.0)
            eng.memset(bank(7), 0.0).then_inc(weights, 1)
            eng.wait_ge(const, CONSTS)
            with eng.Fori(0, B) as b:
                steps[0] = 0
                norm(0)
                attn(0, float(HD) ** -0.5)
                norm(1)
                moe(0)
                norm(2)
                attn(1, float(P) ** -0.5)
                norm(3)
                moe(1)
                norm(4)
                lin()
                norm(5)
                adapter(0)
                norm(6)
                rel()
                norm(7)
                adapter(1)
                eng.nop().then_inc(ended, 1)
                eng.wait_ge(started, b + 1)


_INS = ['L0_attn_a_x', 'L0_attn_a_Wq', 'L0_attn_a_Wk', 'L0_attn_a_Wv', 'L0_attn_a_Wo', 'L0_attn_b_W_attn',
        'L0_attn_b_W_out', 'L0_ffn_Ws', 'L0_ffn_bs', 'L0_ffn_Wg', 'L0_ffn_Wu', 'L0_ffn_Wd', 'L1_attn_a_Wk',
        'L1_attn_a_Wv', 'L1_attn_a_Wq', 'L1_attn_a_Wbeta', 'L1_attn_a_Wout', 'L1_attn_b_Wq', 'L1_attn_b_Wk',
        'L1_attn_b_Wv', 'L1_attn_b_Wp', 'L1_attn_b_bp', 'L1_attn_b_rel_embed', 'L1_ffn_gate_w',
        'L1_ffn_down_w', 'L1_ffn_down_b', 'L1_ffn_up_w', 'L1_ffn_up_b']


def kernel(**inputs):
    import numpy as _np
    import concourse.bacc as _bacc
    from concourse import mybir as _mybir
    from concourse.bass_utils import run_bass_kernel_spmd as _run

    nc = _bacc.Bacc("TRN2", target_bir_lowering=False, num_devices=1)
    arrays, args = {}, []
    for name in _INS:
        a = _np.ascontiguousarray(inputs[name])
        arrays[f"in_{name}_dram"] = a
        args.append(nc.dram_tensor(f"in_{name}_dram", a.shape, _mybir.dt.from_np(a.dtype), kind="ExternalInput").ap())
    shape = arrays["in_L0_attn_a_x_dram"].shape
    args.append(nc.dram_tensor("out_0_dram", shape, _mybir.dt.float32, kind="ExternalOutput").ap())
    build(nc, *args)
    r = _run(nc, [arrays], core_ids=[0])
    return r.results[0]["out_0_dram"]
```

```python
from contextlib import ExitStack

import concourse.bass as bass
from concourse import mybir

F32 = mybir.dt.float32
BF16 = mybir.dt.bfloat16
ACT = mybir.ActivationFunctionType
ALU = mybir.AluOpType
AX = mybir.AxisListType

P = 128
T = 512
NT = T // P
H = 16
HD = P // H
DM = 64
NC2 = H * DM // P
E = 8
EPS = 1e-5
MASKED = -1e30

Q_PART = [0, 1, 2, 0, 1, 0]
K_PART = [0, 0, 0, 1, 1, 2]
SLOTS = len(Q_PART)
KROWS = SLOTS * HD

G4 = 4
NG = H // G4

BLOCKS = [(0, 0), (0, 1), (0, 2), (0, 3), (1, 1), (1, 2), (1, 3), (3, 3), (2, 2), (2, 3)]
SLOT = {b: n for n, b in enumerate(BLOCKS)}
COLS = len(BLOCKS) * P
JOBS = [[0], [1, 3], [2]]
JOB_AT = [0, 512, 1024]
JOB_N = [512, 512, 256]

LAYERS = ["attn_a", "moe_1", "attn_b", "moe_2", "lin_attn", "adapter_1", "rel_attn", "adapter_2"]


def build(nc, a_x, a_wq, a_wk, a_wv, a_wo, b_wattn, b_wout, m_ws, m_bs, m_wg, m_wu, m_wd,
          l_wk, l_wv, l_wq, l_wbeta, l_wout, r_wq, r_wk, r_wv, r_wp, r_bp, r_rel,
          d_gate, d_dw, d_db, d_uw, d_ub, out):
    B = a_x.shape[0]
    F = m_wg.shape[2]
    FT = [(j * P, min(P, F - j * P)) for j in range((F + P - 1) // P)]
    NF = len(FT)
    BN = d_dw.shape[1]
    KD = E * BN // P
    assert (a_x.shape[1], a_x.shape[2]) == (T, P) and r_rel.shape[0] == 2 * P and 2 * BN == P

    with ExitStack() as ctx:
        def sb(name, shape, dt=F32):
            return ctx.enter_context(nc.sbuf_tensor(name, shape, dt))

        def sem(name):
            return ctx.enter_context(nc.semaphore(name))

        ident = sb("ident", [P, P])
        identb = sb("identb", [P, P], BF16)
        mask_qk = sb("mask_qk", [P, P], BF16)
        mask_kq = sb("mask_kq", [P, P], BF16)
        keep_ge = sb("keep_ge", [P, P])
        ones = sb("ones", [P, P])
        half = sb("half", [P, 1])
        spread_q = sb("spread_q", [P, 3, H // 2, 2, 8, HD], BF16)
        spread_k = sb("spread_k", [P, 3, H // 2, 2, 8, HD], BF16)
        pick_max = sb("pick_max", [P, G4, P], BF16)
        head_of = sb("head_of", [P, H])
        pair_of = sb("pair_of", [P, 2])
        before = sb("before", [P, E, E])
        w_a = sb("w_a", [P, 4, P])
        w_b = sb("w_b", [P, 4, P])
        w_r = sb("w_r", [P, 4, P])
        relT = sb("relT", [P, 2, 3 * P], BF16)
        rel_res = sb("rel_res", [P, 2 * P])
        bp_row = sb("bp_row", [1, P])
        ws = sb("ws", [P, E])
        bs_row = sb("bs_row", [1, E])
        wg = sb("wg", [P, E, F])
        wu = sb("wu", [P, E, F])
        wd = sb("wd", [P, E, NF, P])
        wk_l = sb("wk_l", [P, H * DM])
        wv_l = sb("wv_l", [P, H * DM])
        wq_l = sb("wq_l", [P, H * DM])
        wbeta = sb("wbeta", [P, H])
        wout_l = sb("wout_l", [P, NC2, P])
        gateT = sb("gateT", [P, E])
        downT = sb("downT", [P, KD, P])
        upT = sb("upT", [P, KD, P])
        down_b = sb("down_b", [P, KD])
        up_b = sb("up_b", [E, P])
        x = sb("x", [P, NT, P])
        x_next = sb("x_next", [P, NT, P])
        stats = sb("stats", [P, NT, 6])
        moments = sb("moments", [P, NT, 2])
        rstd = sb("rstd", [P, NT])
        xn = sb("xn", [P, NT, P])
        xnT = sb("xnT", [P, T])
        values = sb("values", [P, NT, H, HD + 1])
        neg_maxT = sb("neg_maxT", [P, 2, T], BF16)
        WORK = 29800
        work = sb("work", [P, WORK])

        def part(at, shape, dt=F32):
            n = 1
            for d in shape:
                n *= d
            words = n if dt == F32 else (n + 1) // 2
            assert at + words <= WORK, (at + words, WORK)
            ap = work[:, at:at + words]
            if dt != F32:
                ap = ap.bitcast(dt)
            if len(shape) > 1:
                names = "abcd"[:len(shape)]
                ap = ap.rearrange("p (" + " ".join(names) + ") -> p " + " ".join(names),
                                  **dict(zip(names[1:], shape[1:])))
            return ap, at + words

        NSTAGE = 3 + 1 + 4 + 2 + KD + KD
        stage, at = part(0, [NSTAGE, P])
        stage_gate, at = part(at, [P])
        q_st, at = part(0, [H // 2, T], BF16)
        k_st, at = part(at, [H // 2, T], BF16)
        ring_at = at
        res, at = part(ring_at, [2, T])
        k_parts, at = part(at, [3, T], BF16)
        q_parts, at = part(ring_at + 3072, [3, T + 2], BF16)
        qk_part = lambda w, n: (q_parts[:, n, 1:T + 1], k_parts[:, n, :])[w]
        prob, at = part(at, [2, COLS])
        neg_max, at = part(at, [2, NT, G4])
        max_res, at = part(at, [2, NT, G4])
        max_part, at = part(at, [2, NT, 4 * G4], BF16)
        rden, at = part(at, [2, NT, G4])
        IC = 16
        q_masked0, _ = part(ring_at, [2, IC, NT * H], BF16)
        q_masked1, at = part(ring_at + 2 * T + 3 * T // 2, [2, IC, NT * H], BF16)
        q_masked = (q_masked0, q_masked1)
        assert at <= ring_at + 3072
        r_prob, _ = part(ring_at, [2, COLS])
        r_probT, at2 = part(ring_at + 2 * COLS, [2, COLS])
        sc, at = part(at2, [H, len(BLOCKS), P])
        r_neg_max, at = part(at, [2, NT])
        r_rden, at = part(at, [2, NT, G4])
        silu, at = part(0, [2, T])
        hidden, at = part(at, [2, NF, T])
        lg, at = part(at, [NT, E])
        gt, at = part(at, [NT, E, E])
        eq, at = part(at, [NT, E, E])
        rank, at = part(at, [NT, E])
        top, at = part(at, [NT])
        lgd, at = part(at, [NT, E])
        ex, at = part(at, [NT, E])
        mix, at = part(at, [NT, E])
        tot, at = part(at, [NT])
        l_qT, at = part(0, [NC2, T])
        l_kT, at = part(at, [NC2, T])
        l_k, at = part(at, [NT, H * DM])
        l_v, at = part(at, [NT, H * DM])
        l_vk, at = part(at, [NT, H * DM])
        l_sq, at = part(at, [2, T])
        l_sqk, at = part(at, [2, 512])
        l_wt, at = part(at, [2, 2, NT, P])
        l_st, at = part(at, [2, NT - 1, P])
        l_tmp, at = part(at, [2, NT, P])
        l_beta, at = part(at, [NT, H])
        l_ssum, at = part(at, [2, NT, H])
        l_rec, at = part(at, [2, NT, H])
        l_inv, at = part(at, [2, NT, H])
        pooled, at = part(0, [1])
        pool_rep, at = part(at, [P])
        d_hid, at = part(at, [KD, T])
        d_up, at = part(at, [KD, P])
        d_lg, at = part(at, [E])
        d_negm, at = part(at, [1])
        d_ex, at = part(at, [E])
        d_z, at = part(at, [1])
        d_gt, at = part(at, [E, E])
        d_eq, at = part(at, [E, E])
        d_rank, at = part(at, [E])
        d_w, at = part(at, [E])
        d_s, at = part(at, [1])
        d_w4, at = part(at, [KD])
        d_wT, at = part(at, [P])

        psum = ctx.enter_context(nc.psum_tensor("banks", [P, 8, 512], F32))

        def bank(n):
            return psum[:, n, :]

        loaded = sem("loaded")
        experts_in = sem("expert_weights_loaded")
        lin_in = sem("lin_weights_loaded")
        const = sem("constants")
        zeroed = sem("zeroed")
        stage_T = sem("stage_transposed")
        set_up = sem("vector_set_up")
        weights = sem("weights_ready")
        started = sem("turn_started")
        x_in = sem("x_loaded")
        x_out = sem("x_stored")
        x_free = sem("x_free")
        step = sem("vector_step")
        x_done = sem("layer_done")
        normed = sem("norm_stats")
        rstd_ok = sem("norm_rstd")
        xn_ok = sem("norm_rows")
        xn_T = sem("norm_transposed")
        xnT_ok = sem("norm_columns")
        a_proj = sem("attn_projected")
        a_hi = sem("attn_part_hi")
        a_res = sem("attn_part_rest")
        a_mid = sem("attn_part_mid")
        a_lo = sem("attn_part_lo")
        a_v = sem("attn_values")
        a_spread = sem("attn_spread")
        a_qst = sem("attn_q_stacked")
        a_kst = sem("attn_k_stacked_vec")
        a_ksa = sem("attn_k_stacked_act")
        a_s1 = sem("attn_scores_rows")
        a_max = sem("attn_row_max")
        a_mparts = sem("attn_max_parts")
        a_maxT = sem("attn_max_transposed")
        a_mrow = sem("attn_max_rows")
        a_s2 = sem("attn_scores_columns")
        a_prob = sem("attn_probabilities")
        a_pv = sem("attn_weighted_values")
        a_cols = sem("attn_group_columns")
        a_rows = sem("attn_group_rows")
        a_o = sem("attn_heads_out")
        a_oT = sem("attn_out_transposed")
        a_oTs = sem("attn_out_columns")
        a_y = sem("attn_out_projected")
        r_shift = sem("rel_q_shifted")
        r_qm = sem("rel_q_masked_vec")
        r_qmp = sem("rel_q_masked_pool")
        r_rel_ok = sem("rel_products")
        r_even = sem("rel_even_blocks")
        r_late = sem("rel_even_blocks_act")
        r_odd = sem("rel_odd_blocks")
        r_diag = sem("rel_diagonals")
        r_main = sem("rel_scores_qk")
        r_sum = sem("rel_scores_summed")
        r_sT = sem("rel_scores_transposed")
        r_max = sem("rel_row_max")
        r_p = sem("rel_probabilities")
        r_pT = sem("rel_prob_transposed")
        r_pTa = sem("rel_prob_columns_act")
        r_pTv = sem("rel_prob_columns_vec")
        m_logit = sem("moe_logits")
        m_lgd = sem("moe_logits_shifted")
        m_ex = sem("moe_exp")
        m_mix = sem("moe_mixed")
        m_g = sem("moe_gate_products")
        m_u = sem("moe_up_products")
        m_silu = sem("moe_silu")
        m_h = sem("moe_hidden")
        m_y = sem("moe_down_products")
        m_acc = sem("moe_added")
        l_bz = sem("lin_beta_logits")
        l_be = sem("lin_beta_exp")
        l_bok = sem("lin_beta")
        l_pq = sem("lin_qk_products")
        l_pn = sem("lin_kv_products")
        l_qk = sem("lin_qk_columns")
        l_kv = sem("lin_kv_rows")
        l_sqr = sem("lin_squares")
        l_ss = sem("lin_square_sums")
        l_sqks = sem("lin_key_squares")
        l_ssk = sem("lin_key_square_sums")
        l_ssc = sem("lin_square_sums_copied")
        l_norm = sem("lin_norms")
        l_invs = sem("lin_inverse_norms")
        l_vks = sem("lin_scaled_values")
        l_bv = sem("lin_beta_values")
        l_sc = sem("lin_scores")
        l_wts = sem("lin_masked_scores")
        l_zero = sem("lin_states_zeroed")
        l_stp = sem("lin_state_products")
        l_sts = sem("lin_state_parts")
        l_sums = sem("lin_states")
        l_o = sem("lin_out_products")
        l_ts = sem("lin_out_scaled")
        l_os = sem("lin_out_rows")
        l_oT = sem("lin_out_transposed")
        l_oTs = sem("lin_out_columns")
        l_y = sem("lin_out_projected")
        d_pool = sem("ad_pooled")
        d_gate_ok = sem("ad_gate_logits")
        d_lgs = sem("ad_logits_ready")
        d_exs = sem("ad_exp")
        d_dn = sem("ad_down_products")
        d_hs = sem("ad_hidden")
        d_ws = sem("ad_mix")
        d_ups = sem("ad_up_scaled")
        d_wTp = sem("ad_mix_transposed")
        d_wTs = sem("ad_mix_column")
        d_y = sem("ad_up_products")
        ended = sem("turn_ended")
        turn_sems = range(x_free.num, ended.num + 1)

        x_rows = a_x.rearrange("b (t p) d -> b p t d", p=P)
        out_rows = out.rearrange("b (t p) d -> b p t d", p=P)

        CONSTS = 6 + 2 * SLOTS + 3 + 4
        ROW_JOBS = [(3, 2, 0), (2, 3, 0), (0, 3, 3 * P), (1, 4, 0)]

        block = ctx.enter_context(nc.Block())

        loads = [
            (ws[:, :], m_ws), (bs_row[:, :], m_bs.rearrange("(a n) -> a n", a=1)),
            (w_a[:, 0, :], a_wq), (w_a[:, 1, :], a_wk), (w_a[:, 2, :], a_wv), (w_a[:, 3, :], a_wo),
            (stage[:, 0:3, :], b_wattn.rearrange("(j p) d -> p j d", p=P)),
            (stage[:, 3, :], b_wout), (stage[:, 4, :], r_wq), (stage[:, 5, :], r_wk),
            (stage[:, 6, :], r_wv), (stage[:, 7, :], r_wp),
            (stage[:, 8:10, :], r_rel.rearrange("(j p) d -> p j d", p=P)),
            (stage[:, 10:10 + KD, :], d_dw.rearrange("e c d -> (e c) d").rearrange("(j p) d -> p j d", p=P)),
            (stage[:, 10 + KD:10 + 2 * KD, :].rearrange("p j (e c) -> p (j e) c", e=2),
             d_uw.rearrange("e d c -> d e c")),
            (stage_gate[0:E, :], d_gate),
            (bp_row[:, :], r_bp.rearrange("(a n) -> a n", a=1)),
            (up_b[:, :], d_ub), (down_b[:, :], d_db.rearrange("e c -> (e c)").rearrange("(k p) -> p k", p=P)),
        ]
        expert_loads = [
            (wg[:, :, :], m_wg.rearrange("e d f -> d e f")), (wu[:, :, :], m_wu.rearrange("e d f -> d e f")),
        ] + [(wd[0:n, :, j, :], m_wd[:, f0:f0 + n, :].rearrange("e f d -> f e d")) for j, (f0, n) in enumerate(FT)]
        lin_loads = [
            (wk_l[:, :], l_wk), (wv_l[:, :], l_wv), (wq_l[:, :], l_wq), (wbeta[:, :], l_wbeta),
            (wout_l[:, :, :], l_wout.rearrange("(c p) d -> p c d", p=P)),
        ]

        @block.sync
        def _(sp):
            with nc.allow_non_contiguous_dma(reason="biases by partition"):
                for dst, src in loads:
                    sp.dma_start(dst, src).then_inc(loaded, 16)
            sp.dma_start(x_next[:, :, :], x_rows[0]).then_inc(x_in, 16)
            for dst, src in expert_loads:
                sp.dma_start(dst, src).then_inc(experts_in, 16)
            for dst, src in lin_loads:
                sp.dma_start(dst, src).then_inc(lin_in, 16)
            sp.nop().then_inc(x_free, 1)

            def turn(b, last):
                if not last:
                    sp.wait_ge(x_done, 2)
                    sp.dma_start(x_next[:, :, :], x_rows[b + 1]).then_inc(x_in, 16)
                sp.wait_ge(x_done, 16)
                sp.dma_start(out_rows[b], x[:, :, :]).then_inc(x_out, 16)
                sp.wait_ge(ended, 4)
                sp.sem_clear(turn_sems)
                sp.nop().then_inc(started, 1)
                sp.wait_ge(x_out, 16 * b + 16)
                if not last:
                    sp.nop().then_inc(x_free, 1)

            with sp.Fori(0, B - 1) as b:
                turn(b, False)
            turn(B - 1, True)

        def pool_norm(eng, n):
            for t in range(NT):
                eng.wait_ge(normed, 12 * n + (5, 8, 11, 12)[t])
                eng.tensor_tensor(rstd[:, t:t + 1], rstd[:, t:t + 1], half[:, 0:1],
                                  ALU.pow).then_inc(rstd_ok, 1)

        def mask_q(eng, c, n):
            src = q_parts[:, n, 0:T].rearrange("p (t i) -> p i t", t=NT)[:, IC * c:IC * c + IC, :]
            return eng.tensor_tensor(q_masked[c % 2][:, n, :, :].rearrange("p i (t h) -> p i t h", t=NT),
                                     src.unsqueeze(3).to_broadcast([P, IC, NT, H]),
                                     head_of[:, :].unsqueeze(1).unsqueeze(1).to_broadcast([P, IC, NT, H]),
                                     ALU.mult)

        def pool_rel(eng):
            def mask(c):
                if c % 2 == 0:
                    return
                if c == 1:
                    eng.wait_ge(r_shift, 1)
                    eng.wait_ge(a_lo, 6)
                else:
                    eng.wait_ge(r_rel_ok, 2 * (IC // 8) * (c - 1))
                mask_q(eng, c, 1).then_inc(r_qmp, 1)

            mask(1)
            for c in range(P // IC):
                if c + 2 < P // IC:
                    mask(c + 2)
                eng.wait_ge(r_even, IC // 8 * (c + 1))
                for b in (0, 4, 7, 8):
                    v = sc[:, :, b, IC * c:IC * c + IC]
                    eng.affine_select(out=v, in_=v, compare_op=ALU.is_gt, fill=0.0, base=IC * c,
                                      pattern=[[0, H], [1, IC]],
                                      channel_multiplier=-1).then_inc(r_diag, 1)

        def pool_lin(eng):
            eng.wait_ge(xnT_ok, 5)
            eng.memset(l_st[:, :, :, :], 0.0).then_inc(l_zero, 1)
            for i in range(NC2):
                t, c = i // 2, i % 2
                eng.wait_ge(l_kv, i + 1)
                if i >= 2:
                    eng.wait_ge(l_ssk, i - 1)
                k = l_k[:, t, 512 * c:512 * c + 512]
                eng.tensor_tensor(l_sqk[:, i % 2, :], k, k, ALU.mult).then_inc(l_sqks, 1)
            eng.wait_ge(l_bok, 1)
            for c in range(NC2 + 2):
                if c < NC2:
                    eng.wait_ge(l_vks, c + 1)
                    v = l_v[:, :, P * c:P * c + P].rearrange("p t (r d) -> p t r d", r=2)
                    eng.tensor_tensor(v, v, l_beta[:, :, 2 * c:2 * c + 2].unsqueeze(3)
                                      .to_broadcast([P, NT, 2, DM]), ALU.mult).then_inc(l_bv, 1)
                if c >= 2:
                    eng.wait_ge(l_ts, c - 1)
                    eng.wait_ge(l_bv, c - 1)
                    v = l_v[:, :, P * (c - 2):P * (c - 1)]
                    eng.tensor_tensor(v, v, l_tmp[:, c % 2, :, :], ALU.add).then_inc(l_os, 1)

        @block.gpsimd
        def _(eng):
            zeros = [ident, identb, mask_qk, mask_kq, spread_q, spread_k, pick_max, neg_maxT]
            for z in zeros:
                eng.memset(z[...], 0.0).then_inc(zeroed, 1)
            for o in (keep_ge, head_of, pair_of, before, ones):
                eng.memset(o[...], 1.0).then_inc(zeroed, 1)
            eng.memset(half[:, :], -0.5).then_inc(zeroed, 1)
            eng.memset(values[:, :, :, HD:HD + 1], 1.0).then_inc(zeroed, 1)
            eng.wait_ge(zeroed, len(zeros) + 7)
            for m in (ident, identb):
                eng.affine_select(out=m[:, :], in_=m[:, :], compare_op=ALU.not_equal, fill=1.0, base=0,
                                  pattern=[[-1, P]], channel_multiplier=1).then_inc(const, 1)
            eng.affine_select(out=mask_qk[:, :], in_=mask_qk[:, :], compare_op=ALU.is_ge, fill=MASKED, base=0,
                              pattern=[[-1, P]], channel_multiplier=1).then_inc(const, 1)
            eng.affine_select(out=mask_kq[:, :], in_=mask_kq[:, :], compare_op=ALU.is_ge, fill=MASKED, base=0,
                              pattern=[[1, P]], channel_multiplier=-1).then_inc(const, 1)
            eng.affine_select(out=keep_ge[:, :], in_=keep_ge[:, :], compare_op=ALU.is_ge, fill=0.0, base=0,
                              pattern=[[-1, P]], channel_multiplier=1).then_inc(const, 1)
            eng.affine_select(out=before[:, :, :], in_=before[:, :, :], compare_op=ALU.is_gt, fill=0.0, base=0,
                              pattern=[[1, E], [-1, E]], channel_multiplier=0).then_inc(const, 1)
            n_const = 6
            for spread, of_slot in ((spread_q, Q_PART), (spread_k, K_PART)):
                for slot, x_part in enumerate(of_slot):
                    v = spread[:, x_part, :, :, slot, :]
                    eng.affine_select(out=v, in_=v, compare_op=ALU.not_equal, fill=1.0, base=0,
                                      pattern=[[-16, H // 2], [-8, 2], [-1, HD]],
                                      channel_multiplier=1).then_inc(const, 1)
                    n_const += 1
            for p3 in range(3):
                eng.wait_ge(const, n_const)
                eng.affine_select(out=pick_max[:, :, :], in_=pick_max[:, :, :], compare_op=ALU.not_equal,
                                  fill=1.0, base=-G4 * p3, pattern=[[-1, G4], [0, P]],
                                  channel_multiplier=1).then_inc(const, 1)
                n_const += 1
            for tab, n, width in ((head_of, H, HD), (pair_of, 2, DM)):
                eng.affine_select(out=tab[:, :], in_=tab[:, :], compare_op=ALU.is_ge, fill=0.0, base=0,
                                  pattern=[[-width, n]], channel_multiplier=1).then_inc(const, 1)
                n_const += 1
                eng.wait_ge(const, n_const)
                eng.affine_select(out=tab[:, :], in_=tab[:, :], compare_op=ALU.is_gt, fill=0.0, base=width,
                                  pattern=[[width, n]], channel_multiplier=-1).then_inc(const, 1)
                n_const += 1
            assert n_const == CONSTS
            with eng.Fori(0, B) as b:
                pool_norm(eng, 0)
                pool_norm(eng, 1)
                pool_norm(eng, 2)
                pool_norm(eng, 3)
                pool_norm(eng, 4)
                pool_lin(eng)
                pool_norm(eng, 5)
                pool_norm(eng, 6)
                pool_rel(eng)
                pool_norm(eng, 7)
                eng.nop().then_inc(ended, 1)
                eng.wait_ge(started, b + 1)

        def spread_job(w, at):
            return 4 * (at // 2) + 2 * w + at % 2

        def wait_stacked(eng, n, w, at):
            if w == 0:
                eng.wait_ge(a_qst, H // 2 * n + at + 1)
            elif at < 2:
                eng.wait_ge(a_kst, 2 * n + at + 1)
            else:
                eng.wait_ge(a_ksa, (H // 2 - 2) * n + at - 1)

        def spread_bank(n, i):
            return (4 if n == 2 else 3) + i % 4

        def act_norm(eng, n):
            half_T = T // 2
            for i in range(2):
                eng.wait_ge(xn_T, 2 * n + i + 1)
                cols = slice(half_T * i, half_T * i + half_T)
                m = eng.activation(xnT[:, cols], bank(6 + i)[:, cols], ACT.Copy)
            m.then_inc(xnT_ok, 1)

        def act_parts(eng, n, scale):
            eng.wait_ge(a_proj, 3 * n + 1)
            eng.activation(qk_part(0, 0), bank(0), ACT.Copy, scale=scale).then_inc(a_hi, 1)
            eng.wait_ge(a_proj, 3 * n + 2)
            eng.activation(qk_part(1, 0), bank(1), ACT.Copy).then_inc(a_hi, 1)
            for w in range(2):
                eng.wait_ge(a_res, 2 * n + w + 1)
                eng.activation(qk_part(w, 1), res[:, w, :], ACT.Copy).then_inc(a_mid, 1)

        def act_stack(eng, n, w, at):
            i = spread_job(w, at)
            eng.wait_ge(a_spread, H * n + i + 1)
            eng.activation((q_st, k_st)[w][:, at, :], bank(spread_bank(n, i)),
                           ACT.Copy).then_inc((a_qst, a_ksa)[w], 1)

        def group_columns(eng, n, G, bk):
            eng.wait_ge(a_pv, H * n + G4 * (G + 1))
            if G >= 1:
                eng.wait_ge(a_rows, NG * n + G)
            eng.activation(xnT[:, :], bank(bk), ACT.Copy).then_inc(a_cols, 1)

        def act_attn(eng, n, scale):
            act_parts(eng, n, scale)
            for at in range(0, H // 2, 2):
                act_stack(eng, n, 0, at)
                act_stack(eng, n, 0, at + 1)
                if at >= 2:
                    act_stack(eng, n, 1, at)
                    act_stack(eng, n, 1, at + 1)

            def max_rows(G):
                eng.wait_ge(a_maxT, NG * n + G + 1)
                if G >= 2:
                    eng.wait_ge(a_s2, 3 * (H * n + G4 * (G - 1)))
                eng.activation(neg_maxT[0:3 * G4, G % 2, :], bank(6 + G % 2)[0:3 * G4, 0:T // 2].bitcast(BF16),
                               ACT.Copy).then_inc(a_mrow, 1)

            max_rows(0)
            for h in range(H):
                if h >= 2:
                    eng.wait_ge(a_pv, H * n + h - 1)
                for j in range(3):
                    if j == 0 and h % G4 == G4 - 1 and h < H - 1:
                        max_rows(h // G4 + 1)
                    eng.wait_ge(a_s2, 3 * (H * n + h) + j + 1)
                    eng.activation(prob[:, h % 2, JOB_AT[j]:JOB_AT[j] + JOB_N[j]],
                                   bank(3 + j)[:, 0:JOB_N[j]], ACT.Exp).then_inc(a_prob, 1)
                if h % G4 == 0 and h > 0:
                    group_columns(eng, n, h // G4 - 1, 6 + (h // G4 - 1) % 2)
            group_columns(eng, n, NG - 1, 6 + (NG - 1) % 2)
            eng.wait_ge(a_oT, n + 1)
            eng.activation(xnT[:, :], bank(0), ACT.Copy).then_inc(a_oTs, 1)

        def act_moe(eng, n):
            eng.wait_ge(m_lgd, n + 1)
            eng.activation(ex[:, :, :], lgd[:, :, :], ACT.Exp).then_inc(m_ex, 1)
            for i in range(E * NF):
                w = FT[i % NF][1]
                eng.wait_ge(m_g, E * NF * n + i + 1)
                if i >= 2:
                    eng.wait_ge(m_h, E * NF * n + i - 1)
                eng.activation(silu[0:w, i % 2, :], bank(i % 2)[0:w, :], ACT.Silu).then_inc(m_silu, 1)

        def act_lin(eng):
            eng.wait_ge(l_bz, 1)
            eng.activation(l_beta[:, :, :], bank(6)[:, 0:NT * H].rearrange("p (t h) -> p t h", t=NT),
                           ACT.Exp, scale=-1.0).then_inc(l_be, 1)
            for i in range(2 * NC2):
                dst = (l_qT, l_kT)[i % 2][:, i // 2, :]
                eng.wait_ge(l_pq, i + 1)
                eng.activation(dst, bank(i % 2), ACT.Copy).then_inc(l_qk, 1)
                if i % 2 == 0:
                    eng.wait_ge(l_qk, i + 1)
                    if i >= 4:
                        eng.wait_ge(l_ss, i // 2 - 1)
                    eng.activation(l_sq[:, i // 2 % 2, :], dst, ACT.Square).then_inc(l_sqr, 1)
            eng.wait_ge(l_ssc, 1)
            eng.activation(l_inv[:, :, :, :], l_ssum[:, :, :, :], ACT.Sqrt).then_inc(l_norm, 1)

            def columns(c):
                eng.wait_ge(l_oT, c + 1)
                eng.activation(l_kT[:, c, :], bank(6 + c % 2), ACT.Copy).then_inc(l_oTs, 1)

            for c in range(NC2):
                eng.wait_ge(l_stp, c + 1)
                if c >= 2:
                    eng.wait_ge(l_o, c - 1)
                else:
                    eng.wait_ge(l_zero, 1)
                for r in range(2):
                    own = slice(DM * r, DM * r + DM)
                    i = eng.activation(l_st[own, c % 2, :, own],
                                       bank(2 + c % 2)[own, 0:(NT - 1) * P].rearrange("p (u d) -> p u d", d=P)[:, :, own],
                                       ACT.Copy)
                i.then_inc(l_sts, 1)
                if c >= 2:
                    columns(c - 2)
            columns(NC2 - 2)
            columns(NC2 - 1)

        def act_adapter(eng, n):
            eng.wait_ge(d_lgs, n + 1)
            eng.activation(d_ex[:, :], d_lg[:, :], ACT.Exp, bias=d_negm[:, 0:1],
                           accum_out=d_z[:, 0:1]).then_inc(d_exs, 1)
            for k in range(KD):
                eng.wait_ge(d_dn, KD * n + k + 1)
                eng.activation(d_hid[:, k, :], bank(k), ACT.Gelu, bias=down_b[:, k:k + 1]).then_inc(d_hs, 1)
            eng.wait_ge(d_wTp, n + 1)
            eng.activation(d_wT[0:E, :], bank(5)[0:E, 0:P], ACT.Copy).then_inc(d_wTs, 1)

        def act_rel(eng):
            act_parts(eng, 2, float(HD) ** -0.5)
            act_stack(eng, 2, 0, 0)
            act_stack(eng, 2, 0, 1)
            for i in range(P // 8):
                q8 = slice(8 * i, 8 * i + 8)
                eng.wait_ge(r_rel_ok, 2 * i + 2)
                v = bank((2 * i + 1) % 4).rearrange("p (i t h) -> p h t i", i=8, t=NT)
                eng.activation(sc[:, :, 1:10:4, q8], v[:, :, 1:4, :], ACT.Copy)
                eng.activation(sc[:, :, 3, q8], v[:, :, 3, :], ACT.Copy).then_inc(r_odd, 1)
                eng.wait_ge(r_even, i + 1)
                v = bank((2 * i) % 4).rearrange("p (i t h) -> p h t i", i=8, t=NT)
                eng.activation(sc[:, :, 2:7:4, q8], v[:, :, 2:4, :], ACT.Copy).then_inc(r_late, 1)
                if i % 4 == 2 and i // 2 + 1 < H // 2:
                    act_stack(eng, 2, 0, i // 2 + 1)
                    act_stack(eng, 2, 0, i // 2 + 2)
                if i % 4 == 0 and i > 0:
                    act_stack(eng, 2, 1, i // 2)
                    act_stack(eng, 2, 1, i // 2 + 1)

            def exps(h):
                at = {0: 0, 1: P, 2: 3 * P, 3: 6 * P}
                if h >= 2:
                    eng.wait_ge(r_pT, 3 * (h - 1))
                for n, (t, bk, col) in enumerate(ROW_JOBS):
                    eng.wait_ge(r_max, 4 * h + (3 if n == 1 else n + 1))
                    eng.activation(r_prob[:, h % 2, at[t]:at[t] + (t + 1) * P],
                                   bank(bk)[:, col:col + (t + 1) * P], ACT.Exp,
                                   bias=r_neg_max[:, h % 2, t:t + 1]).then_inc(r_p, 1)

            def columns(h):
                for j in range(2):
                    eng.wait_ge(r_pT, 3 * h + j + 1)
                    if h >= 2:
                        eng.wait_ge(a_pv, 2 * H + h - 1)
                    eng.activation(r_probT[:, h % 2, JOB_AT[j]:JOB_AT[j] + JOB_N[j]],
                                   bank(5 + (3 * h + j) % 2)[:, 0:JOB_N[j]], ACT.Copy).then_inc(r_pTa, 1)

            for i in range(1, H + 3):
                if i - 3 >= G4 and (i - 3) % G4 == 0:
                    group_columns(eng, 2, (i - 3) // G4 - 1, 7)
                if 2 <= i <= H + 1:
                    columns(i - 2)
                if i <= H:
                    exps(i - 1)
            group_columns(eng, 2, NG - 1, 7)
            eng.wait_ge(a_oT, 3)
            eng.activation(xnT[:, :], bank(0), ACT.Copy).then_inc(a_oTs, 1)

        @block.scalar
        def _(eng):
            eng.wait_ge(weights, 6)
            with eng.Fori(0, B) as b:
                act_norm(eng, 0)
                act_attn(eng, 0, float(HD) ** -0.5)
                act_norm(eng, 1)
                act_moe(eng, 0)
                act_norm(eng, 2)
                act_attn(eng, 1, float(P) ** -0.5)
                act_norm(eng, 3)
                act_moe(eng, 1)
                act_norm(eng, 4)
                act_lin(eng)
                act_norm(eng, 5)
                act_adapter(eng, 0)
                act_norm(eng, 6)
                act_rel(eng)
                act_norm(eng, 7)
                act_adapter(eng, 1)
                eng.nop().then_inc(ended, 1)
                eng.wait_ge(started, b + 1)

        def pe_norm(eng, n):
            for t in range(NT):
                eng.wait_ge(xn_ok, 4 * n + t + 1)
                m = eng.transpose(bank(6 + t // 2)[:, P * t:P * t + P], xn[:, t, :], ident[:, :])
                if t % 2 == 1:
                    m.then_inc(xn_T, 1)

        def pe_project(eng, n, w):
            eng.wait_ge(xnT_ok, (0, 2, 6)[n] + 1)
            eng.matmul(bank(0), w[:, 0, :], xnT[:, :], start=True, stop=True).then_inc(a_proj, 1)
            eng.matmul(bank(1), w[:, 1, :], xnT[:, :], start=True, stop=True).then_inc(a_proj, 1)
            for t in range(NT):
                m = eng.matmul(bank(2)[:, P * t:P * t + P], xnT[:, P * t:P * t + P], w[:, 2, :],
                               start=True, stop=True)
            m.then_inc(a_proj, 1)

        def pe_spread(eng, n, step):
            w2 = step % 2
            places = [2 * (step // 2), 2 * (step // 2) + 1]
            if step >= 2:
                wait_stacked(eng, n, w2, places[1] - 2)
            for x_part in range(3):
                if step < 2:
                    eng.wait_ge((a_hi, a_mid, a_lo)[x_part], 2 * n + w2 + 1)
                for at in places:
                    spread = (spread_q, spread_k)[w2][:, x_part, at].rearrange("p r s d -> p (r s d)")
                    m = eng.matmul(bank(spread_bank(n, spread_job(w2, at))), spread,
                                   qk_part(w2, x_part), start=(x_part == 0), stop=(x_part == 2))
                    if x_part == 2:
                        m.then_inc(a_spread, 1)

        def weigh_columns(eng, bk, h, p_cols):
            row = 32 * (h % G4)
            for s in range(NT):
                at = P * SLOT[(s, s)]
                m = eng.matmul(bank(bk)[row:row + HD + 1, P * s:T], values[:, s, h, :],
                               p_cols[:, h % 2, at:at + T - P * s], start=(s == 0), stop=(s == NT - 1))
            m.then_inc(a_pv, 1)

        def group_rows(eng, n, G, bk):
            eng.wait_ge(a_cols, NG * n + G + 1)
            for t in range(NT):
                m = eng.transpose(bank(bk)[:, P * t:P * t + P], xnT[:, P * t:P * t + P], ident[:, :])
            m.then_inc(a_rows, 1)

        def pe_out(eng, n, w, bias):
            eng.wait_ge(a_o, NG * (n + 1))
            for t in range(NT):
                m = eng.transpose(bank(0)[:, P * t:P * t + P], xn[:, t, :], ident[:, :])
            m.then_inc(a_oT, 1)
            eng.wait_ge(a_oTs, n + 1)
            for t in range(NT):
                o = bank(1 + t // 2)[:, P * (t % 2):P * (t % 2) + P]
                m = eng.matmul(o, xnT[:, P * t:P * t + P], w[:, 3, :], start=True, stop=bias is None)
                if bias is not None:
                    m = eng.matmul(o, ones[0:1, 0:P], bias, start=False, stop=True)
                if t % 2 == 1:
                    m.then_inc(a_y, 1)

        def rows_of(G):
            return ([[(hh, 3, 0)] for hh in range(G4)] + [[(hh, 2, 0)] for hh in range(G4)] +
                    [[(r, t, 0), (r + 2, t, (t + 1) * P)] for t in (1, 0) for r in range(2)])

        NROW = len(rows_of(0))
        AHEAD = 7

        def stacked(st, h, cols):
            r = h % 2
            return st[64 * r:64 * r + KROWS, h // 2, cols]

        def pe_attn(eng, n, w):
            pe_project(eng, n, w)

            def score_rows(G, jobs):
                for i in jobs:
                    k = NROW * G + i
                    if k == 2:
                        eng.wait_ge(a_v, n + 1)
                    if k >= 3:
                        eng.wait_ge(a_max, NROW * NG * n + k - 2)
                    for hh, t, col in rows_of(G)[i]:
                        h, N = G4 * G + hh, (t + 1) * P
                        for w2 in range(2):
                            wait_stacked(eng, n, w2, h // 2)
                        eng.matmul(bank(k % 3)[:, col:col + N], stacked(q_st, h, slice(P * t, P * t + P)),
                                   stacked(k_st, h, slice(0, N)), start=True, stop=False)
                        m = eng.matmul(bank(k % 3)[:, col + N - P:col + N], identb[:, :], mask_qk[:, :],
                                       start=False, stop=True)
                    m.then_inc(a_s1, 1)

            def max_columns(G):
                eng.wait_ge(a_mparts, NG * n + G + 1)
                if G == 0:
                    wait_stacked(eng, n, 1, H // 2 - 1)
                if G >= 2:
                    eng.wait_ge(a_o, NG * n + G - 1)
                for t in range(NT):
                    m = eng.transpose(bank(6 + G % 2)[0:3 * G4, P // 2 * t:P // 2 * (t + 1)].bitcast(BF16),
                                      max_part[:, G % 2, t, 0:3 * G4], identb[:, :])
                m.then_inc(a_maxT, 1)

            def score_columns(h):
                G, hh = h // G4, h % G4
                if hh == 0:
                    eng.wait_ge(a_mrow, NG * n + G + 1)
                for j in range(3):
                    if h >= 1:
                        eng.wait_ge(a_prob, 3 * (H * n + h - 1) + j + 1)
                    col = 0
                    for s in JOBS[j]:
                        N = T - P * s
                        eng.matmul(bank(3 + j)[:, col:col + N], stacked(k_st, h, slice(P * s, P * s + P)),
                                   stacked(q_st, h, slice(P * s, T)), start=True, stop=False)
                        eng.matmul(bank(3 + j)[:, col:col + P], identb[:, :], mask_kq[:, :],
                                   start=False, stop=False)
                        m = eng.matmul(bank(3 + j)[:, col:col + N], pick_max[:, hh, :],
                                       neg_maxT[:, G % 2, P * s:T], start=False, stop=True)
                        col += N
                    m.then_inc(a_s2, 1)

            def weigh(h):
                G, hh = h // G4, h % G4
                eng.wait_ge(a_prob, 3 * (H * n + h + 1))
                weigh_columns(eng, 6 + G % 2, h, prob)

            for step in range(H // 2):
                pe_spread(eng, n, step)
                if step >= 2:
                    score_rows(0, range(2 * (step - 2), 2 * (step - 1)))
            score_rows(1, range(0, 3))
            max_columns(0)
            score_rows(1, range(3, AHEAD))
            for h in range(H):
                G = h // G4
                score_columns(h)
                if h % G4 == 0 and G + 1 < NG:
                    score_rows(G + 1, range(AHEAD, NROW))
                if h % G4 == 1 and G >= 1:
                    group_rows(eng, n, G - 1, 6 + (G - 1) % 2)
                if h % G4 >= 2 and G + 2 < NG:
                    score_rows(G + 2, (range(0, 3), range(3, AHEAD))[h % G4 - 2])
                if h % G4 == 2 and G + 1 < NG:
                    max_columns(G + 1)
                if h >= 1:
                    weigh(h - 1)
            weigh(H - 1)
            group_rows(eng, n, NG - 1, 6 + (NG - 1) % 2)
            pe_out(eng, n, w, None)

        def pe_moe(eng, n):
            eng.wait_ge(experts_in, 16 * len(expert_loads))
            eng.wait_ge(xnT_ok, 2 * n + 2)
            for t in range(NT):
                eng.matmul(bank(6)[:, E * t:E * t + E], xnT[:, P * t:P * t + P], ws[:, :], start=True, stop=False)
                m = eng.matmul(bank(6)[:, E * t:E * t + E], ones[0:1, 0:P], bs_row[:, :], start=False, stop=True)
            m.then_inc(m_logit, 1)

            def down(e):
                eng.wait_ge(m_h, NF * (E * n + e + 1))
                if e >= 2:
                    eng.wait_ge(m_acc, E * n + e - 1)
                for t in range(NT):
                    for j, (_, w) in enumerate(FT):
                        m = eng.matmul(bank(4 + e % 2)[:, P * t:P * t + P],
                                       hidden[0:w, e % 2, j, P * t:P * t + P], wd[0:w, e, j, :],
                                       start=(j == 0), stop=(j == NF - 1))
                m.then_inc(m_y, 1)

            for e in range(E):
                for j, (f0, w) in enumerate(FT):
                    i = NF * e + j
                    if i >= 2:
                        eng.wait_ge(m_silu, E * NF * n + i - 1)
                    eng.matmul(bank(i % 2)[0:w, :], wg[:, e, f0:f0 + w], xnT[:, :],
                               start=True, stop=True).then_inc(m_g, 1)
                    if i >= 2:
                        eng.wait_ge(m_h, E * NF * n + i - 1)
                    eng.matmul(bank(2 + i % 2)[0:w, :], wu[:, e, f0:f0 + w], xnT[:, :],
                               start=True, stop=True).then_inc(m_u, 1)
                if e >= 1:
                    down(e - 1)
            down(E - 1)

        def pe_lin(eng):
            eng.wait_ge(lin_in, 16 * len(lin_loads))
            eng.wait_ge(xnT_ok, 5)
            for t in range(NT):
                m = eng.matmul(bank(6)[:, H * t:H * t + H], xnT[:, P * t:P * t + P], wbeta[:, :],
                               start=True, stop=True)
            m.then_inc(l_bz, 1)

            def sum_squares(i):
                eng.wait_ge(l_sqr, i + 1)
                for t in range(NT):
                    at = H * t + 2 * i
                    m = eng.matmul(bank(5)[:, at:at + 2], l_sq[:, i % 2, P * t:P * t + P], pair_of[:, :],
                                   start=True, stop=True)
                m.then_inc(l_ss, 1)

            for i in range(2 * NC2):
                if i >= 2:
                    eng.wait_ge(l_qk, i - 1)
                eng.matmul(bank(i % 2), (wq_l, wk_l)[i % 2][:, P * (i // 2):P * (i // 2) + P], xnT[:, :],
                           start=True, stop=True).then_inc(l_pq, 1)
                if i >= 2:
                    eng.wait_ge(l_kv, i - 1)
                t, c = (i % 8) // 2, i % 2
                eng.matmul(bank(2 + i % 2), xnT[:, P * t:P * t + P],
                           (wk_l, wv_l)[i // 8][:, 512 * c:512 * c + 512], start=True, stop=True).then_inc(l_pn, 1)
                if i % 2 == 1:
                    sum_squares(i // 2)

            def scores(c):
                for r in range(2):
                    h = 2 * c + r
                    if h >= 2:
                        eng.wait_ge(l_wts, h - 1)
                    else:
                        eng.wait_ge(l_qk, 2 * NC2)
                    for t in range(NT):
                        m = eng.matmul(bank(r)[:, P * t:P * t + P], l_kT[64 * r:64 * r + 64, c, P * t:P * t + P],
                                       l_qT[64 * r:64 * r + 64, c, P * t:P * t + P], start=True, stop=True)
                    m.then_inc(l_sc, 1)

            def states(c):
                eng.wait_ge(l_vks, c + 1)
                if c >= 2:
                    eng.wait_ge(l_sts, c - 1)
                else:
                    eng.wait_ge(l_kv, 2 * NC2)
                for u in range(NT - 1):
                    m = eng.matmul(bank(2 + c % 2)[:, P * u:P * u + P], l_k[:, u + 1, P * c:P * c + P],
                                   l_vk[:, u + 1, P * c:P * c + P], start=True, stop=True)
                m.then_inc(l_stp, 1)

            def outputs(c):
                eng.wait_ge(l_wts, 2 * c + 2)
                eng.wait_ge(l_sums, c + 1)
                if c >= 2:
                    eng.wait_ge(l_ts, c - 1)
                else:
                    eng.wait_ge(l_ssc, 1)
                for t in range(NT):
                    o = bank(4 + c % 2)[:, P * t:P * t + P]
                    for r in range(2):
                        m = eng.matmul(o[:, DM * r:DM * r + DM], l_wt[:, c % 2, r, t, :],
                                       l_vk[:, t, P * c + DM * r:P * c + DM * r + DM],
                                       start=(r == 0), stop=(t == NT - 1 and r == 1), skip_group_check=True)
                    if t < NT - 1:
                        m = eng.matmul(o, l_qT[:, c, P * t:P * t + P], l_st[:, c % 2, t, :],
                                       start=False, stop=True, skip_group_check=True)
                m.then_inc(l_o, 1)

            def transposes(c):
                eng.wait_ge(l_os, c + 1)
                if c >= 2:
                    eng.wait_ge(l_oTs, c - 1)
                for t in range(NT):
                    m = eng.transpose(bank(6 + c % 2)[:, P * t:P * t + P], l_v[:, t, P * c:P * c + P], ident[:, :])
                m.then_inc(l_oT, 1)

            for c in range(NC2 + 3):
                if c < NC2:
                    scores(c)
                    states(c)
                if 1 <= c <= NC2:
                    outputs(c - 1)
                if c >= 3:
                    transposes(c - 3)
            eng.wait_ge(l_oTs, NC2)
            for t in range(NT):
                for c in range(NC2):
                    m = eng.matmul(bank(t // 2)[:, P * (t % 2):P * (t % 2) + P], l_kT[:, c, P * t:P * t + P],
                                   wout_l[:, c, :], start=(c == 0), stop=(c == NC2 - 1))
                if t % 2 == 1:
                    m.then_inc(l_y, 1)

        def pe_adapter(eng, n):
            eng.wait_ge(xnT_ok, (6, 8)[n])
            for k in range(KD):
                eng.matmul(bank(k), downT[:, k, :], xnT[:, :], start=True, stop=True).then_inc(d_dn, 1)
                if k == 0:
                    eng.wait_ge(d_pool, n + 1)
                    eng.matmul(bank(6)[:, 0:E], pool_rep[:, :], gateT[:, :], start=True,
                               stop=True).then_inc(d_gate_ok, 1)
            eng.wait_ge(d_ws, n + 1)
            eng.transpose(bank(5)[0:E, 0:P], d_w[:, :], ident[:, :]).then_inc(d_wTp, 1)
            eng.wait_ge(d_wTs, n + 1)
            eng.wait_ge(d_hs, KD * (n + 1))
            eng.wait_ge(d_ups, n + 1)
            for t in range(NT):
                o = bank(4 + t // 2)[:, P * (t % 2):P * (t % 2) + P]
                for k in range(KD):
                    eng.matmul(o, d_hid[:, k, P * t:P * t + P], d_up[:, k, :], start=(k == 0), stop=False)
                m = eng.matmul(o, d_wT[0:E, :], up_b[:, :], start=False, stop=True)
                if t % 2 == 1:
                    m.then_inc(d_y, 1)

        def pe_rel(eng, w):
            pe_project(eng, 2, w)
            eng.wait_ge(a_res, 6)
            eng.wait_ge(a_v, 3)
            pe_spread(eng, 2, 0)
            pe_spread(eng, 2, 1)
            for i in range(P // 8):
                for par in range(2):
                    k = 2 * i + par
                    if i >= 2:
                        eng.wait_ge((r_even, r_odd)[par], i - 1)
                    if i >= 2 and par == 0:
                        eng.wait_ge(r_late, i - 1)
                    c = 8 * i // IC
                    eng.wait_ge(r_qm, c + 1 + c // 2 + 1)
                    if c >= 1:
                        eng.wait_ge(r_qmp, (c + 1) // 2)
                    for q in range(8 * i, 8 * i + 8):
                        first = (P * par - q) % (2 * P)
                        for n, (rp, qp) in enumerate([(0, 0), (0, 1), (1, 0)]):
                            m = eng.matmul(bank(k % 4)[:, 64 * (q % 8):64 * (q % 8) + 64],
                                           relT[:, rp, first:first + P], q_masked[c % 2][:, qp, q % IC, :],
                                           start=(n == 0), stop=(n == 2))
                    m.then_inc(r_rel_ok, 1)
                if i % 2 == 1 and i // 2 + 2 < H // 2:
                    pe_spread(eng, 2, i // 2 + 2)

            def qk(h, j):
                k = 3 * h + j
                if k >= 2:
                    eng.wait_ge(r_sum, k - 1)
                else:
                    eng.wait_ge(r_even, P // 8)
                    eng.wait_ge(r_late, P // 8)
                    eng.wait_ge(r_odd, P // 8)
                    wait_stacked(eng, 2, 0, H // 2 - 1)
                    wait_stacked(eng, 2, 1, H // 2 - 1)
                col = 0
                for s in JOBS[j]:
                    N = T - P * s
                    eng.matmul(bank(k % 2)[:, col:col + N], stacked(k_st, h, slice(P * s, P * s + P)),
                               stacked(q_st, h, slice(P * s, T)), start=True, stop=False)
                    m = eng.matmul(bank(k % 2)[:, col:col + P], identb[:, :], mask_kq[:, :],
                                   start=False, stop=True)
                    col += N
                m.then_inc(r_main, 1)

            def rows(h):
                eng.wait_ge(r_sum, 3 * (h + 1))
                for i, (t, bk, col) in enumerate(ROW_JOBS):
                    if h >= 1 and i != 2:
                        eng.wait_ge(r_p, 4 * (h - 1) + (1, 3, 3, 4)[i])
                    for s in range(t + 1):
                        m = eng.transpose(bank(bk)[:, col + P * s:col + P * s + P], sc[:, h, SLOT[(s, t)], :],
                                          ident[:, :])
                    if i != 1:
                        m.then_inc(r_sT, 1)

            def columns(h, j):
                at = {0: 0, 1: P, 2: 3 * P, 3: 6 * P}
                k = 3 * h + j
                if j == 0:
                    eng.wait_ge(r_p, 4 * (h + 1))
                    if h >= G4 + 2 and h % G4 == 2:
                        eng.wait_ge(a_o, 2 * NG + h // G4)
                if k >= 2:
                    h2, j2 = (k - 2) // 3, (k - 2) % 3
                    if j2 < 2:
                        eng.wait_ge(r_pTa, 2 * h2 + j2 + 1)
                    else:
                        eng.wait_ge(r_pTv, h2 + 1)
                first = JOB_AT[j] // P
                for b in range(first, first + JOB_N[j] // P):
                    s, t = BLOCKS[b]
                    m = eng.transpose(bank(5 + k % 2)[:, P * (b - first):P * (b - first) + P],
                                      r_prob[:, h % 2, at[t] + P * s:at[t] + P * s + P], ident[:, :])
                m.then_inc(r_pT, 1)

            def weigh(h):
                G, hh = h // G4, h % G4
                eng.wait_ge(r_pTa, 2 * h + 2)
                eng.wait_ge(r_pTv, h + 1)
                if hh == 0 and G >= 1:
                    eng.wait_ge(a_cols, 2 * NG + G)
                weigh_columns(eng, 7, h, r_probT)

            for i in range(H + 3):
                if i < H:
                    qk(i, 0)
                    qk(i, 1)
                if 1 <= i <= H:
                    rows(i - 1)
                if 2 <= i <= H + 1:
                    columns(i - 2, 0)
                    columns(i - 2, 1)
                if i < H:
                    qk(i, 2)
                if 2 <= i <= H + 1:
                    columns(i - 2, 2)
                if i - 3 >= G4 and (i - 3) % G4 == 0:
                    eng.wait_ge(r_pTa, 2 * (i - 2) + 2)
                    group_rows(eng, 2, (i - 3) // G4 - 1, 5 + (3 * (i - 2) + 1) % 2)
                if i >= 3:
                    weigh(i - 3)
            group_rows(eng, 2, NG - 1, 7)
            pe_out(eng, 2, w, bp_row[:, :])

        @block.tensor
        def _(eng):
            eng.wait_ge(loaded, 16 * len(loads))
            eng.wait_ge(const, CONSTS)
            for n in range(NSTAGE):
                m = eng.transpose(bank(n // 4)[:, P * (n % 4):P * (n % 4) + P], stage[:, n, :], ident[:, :])
                if n % 4 == 3 or n == NSTAGE - 1:
                    m.then_inc(stage_T, 1)
            eng.transpose(bank(6)[:, 0:E], stage_gate[0:E, :], ident[0:E, 0:E]).then_inc(stage_T, 1)
            eng.wait_ge(weights, 6)
            with eng.Fori(0, B) as b:
                pe_norm(eng, 0)
                pe_attn(eng, 0, w_a)
                pe_norm(eng, 1)
                pe_moe(eng, 0)
                pe_norm(eng, 2)
                pe_attn(eng, 1, w_b)
                pe_norm(eng, 3)
                pe_moe(eng, 1)
                pe_norm(eng, 4)
                pe_lin(eng)
                pe_norm(eng, 5)
                pe_adapter(eng, 0)
                pe_norm(eng, 6)
                pe_rel(eng, w_r)
                pe_norm(eng, 7)
                pe_adapter(eng, 1)
                eng.nop().then_inc(ended, 1)
                eng.wait_ge(started, b + 1)

        @block.vector
        def _(eng):
            steps = [0]

            def link(ins):
                steps[0] += 1
                ins.then_inc(step, 1)
                eng.wait_ge(step, steps[0])

            def flat(n):
                return bank(n).rearrange("p (t d) -> p t d", t=NT)

            def norm(n, rest_of_x=None):
                if n > 0:
                    eng.wait_ge(x_done, 2 * n - 1)
                src = x_next if n == 0 else x
                for seen, what, t in ((0, "stats", 0), (0, "stats", 1), (1, "mean", 0), (0, "stats", 2),
                                      (3, "var", 0), (2, "mean", 1), (0, "stats", 3), (6, "var", 1),
                                      (4, "mean", 2), (7, "mean", 3), (9, "var", 2), (10, "var", 3)):
                    if (what, t) == ("stats", 2) and n > 0:
                        if rest_of_x:
                            rest_of_x()
                        eng.wait_ge(x_done, 2 * n)
                    if seen:
                        eng.wait_ge(normed, 12 * n + seen)
                    if what == "stats":
                        m = eng.bn_stats(stats[:, t, :], src[:, t, :])
                    elif what == "mean":
                        m = eng.bn_aggr(moments[:, t, :], stats[:, t, :])
                    else:
                        m = eng.tensor_scalar(rstd[:, t:t + 1], moments[:, t, 1:2], EPS, None, ALU.add)
                    m.then_inc(normed, 1)
                for t in range(NT):
                    eng.wait_ge(rstd_ok, NT * n + t + 1)
                    eng.tensor_scalar(xn[:, t, :], src[:, t, :], moments[:, t, 0:1], rstd[:, t:t + 1],
                                      ALU.subtract, ALU.mult).then_inc(xn_ok, 1)

            def add_to_x(bk, done, n, src=x):
                def half(i):
                    eng.wait_ge(done, 2 * n + i + 1)
                    tiles = slice(2 * i, 2 * i + 2)
                    eng.tensor_tensor(x[:, tiles, :], src[:, tiles, :],
                                      bank(bk + i)[:, 0:2 * P].rearrange("p (t d) -> p t d", t=2),
                                      ALU.add).then_inc(x_done, 1)

                half(0)
                return lambda: half(1)

            def parts_of_qk(n, scale):
                for w in range(2):
                    eng.wait_ge(a_hi, 2 * n + w + 1)
                    eng.scalar_tensor_tensor(out=res[:, w, :], in0=bank(w), scalar=(scale, 1.0)[w],
                                             in1=qk_part(w, 0), op0=ALU.mult,
                                             op1=ALU.subtract).then_inc(a_res, 1)
                if n == 2:
                    eng.memset(q_parts[:, 0:2, 0:1], 0.0).then_inc(r_shift, 1)
                for w in range(2):
                    eng.wait_ge(a_res, 2 * n + w + 1)
                    eng.wait_ge(a_mid, 2 * n + w + 1)
                    eng.tensor_tensor(qk_part(w, 2), res[:, w, :], qk_part(w, 1),
                                      ALU.subtract).then_inc(a_lo, 1)
                eng.wait_ge(a_proj, 3 * n + 3)
                eng.tensor_copy(values[:, :, :, 0:HD], bank(2).rearrange("p (t h d) -> p t h d", t=NT, h=H))\
                   .then_inc(a_v, 1)

            def stack_k(n, at):
                i = spread_job(1, at)
                eng.wait_ge(a_spread, H * n + i + 1)
                eng.tensor_copy(k_st[:, at, :], bank(spread_bank(n, i))).then_inc(a_kst, 1)

            def heads_out(n, G, bk, inv):
                eng.wait_ge(a_rows, NG * n + G + 1)
                o = bank(bk).rearrange("p (t h d) -> p t h d", t=NT, h=G4)
                link(eng.reciprocal(inv[:, G % 2, :, :].unsqueeze(3), o[:, :, :, HD:HD + 1]))
                eng.tensor_tensor(
                    xn[:, :, HD * G4 * G:HD * G4 * (G + 1)].rearrange("p t (h d) -> p t h d", h=G4),
                    o[:, :, :, 0:HD], inv[:, G % 2, :, :].unsqueeze(3).to_broadcast([P, NT, G4, HD]),
                    ALU.mult).then_inc(a_o, 1)

            def attn(n, scale):
                parts_of_qk(n, scale)

                def row_max(G, jobs):
                    for i in jobs:
                        k = NROW * (NG * n + G) + i
                        eng.wait_ge(a_s1, k + 1)
                        job = rows_of(G)[i]
                        hh, t, _ = job[0]
                        src = bank((NROW * G + i) % 3)[:, 0:len(job) * (t + 1) * P]
                        src = src.rearrange("p (h k) -> p h k", h=len(job))
                        hs = slice(hh, hh + 2 * len(job) - 1, 2)
                        eng.tensor_reduce(neg_max[:, G % 2, t, hs], src, AX.X, ALU.max,
                                          negate=True).then_inc(a_max, 1)

                def split_max(G):
                    b = G % 2
                    eng.wait_ge(a_max, NROW * (NG * n + G + 1))
                    hi, mid, lo = (max_part[:, b, :, G4 * p:G4 * p + G4] for p in range(3))
                    link(eng.tensor_copy(hi, neg_max[:, b, :, :]))
                    link(eng.tensor_tensor(max_res[:, b, :, :], neg_max[:, b, :, :], hi, ALU.subtract))
                    link(eng.tensor_copy(mid, max_res[:, b, :, :]))
                    eng.tensor_tensor(lo, max_res[:, b, :, :], mid, ALU.subtract).then_inc(a_mparts, 1)

                stack_k(n, 0)
                stack_k(n, 1)
                row_max(0, range(NROW))
                split_max(0)
                row_max(1, range(AHEAD))
                for G in range(NG):
                    if G + 1 < NG:
                        row_max(G + 1, range(AHEAD, NROW))
                        split_max(G + 1)
                    if G >= 1:
                        heads_out(n, G - 1, 6 + (G - 1) % 2, rden)
                    if G + 2 < NG:
                        row_max(G + 2, range(AHEAD))
                heads_out(n, NG - 1, 6 + (NG - 1) % 2, rden)
                if n == 0:
                    eng.wait_ge(x_free, 1)
                return add_to_x(1, a_y, n, x if n else x_next)

            def moe(n):
                eng.wait_ge(m_logit, n + 1)
                link(eng.tensor_copy(lg[:, :, :], bank(6)[:, 0:NT * E].rearrange("p (t e) -> p t e", t=NT)))
                link(eng.tensor_reduce(top[:, :], lg[:, :, :], AX.X, ALU.max))
                eng.tensor_tensor(lgd[:, :, :], lg[:, :, :], top[:, :].unsqueeze(2).to_broadcast([P, NT, E]),
                                  ALU.subtract).then_inc(m_lgd, 1)
                mine = lg[:, :, :].unsqueeze(3).to_broadcast([P, NT, E, E])
                other = lg[:, :, :].unsqueeze(2).to_broadcast([P, NT, E, E])
                link(eng.tensor_tensor(eq[:, :, :, :], other, mine, ALU.is_equal))
                link(eng.tensor_tensor(eq[:, :, :, :], eq[:, :, :, :],
                                       before[:, :, :].unsqueeze(1).to_broadcast([P, NT, E, E]), ALU.mult))
                link(eng.tensor_tensor(gt[:, :, :, :], other, mine, ALU.is_gt))
                link(eng.tensor_tensor(gt[:, :, :, :], gt[:, :, :, :], eq[:, :, :, :], ALU.add))
                link(eng.tensor_reduce(rank[:, :, :], gt[:, :, :, :], AX.X, ALU.add))
                eng.wait_ge(m_ex, n + 1)
                link(eng.scalar_tensor_tensor(out=mix[:, :, :], in0=rank[:, :, :], scalar=2.0, in1=ex[:, :, :],
                                              op0=ALU.is_lt, op1=ALU.mult))
                link(eng.tensor_reduce(tot[:, :], mix[:, :, :], AX.X, ALU.add))
                link(eng.reciprocal(tot[:, :], tot[:, :]))
                eng.tensor_tensor(mix[:, :, :], mix[:, :, :], tot[:, :].unsqueeze(2).to_broadcast([P, NT, E]),
                                  ALU.mult).then_inc(m_mix, 1)

                def add(e):
                    eng.wait_ge(m_y, E * n + e + 1)
                    if e == 0:
                        eng.wait_ge(m_mix, n + 1)
                    else:
                        eng.wait_ge(m_acc, E * n + e)
                    for t in range(NT):
                        i = eng.scalar_tensor_tensor(out=x[:, t, :], in0=bank(4 + e % 2)[:, P * t:P * t + P],
                                                     scalar=mix[:, t, e:e + 1], in1=x[:, t, :],
                                                     op0=ALU.mult, op1=ALU.add)
                    i.then_inc(m_acc, 1)
                    if e == E - 1:
                        eng.wait_ge(m_acc, E * (n + 1))
                        eng.nop().then_inc(x_done, 2)

                for e in range(E):
                    for j, (_, w) in enumerate(FT):
                        i = NF * e + j
                        eng.wait_ge(m_u, E * NF * n + i + 1)
                        eng.wait_ge(m_silu, E * NF * n + i + 1)
                        if e >= 2:
                            eng.wait_ge(m_y, E * n + e - 1)
                        eng.tensor_tensor(hidden[0:w, e % 2, j, :], silu[0:w, i % 2, :], bank(2 + i % 2)[0:w, :],
                                          ALU.mult).then_inc(m_h, 1)
                    if e >= 1:
                        add(e - 1)
                add(E - 1)

            def lin():
                eng.wait_ge(l_be, 1)
                link(eng.tensor_scalar(l_beta[:, :, :], l_beta[:, :, :], 1.0, None, ALU.add))
                eng.reciprocal(l_beta[:, :, :], l_beta[:, :, :]).then_inc(l_bok, 1)
                for i in range(2 * NC2):
                    t, c = (i % 8) // 2, i % 2
                    eng.wait_ge(l_pn, i + 1)
                    eng.tensor_copy((l_k, l_v)[i // 8][:, t, 512 * c:512 * c + 512], bank(2 + i % 2))\
                       .then_inc(l_kv, 1)
                    if 1 <= i <= NC2:
                        j = i - 1
                        eng.wait_ge(l_sqks, j + 1)
                        eng.tensor_reduce(l_ssum[:, 1, j // 2, 8 * (j % 2):8 * (j % 2) + 8],
                                          l_sqk[:, j % 2, :].rearrange("p (h d) -> p h d", d=DM), AX.X,
                                          ALU.add).then_inc(l_ssk, 1)
                eng.wait_ge(l_ss, NC2)
                eng.tensor_copy(l_ssum[:, 0, :, :].rearrange("p t h -> p (t h)"),
                                bank(5)[:, 0:NT * H]).then_inc(l_ssc, 1)
                eng.wait_ge(l_norm, 1)
                eng.wait_ge(l_ssc, 1)
                eng.wait_ge(l_ssk, NC2)
                link(eng.tensor_scalar(l_inv[:, :, :, :], l_inv[:, :, :, :], 1e-18, None, ALU.max))
                link(eng.reciprocal(l_rec[:, :, :, :], l_inv[:, :, :, :]))
                link(eng.tensor_tensor(l_rec[:, :, :, :], l_rec[:, :, :, :], l_ssum[:, :, :, :], ALU.mult))
                link(eng.tensor_tensor(l_inv[:, :, :, :], l_inv[:, :, :, :], l_rec[:, :, :, :], ALU.add))
                link(eng.tensor_scalar(l_inv[:, :, :, :], l_inv[:, :, :, :], 0.5, None, ALU.mult))
                link(eng.tensor_scalar(l_inv[:, :, :, :], l_inv[:, :, :, :], 1e-12, None, ALU.max))
                link(eng.reciprocal(l_inv[:, :, :, :], l_inv[:, :, :, :]))
                link(eng.tensor_scalar(l_inv[:, 0, :, :], l_inv[:, 0, :, :], float(DM) ** -0.5, None, ALU.mult))
                eng.wait_ge(l_kv, 2 * NC2)

                def scale_values(c):
                    src = l_v[:, :, P * c:P * c + P].rearrange("p t (r d) -> p t r d", r=2)
                    dst = l_vk[:, :, P * c:P * c + P].rearrange("p t (r d) -> p t r d", r=2)
                    eng.tensor_tensor(dst, src,
                                      l_inv[:, 1, :, 2 * c:2 * c + 2].unsqueeze(3).to_broadcast([P, NT, 2, DM]),
                                      ALU.mult).then_inc(l_vks, 1)

                def mask_scores(c):
                    for r in range(2):
                        h = 2 * c + r
                        eng.wait_ge(l_sc, h + 1)
                        if c >= 2:
                            eng.wait_ge(l_o, c - 1)
                        eng.tensor_tensor(l_wt[:, c % 2, r, :, :], flat(r),
                                          keep_ge[:, :].unsqueeze(1).to_broadcast([P, NT, P]),
                                          ALU.mult).then_inc(l_wts, 1)

                def sum_states(c):
                    eng.wait_ge(l_sts, c + 1)
                    s = [l_st[:, c % 2, u, :] for u in range(NT - 1)]
                    link(eng.tensor_tensor(s[1], s[1], s[2], ALU.add))
                    eng.tensor_tensor(s[0], s[0], s[1], ALU.add).then_inc(l_sums, 1)

                def scale_out(c):
                    eng.wait_ge(l_o, c + 1)
                    if c >= 2:
                        eng.wait_ge(l_os, c - 1)
                    o = bank(4 + c % 2).rearrange("p (t r d) -> p t r d", t=NT, r=2)
                    dst = l_tmp[:, c % 2, :, :].rearrange("p t (r d) -> p t r d", r=2)
                    eng.tensor_tensor(dst, o,
                                      l_inv[:, 0, :, 2 * c:2 * c + 2].unsqueeze(3).to_broadcast([P, NT, 2, DM]),
                                      ALU.mult).then_inc(l_ts, 1)

                scale_values(0)
                scale_values(1)
                for c in range(NC2):
                    mask_scores(c)
                    if c + 2 < NC2:
                        scale_values(c + 2)
                    sum_states(c)
                    if c >= 1:
                        scale_out(c - 1)
                scale_out(NC2 - 1)
                return add_to_x(0, l_y, 0)

            def adapter(n):
                eng.wait_ge(xnT_ok, (6, 8)[n])
                link(eng.tensor_reduce(pooled[:, 0:1], xnT[:, :], AX.X, ALU.add))
                eng.tensor_scalar(pool_rep[:, :], ones[:, :], pooled[:, 0:1], 1.0 / T, ALU.mult,
                                  ALU.mult).then_inc(d_pool, 1)
                eng.wait_ge(d_gate_ok, n + 1)
                link(eng.tensor_copy(d_lg[:, :], bank(6)[:, 0:E]))
                eng.tensor_reduce(d_negm[:, 0:1], d_lg[:, :], AX.X, ALU.max, negate=True).then_inc(d_lgs, 1)
                mine = d_lg[:, :].unsqueeze(2).to_broadcast([P, E, E])
                other = d_lg[:, :].unsqueeze(1).to_broadcast([P, E, E])
                link(eng.tensor_tensor(d_eq[:, :, :], other, mine, ALU.is_equal))
                link(eng.tensor_tensor(d_eq[:, :, :], d_eq[:, :, :], before[:, :, :], ALU.mult))
                link(eng.tensor_tensor(d_gt[:, :, :], other, mine, ALU.is_gt))
                link(eng.tensor_tensor(d_gt[:, :, :], d_gt[:, :, :], d_eq[:, :, :], ALU.add))
                link(eng.tensor_reduce(d_rank[:, :], d_gt[:, :, :], AX.X, ALU.add))
                eng.wait_ge(d_exs, n + 1)
                link(eng.scalar_tensor_tensor(out=d_w[:, :], in0=d_rank[:, :], scalar=2.0, in1=d_ex[:, :],
                                              op0=ALU.is_lt, op1=ALU.mult))
                link(eng.tensor_reduce(d_s[:, 0:1], d_w[:, :], AX.X, ALU.add))
                link(eng.scalar_tensor_tensor(out=d_s[:, 0:1], in0=d_z[:, 0:1], scalar=1e-8, in1=d_s[:, 0:1],
                                              op0=ALU.mult, op1=ALU.add))
                link(eng.reciprocal(d_s[:, 0:1], d_s[:, 0:1]))
                eng.tensor_scalar(d_w[:, :], d_w[:, :], d_s[:, 0:1], None, ALU.mult).then_inc(d_ws, 1)
                eng.wait_ge(d_ws, n + 1)
                link(eng.tensor_scalar(d_w4[:, :], d_w[:, 0:E:2], pair_of[:, 0:1], None, ALU.mult))
                link(eng.scalar_tensor_tensor(out=d_w4[:, :], in0=d_w[:, 1:E:2], scalar=pair_of[:, 1:2],
                                              in1=d_w4[:, :], op0=ALU.mult, op1=ALU.add))
                for k in range(KD):
                    i = eng.tensor_scalar(d_up[:, k, :], upT[:, k, :], d_w4[:, k:k + 1], None, ALU.mult)
                i.then_inc(d_ups, 1)
                return add_to_x(4, d_y, n)

            def rel():
                parts_of_qk(2, float(HD) ** -0.5)

                def mask(c):
                    if c == 0:
                        eng.wait_ge(r_shift, 1)
                        eng.wait_ge(a_lo, 6)
                    if c >= 2:
                        eng.wait_ge(r_rel_ok, 2 * (IC // 8) * (c - 1))
                    mask_q(eng, c, 0).then_inc(r_qm, 1)
                    if c % 2 == 0:
                        mask_q(eng, c, 1).then_inc(r_qm, 1)

                mask(0)
                stack_k(2, 0)
                mask(1)
                stack_k(2, 1)
                for i in range(P // 8):
                    eng.wait_ge(r_rel_ok, 2 * i + 1)
                    v = bank((2 * i) % 4).rearrange("p (i t h) -> p h t i", i=8, t=NT)
                    q8 = slice(8 * i, 8 * i + 8)
                    eng.tensor_copy(sc[:, :, 0:9:4, q8], v[:, :, 0:3, :])
                    eng.tensor_copy(sc[:, :, 7, q8], v[:, :, 3, :]).then_inc(r_even, 1)
                    if i % 2 == 1:
                        if i // 2 + 2 < P // IC:
                            mask(i // 2 + 2)
                eng.wait_ge(r_late, P // 8)
                eng.wait_ge(r_odd, P // 8)
                eng.wait_ge(r_even, P // 8)
                eng.wait_ge(r_diag, 4 * (P // IC))

                def add(h, j):
                    k = 3 * h + j
                    eng.wait_ge(r_main, k + 1)
                    b = JOB_AT[j] // P
                    v = sc[:, h, b:b + JOB_N[j] // P, :].rearrange("p b i -> p (b i)")
                    eng.tensor_tensor(v, v, bank(k % 2)[:, 0:JOB_N[j]], ALU.add).then_inc(r_sum, 1)

                def row_max(h):
                    for i, (t, bk, col) in enumerate(ROW_JOBS):
                        eng.wait_ge(r_sT, 3 * h + (1, 2, 2, 3)[i])
                        eng.tensor_reduce(r_neg_max[:, h % 2, t:t + 1], bank(bk)[:, col:col + (t + 1) * P], AX.X,
                                          ALU.max, negate=True).then_inc(r_max, 1)

                def column(h):
                    eng.wait_ge(r_pT, 3 * h + 3)
                    if h >= 2:
                        eng.wait_ge(a_pv, 2 * H + h - 1)
                    eng.tensor_copy(r_probT[:, h % 2, JOB_AT[2]:JOB_AT[2] + JOB_N[2]],
                                    bank(5 + (3 * h + 2) % 2)[:, 0:JOB_N[2]]).then_inc(r_pTv, 1)

                for i in range(H + 2):
                    if i < H:
                        add(i, 0)
                        add(i, 1)
                    if 1 <= i <= H:
                        row_max(i - 1)
                    if i < H:
                        add(i, 2)
                    if i >= 2:
                        column(i - 2)
                    if i - 3 >= G4 and (i - 3) % G4 == 0:
                        heads_out(2, (i - 3) // G4 - 1, 5 + (3 * (i - 2) + 1) % 2, r_rden)
                heads_out(2, NG - 1, 7, r_rden)
                return add_to_x(1, a_y, 2)

            for n in range((NSTAGE + 3) // 4):
                eng.wait_ge(stage_T, n + 1)
            b4 = [bank(n).rearrange("p (j d) -> p j d", d=P) for n in range(8)]
            eng.tensor_copy(w_b[:, :, :], b4[0]).then_inc(weights, 1)
            eng.tensor_copy(w_r[:, :, :], b4[1]).then_inc(weights, 1)
            eng.tensor_copy(relT[:, 0, 0:2 * P], bank(2)[:, 0:2 * P]).then_inc(set_up, 1)
            eng.tensor_copy(relT[:, 0, 2 * P:3 * P], bank(2)[:, 0:P])
            eng.wait_ge(set_up, 1)
            eng.tensor_tensor(rel_res[:, :], bank(2)[:, 0:2 * P], relT[:, 0, 0:2 * P],
                              ALU.subtract).then_inc(set_up, 1)
            eng.wait_ge(set_up, 2)
            eng.tensor_copy(relT[:, 1, 0:2 * P], rel_res[:, :])
            eng.tensor_copy(relT[:, 1, 2 * P:3 * P], rel_res[:, 0:P])
            eng.tensor_copy(downT[:, 0:2, :], b4[2][:, 2:4, :]).then_inc(weights, 1)
            eng.tensor_copy(downT[:, 2:4, :], b4[3][:, 0:2, :])
            eng.tensor_copy(upT[:, 0:2, :], b4[3][:, 2:4, :]).then_inc(weights, 1)
            eng.tensor_copy(upT[:, 2:4, :], b4[4][:, 0:2, :]).then_inc(weights, 1)
            eng.wait_ge(stage_T, (NSTAGE + 3) // 4 + 1)
            eng.tensor_copy(gateT[:, :], bank(6)[:, 0:E]).then_inc(set_up, 1)
            eng.wait_ge(set_up, 3)
            eng.memset(bank(6), 0.0)
            eng.memset(bank(7), 0.0).then_inc(weights, 1)
            eng.wait_ge(const, CONSTS)
            with eng.Fori(0, B) as b:
                steps[0] = 0
                eng.wait_ge(x_in, 16 * b + 16)
                norm(0)
                rest = attn(0, float(HD) ** -0.5)
                norm(1, rest)
                moe(0)
                norm(2)
                rest = attn(1, float(P) ** -0.5)
                norm(3, rest)
                moe(1)
                norm(4)
                rest = lin()
                norm(5, rest)
                rest = adapter(0)
                norm(6, rest)
                rest = rel()
                norm(7, rest)
                rest = adapter(1)
                rest()
                eng.nop().then_inc(ended, 1)
                eng.wait_ge(started, b + 1)


_INS = ['L0_attn_a_x', 'L0_attn_a_Wq', 'L0_attn_a_Wk', 'L0_attn_a_Wv', 'L0_attn_a_Wo', 'L0_attn_b_W_attn',
        'L0_attn_b_W_out', 'L0_ffn_Ws', 'L0_ffn_bs', 'L0_ffn_Wg', 'L0_ffn_Wu', 'L0_ffn_Wd', 'L1_attn_a_Wk',
        'L1_attn_a_Wv', 'L1_attn_a_Wq', 'L1_attn_a_Wbeta', 'L1_attn_a_Wout', 'L1_attn_b_Wq', 'L1_attn_b_Wk',
        'L1_attn_b_Wv', 'L1_attn_b_Wp', 'L1_attn_b_bp', 'L1_attn_b_rel_embed', 'L1_ffn_gate_w',
        'L1_ffn_down_w', 'L1_ffn_down_b', 'L1_ffn_up_w', 'L1_ffn_up_b']


def kernel(**inputs):
    import numpy as _np
    import concourse.bacc as _bacc
    from concourse import mybir as _mybir
    from concourse.bass_utils import run_bass_kernel_spmd as _run

    nc = _bacc.Bacc("TRN2", target_bir_lowering=False, num_devices=1)
    arrays, args = {}, []
    for name in _INS:
        a = _np.ascontiguousarray(inputs[name])
        arrays[f"in_{name}_dram"] = a
        args.append(nc.dram_tensor(f"in_{name}_dram", a.shape, _mybir.dt.from_np(a.dtype), kind="ExternalInput").ap())
    shape = arrays["in_L0_attn_a_x_dram"].shape
    args.append(nc.dram_tensor("out_0_dram", shape, _mybir.dt.float32, kind="ExternalOutput").ap())
    build(nc, *args)
    r = _run(nc, [arrays], core_ids=[0])
    return r.results[0]["out_0_dram"]
```
